# Optimizing a Trainium2 kernel written in Bass

```python
import numpy as np
import jax
import jax.numpy as jnp

def _softmax(x, axis=-1):
    return jax.nn.softmax(x, axis=axis)

def _gelu(x):
    return jax.nn.gelu(x, approximate=True)

def _silu(x):
    return jax.nn.silu(x)

def _sigmoid(x):
    return jax.nn.sigmoid(x)

def _layernorm(x, axis=-1, eps=1e-05):
    m = jnp.mean(x, axis=axis, keepdims=True)
    v = jnp.var(x, axis=axis, keepdims=True)
    return (x - m) / jnp.sqrt(v + eps)

def _scatter_add(tgt, idx, src, axis=0):
    return tgt.at[idx].add(src)

def _segment_sum(src, seg, n):
    return jax.ops.segment_sum(src, seg, n)
kernel_name = 'mk_decoder_postln_d1_seqx_r8_bf9986'

def setup_inputs(seed: int=0):
    np.random.seed(seed)
    _w = jnp.asarray

    def _rec_inputs():
        import jax
        import jax.numpy as jnp
        _rk = jax.random.key(seed)
        x = 7.22e-05 + 1 * jax.random.normal(jax.random.fold_in(_rk, 1), (2, 256, 512), jnp.float32)
        _lenS = 256 - jax.random.randint(jax.random.fold_in(_rk, 7), (2,), 0, max(1, 256 // 4) + 1, jnp.int32)
        _lenS2 = 512 - jax.random.randint(jax.random.fold_in(_rk, 8), (2,), 0, max(1, 512 // 4) + 1, jnp.int32)
        _ctx_4096P = jax.random.normal(jax.random.fold_in(_rk, 11), (2, 16, 512), jnp.float32)
        _ctx_4096c = jax.random.dirichlet(jax.random.fold_in(_rk, 511), 0.3 * jnp.ones((16,), jnp.float32), (2, 512))
        _ctx_4096t = jnp.einsum('bsk,bkd->bsd', _ctx_4096c, _ctx_4096P)
        _ctx_4096t = _ctx_4096t * jax.lax.rsqrt(jnp.mean(jnp.square(_ctx_4096t)) + 1e-12) * 0.953939
        ctx_4096 = 4.13588e-05 + 0.999923 * (_ctx_4096t + 0.3 * jax.random.normal(jax.random.fold_in(_rk, 611), (2, 512, 512), jnp.float32))
        return (x, ctx_4096)
    x, ctx_4096 = _rec_inputs()

    def _L0_attn_setup():
        import jax, jax.numpy as jnp
        import numpy as np
        H_M, P_M, G_M, N_M, K_CONV, CHUNK = (128, 64, 8, 128, 4, 128)
        D_MODEL = 512
        D_INNER = H_M * P_M
        CONV_DIM = D_INNER + 2 * G_M * N_M
        PROJ_DIM = D_INNER + CONV_DIM + H_M
        EPS = 1e-05

        def segsum(x):
            l = x.shape[-1]
            xe = jnp.broadcast_to(x[..., None], x.shape + (l,))
            m1 = jnp.tril(jnp.ones((l, l), dtype=bool), -1)
            s = jnp.cumsum(jnp.where(m1, xe, 0.0), axis=-2)
            m2 = jnp.tril(jnp.ones((l, l), dtype=bool), 0)
            return jnp.where(m2, s, -jnp.inf)

        def causal_conv(x, w, bconv):
            k = w.shape[1]
            s = x.shape[1]
            xp = jnp.pad(x, ((0, 0), (k - 1, 0), (0, 0)))
            y = sum((xp[:, i:i + s, :] * w[:, i] for i in range(k)))
            return y + bconv
        key = jax.random.key(seed)
        ks = jax.random.split(key, 8)
        B_, S = (1, 256)
        sc = 0.02
        return {'x': jax.random.normal(ks[0], (B_, S, D_MODEL), dtype=jnp.float32), 'norm_w': jnp.ones((D_MODEL,), dtype=jnp.float32), 'in_proj_w': jax.random.normal(ks[1], (PROJ_DIM, D_MODEL), dtype=jnp.float32) * sc, 'conv_w': jax.random.normal(ks[2], (CONV_DIM, K_CONV), dtype=jnp.float32) * 0.2, 'conv_b': jnp.zeros((CONV_DIM,), dtype=jnp.float32), 'dt_bias': jax.random.uniform(ks[3], (H_M,), dtype=jnp.float32) * 0.1, 'A_log': jnp.log(1.0 + 15.0 * jax.random.uniform(ks[4], (H_M,), dtype=jnp.float32)), 'Dp': jnp.ones((H_M,), dtype=jnp.float32), 'gnorm_w': jnp.ones((D_INNER,), dtype=jnp.float32), 'out_proj_w': jax.random.normal(ks[5], (D_MODEL, D_INNER), dtype=jnp.float32) * sc}
    _L0_attn_all = _L0_attn_setup()
    _L0_attn_in = {k: v for k, v in _L0_attn_all.items() if k in ('norm_w', 'in_proj_w', 'conv_w', 'conv_b', 'dt_bias', 'A_log', 'Dp', 'gnorm_w', 'out_proj_w')}
    del _L0_attn_all

    def _L0_xattn_setup():
        import jax, jax.numpy as jnp
        import numpy as np
        DIM = 512
        NUM_HEADS = 32
        NUM_KV_HEADS = 8
        HEAD_DIM = DIM // NUM_HEADS
        KV_DIM = DIM // (NUM_HEADS // NUM_KV_HEADS)
        B, S = (1, 256)
        key = jax.random.key(seed)
        ks = jax.random.split(key, 7)
        w_scale = DIM ** (-0.5)
        return {'query': jax.random.normal(ks[0], (B, S, DIM), jnp.float32), 'key': jax.random.normal(ks[1], (B, S, DIM), jnp.float32), 'value': jax.random.normal(ks[2], (B, S, DIM), jnp.float32), 'Wq': jax.random.normal(ks[3], (DIM, DIM), jnp.float32) * w_scale, 'Wk': jax.random.normal(ks[4], (DIM, KV_DIM), jnp.float32) * w_scale, 'Wv': jax.random.normal(ks[5], (DIM, KV_DIM), jnp.float32) * w_scale, 'Wo': jax.random.normal(ks[6], (DIM, DIM), jnp.float32) * w_scale}
    _L0_xattn_all = _L0_xattn_setup()
    _L0_xattn_in = {k: v for k, v in _L0_xattn_all.items() if k in ('Wq', 'Wk', 'Wv', 'Wo')}
    del _L0_xattn_all

    def _L0_ffn_setup():
        import jax, jax.numpy as jnp
        import numpy as np
        B, S, D = (4, 256, 512)
        NUM_EXPERTS, TOP_K = (3, 2)

        def _expert_outputs(h, w1, b1, w2, b2):
            pre = jnp.einsum('bsd,edf->ebsf', h, w1) + b1[:, None, None, :]
            act = jnp.stack([jnp.tanh(pre[0]), jax.nn.gelu(pre[1], approximate=False), jax.nn.silu(pre[2])])
            return jnp.einsum('ebsf,efd->ebsd', act, w2) + b2[:, None, None, :]
        key = jax.random.key(seed)
        ks = jax.random.split(key, 8)
        scale_in = 1.0 / np.sqrt(D)
        scale_gate = 1.0 / np.sqrt(D + 1)
        return {'h': jax.random.normal(ks[0], (B, S, D), dtype=jnp.float32), 'gate_w': jax.random.uniform(ks[1], (D + 1, NUM_EXPERTS), minval=-scale_gate, maxval=scale_gate, dtype=jnp.float32), 'gate_b': jnp.zeros((NUM_EXPERTS,), dtype=jnp.float32), 'w1': jax.random.uniform(ks[2], (NUM_EXPERTS, D, D), minval=-scale_in, maxval=scale_in, dtype=jnp.float32), 'b1': jnp.zeros((NUM_EXPERTS, D), dtype=jnp.float32), 'w2': jax.random.uniform(ks[3], (NUM_EXPERTS, D, D), minval=-scale_in, maxval=scale_in, dtype=jnp.float32), 'b2': jnp.zeros((NUM_EXPERTS, D), dtype=jnp.float32)}
    _L0_ffn_all = _L0_ffn_setup()
    _L0_ffn_in = {k: v for k, v in _L0_ffn_all.items() if k in ('gate_w', 'gate_b', 'w1', 'b1', 'w2', 'b2')}
    del _L0_ffn_all
    return {'x': x, 'ctx_4096': ctx_4096, 'L0_attn_norm_w': _L0_attn_in['norm_w'], 'L0_attn_in_proj_w': _L0_attn_in['in_proj_w'], 'L0_attn_conv_w': _L0_attn_in['conv_w'], 'L0_attn_conv_b': _L0_attn_in['conv_b'], 'L0_attn_dt_bias': _L0_attn_in['dt_bias'], 'L0_attn_A_log': _L0_attn_in['A_log'], 'L0_attn_Dp': _L0_attn_in['Dp'], 'L0_attn_gnorm_w': _L0_attn_in['gnorm_w'], 'L0_attn_out_proj_w': _L0_attn_in['out_proj_w'], 'L0_xattn_Wq': _L0_xattn_in['Wq'], 'L0_xattn_Wk': _L0_xattn_in['Wk'], 'L0_xattn_Wv': _L0_xattn_in['Wv'], 'L0_xattn_Wo': _L0_xattn_in['Wo'], 'L0_ffn_gate_w': _L0_ffn_in['gate_w'], 'L0_ffn_gate_b': _L0_ffn_in['gate_b'], 'L0_ffn_w1': _L0_ffn_in['w1'], 'L0_ffn_b1': _L0_ffn_in['b1'], 'L0_ffn_w2': _L0_ffn_in['w2'], 'L0_ffn_b2': _L0_ffn_in['b2']}

def reference(x, ctx_4096, L0_attn_norm_w, L0_attn_in_proj_w, L0_attn_conv_w, L0_attn_conv_b, L0_attn_dt_bias, L0_attn_A_log, L0_attn_Dp, L0_attn_gnorm_w, L0_attn_out_proj_w, L0_xattn_Wq, L0_xattn_Wk, L0_xattn_Wv, L0_xattn_Wo, L0_ffn_gate_w, L0_ffn_gate_b, L0_ffn_w1, L0_ffn_b1, L0_ffn_w2, L0_ffn_b2):
    import jax
    import jax.numpy as jnp

    def _L0_attn_ref(x, norm_w, in_proj_w, conv_w, conv_b, dt_bias, A_log, Dp, gnorm_w, out_proj_w):
        import jax, jax.numpy as jnp
        import numpy as np
        H_M, P_M, G_M, N_M, K_CONV, CHUNK = (128, 64, 8, 128, 4, 128)
        D_MODEL = 512
        D_INNER = H_M * P_M
        CONV_DIM = D_INNER + 2 * G_M * N_M
        PROJ_DIM = D_INNER + CONV_DIM + H_M
        EPS = 1e-05

        def segsum(x):
            l = x.shape[-1]
            xe = jnp.broadcast_to(x[..., None], x.shape + (l,))
            m1 = jnp.tril(jnp.ones((l, l), dtype=bool), -1)
            s = jnp.cumsum(jnp.where(m1, xe, 0.0), axis=-2)
            m2 = jnp.tril(jnp.ones((l, l), dtype=bool), 0)
            return jnp.where(m2, s, -jnp.inf)

        def causal_conv(x, w, bconv):
            k = w.shape[1]
            s = x.shape[1]
            xp = jnp.pad(x, ((0, 0), (k - 1, 0), (0, 0)))
            y = sum((xp[:, i:i + s, :] * w[:, i] for i in range(k)))
            return y + bconv
        b, s, _ = x.shape
        residual = x
        h = x * jax.lax.rsqrt(jnp.mean(x * x, axis=-1, keepdims=True) + EPS) * norm_w
        proj = jnp.einsum('bsd,od->bso', h, in_proj_w)
        gate = proj[..., :D_INNER]
        hBC = proj[..., D_INNER:D_INNER + CONV_DIM]
        dt = proj[..., D_INNER + CONV_DIM:]
        hBC = jax.nn.silu(causal_conv(hBC, conv_w, conv_b))
        hid = hBC[..., :D_INNER].reshape(b, s, H_M, P_M)
        B = hBC[..., D_INNER:D_INNER + G_M * N_M].reshape(b, s, G_M, N_M)
        C = hBC[..., D_INNER + G_M * N_M:].reshape(b, s, G_M, N_M)
        dt = jax.nn.softplus(dt + dt_bias)
        A = -jnp.exp(A_log)
        pad = -s % CHUNK
        D_res = Dp[None, None, :, None] * hid
        hid_dt = hid * dt[..., None]
        A_full = A[None, None, :] * dt

        def padseq(t):
            return jnp.pad(t, [(0, 0), (0, pad)] + [(0, 0)] * (t.ndim - 2))
        hid_dt, A_full, Bp, Cp = (padseq(hid_dt), padseq(A_full), padseq(B), padseq(C))
        S = s + pad
        c, l = (S // CHUNK, CHUNK)
        hc = hid_dt.reshape(b, c, l, H_M, P_M)
        Ac = A_full.reshape(b, c, l, H_M).transpose(0, 3, 1, 2)
        rep = H_M // G_M
        Bh = jnp.repeat(Bp.reshape(b, c, l, G_M, N_M), rep, axis=3)
        Ch = jnp.repeat(Cp.reshape(b, c, l, G_M, N_M), rep, axis=3)
        A_cs = jnp.cumsum(Ac, axis=-1)
        L = jnp.exp(segsum(Ac))
        M = jnp.einsum('bcihn,bcjhn->bcijh', Ch, Bh) * jnp.transpose(L, (0, 2, 3, 4, 1))
        Y_diag = jnp.einsum('bcijh,bcjhp->bcihp', M, hc)
        decay_states = jnp.exp(A_cs[..., -1:] - A_cs)
        states = jnp.einsum('bclhn,bhcl,bclhp->bchpn', Bh, decay_states, hc)
        A_last = jnp.pad(A_cs[..., -1], ((0, 0), (0, 0), (1, 0)))
        decay_chunk = jnp.exp(segsum(A_last))
        states_cat = jnp.concatenate([jnp.zeros_like(states[:, :1]), states], axis=1)
        prev_states = jnp.einsum('bhij,bjhpn->bihpn', decay_chunk, states_cat)[:, :-1]
        Y_off = jnp.einsum('bclhn,bchpn,bhcl->bclhp', Ch, prev_states, jnp.exp(A_cs))
        y = (Y_diag + Y_off).reshape(b, S, H_M, P_M)[:, :s] + D_res
        y = y.reshape(b, s, D_INNER)
        yg = y * jax.nn.silu(gate)
        gsz = D_INNER // G_M
        ygr = yg.reshape(b, s, G_M, gsz)
        ygr = ygr * jax.lax.rsqrt(jnp.mean(ygr * ygr, axis=-1, keepdims=True) + EPS)
        y = ygr.reshape(b, s, D_INNER) * gnorm_w
        out = jnp.einsum('bsd,od->bso', y, out_proj_w)
        return residual + out

    def _L0_xattn_ref(query, key, value, Wq, Wk, Wv, Wo):
        import jax, jax.numpy as jnp
        import numpy as np
        DIM = 512
        NUM_HEADS = 32
        NUM_KV_HEADS = 8
        HEAD_DIM = DIM // NUM_HEADS
        KV_DIM = DIM // (NUM_HEADS // NUM_KV_HEADS)
        B, S = (1, 256)
        b, sq, _ = query.shape
        _, sk, _ = key.shape
        rep = NUM_HEADS // NUM_KV_HEADS
        q = (query @ Wq).reshape(b, sq, NUM_HEADS, HEAD_DIM).transpose(0, 2, 1, 3)
        k = (key @ Wk).reshape(b, sk, NUM_KV_HEADS, HEAD_DIM).transpose(0, 2, 1, 3)
        v = (value @ Wv).reshape(b, sk, NUM_KV_HEADS, HEAD_DIM).transpose(0, 2, 1, 3)
        k = jnp.repeat(k, rep, axis=1)
        v = jnp.repeat(v, rep, axis=1)
        scale = HEAD_DIM ** (-0.5)
        scores = jnp.einsum('bhqd,bhkd->bhqk', q, k) * scale
        probs = jax.nn.softmax(scores, axis=-1)
        out = jnp.einsum('bhqk,bhkd->bhqd', probs, v)
        out = out.transpose(0, 2, 1, 3).reshape(b, sq, DIM)
        return out @ Wo

    def _L0_ffn_ref(h, gate_w, gate_b, w1, b1, w2, b2):
        import jax, jax.numpy as jnp
        import numpy as np
        B, S, D = (4, 256, 512)
        NUM_EXPERTS, TOP_K = (3, 2)

        def _expert_outputs(h, w1, b1, w2, b2):
            pre = jnp.einsum('bsd,edf->ebsf', h, w1) + b1[:, None, None, :]
            act = jnp.stack([jnp.tanh(pre[0]), jax.nn.gelu(pre[1], approximate=False), jax.nn.silu(pre[2])])
            return jnp.einsum('ebsf,efd->ebsd', act, w2) + b2[:, None, None, :]
        b, s, d = h.shape
        vision_len = int(s * 0.3)
        text_strength = jnp.mean(jnp.abs(h[:, vision_len:, :]), axis=(1, 2), keepdims=True)
        vision_strength = jnp.mean(jnp.abs(h[:, :vision_len, :]), axis=(1, 2), keepdims=True)
        modality_ratio = text_strength / (vision_strength + 1e-08)
        modality_ratio = jnp.broadcast_to(modality_ratio, (b, s, 1))
        router_input = jnp.concatenate([h, modality_ratio], axis=-1)
        gate_logits = router_input @ gate_w + gate_b
        gate_scores = jax.nn.softmax(gate_logits, axis=-1)
        top_val, top_idx = jax.lax.top_k(gate_scores, TOP_K)
        top_val = top_val / (jnp.sum(top_val, axis=-1, keepdims=True) + 1e-08)
        expert_out = _expert_outputs(h, w1, b1, w2, b2)
        moe_out = jnp.zeros_like(h)
        batch_idx = jnp.arange(b)
        for i in range(TOP_K):
            j = top_idx[:, 0, i]
            out_i = expert_out[j, batch_idx]
            moe_out = moe_out + top_val[..., i:i + 1] * out_i
        return moe_out
    x = _layernorm(x + _L0_attn_ref(x, L0_attn_norm_w, L0_attn_in_proj_w, L0_attn_conv_w, L0_attn_conv_b, L0_attn_dt_bias, L0_attn_A_log, L0_attn_Dp, L0_attn_gnorm_w, L0_attn_out_proj_w), axis=-1)
    x = _layernorm(x + _L0_xattn_ref(x, ctx_4096, ctx_4096, L0_xattn_Wq, L0_xattn_Wk, L0_xattn_Wv, L0_xattn_Wo), axis=-1)
    x = _layernorm(x + _L0_ffn_ref(x, L0_ffn_gate_w, L0_ffn_gate_b, L0_ffn_w1, L0_ffn_b1, L0_ffn_w2, L0_ffn_b2), axis=-1)
    return x

_drawn_inputs = setup_inputs


def setup_inputs(seed=0):
    import zlib

    import numpy as np

    out = dict(_drawn_inputs(seed))
    spreads = {'L0_attn_norm_w': (1.0, 0.2),
     'L0_attn_conv_b': (0.0, 0.1),
     'L0_attn_Dp': (1.0, 0.2),
     'L0_attn_gnorm_w': (1.0, 0.2),
     'L0_ffn_gate_b': (0.0, 0.1),
     'L0_ffn_b1': (0.0, 0.321),
     'L0_ffn_b2': (0.0, 0.1)}
    factors = {'L0_attn_dt_bias': 8.0, 'L0_attn_A_log': 8.0}
    for name, (base, spread) in spreads.items():
        noise = np.random.default_rng([zlib.crc32(name.encode()), seed]).standard_normal(out[name].shape)
        drawn = base * np.exp(spread * noise) if base else spread * noise
        out[name] = jnp.asarray(drawn.astype(out[name].dtype))
    for name, factor in factors.items():
        out[name] = (out[name] * factor).astype(out[name].dtype)
    return out
```

```python
from contextlib import ExitStack

import concourse.bass as bass
from concourse import mybir

ALU = mybir.AluOpType
ACT = mybir.ActivationFunctionType
AX = mybir.AxisListType
F32 = mybir.dt.float32
BF16 = mybir.dt.bfloat16
F32R = mybir.dt.float32r

P = 128
NB, SEQ, D = 2, 256, 512
T = NB * SEQ
TT = T // P
KD = D // P
HEADS, HD, GROUPS, NST = 128, 64, 8, 128
DIN = HEADS * HD
TILES = DIN // P
U = TILES // GROUPS
HG = HEADS // GROUPS
KC = 4
GCH = DIN // GROUPS
EPS = 1e-5
EB = SEQ
CS = 512
CT = NB * CS
AH, KVH, AD = 32, 8, 16
REP = AH // KVH
KVW = KVH * AD
SCALE = AD ** -0.5
NE = 3
VIS = int(SEQ * 0.3)
SEL_B = 35
RING = 3
WR = 4


def decoder_program(nc, A):
    with ExitStack() as ctx:
        x_acc = ctx.enter_context(nc.sbuf_tensor("x_acc", [P, TT, D], F32))
        ssm_block(nc, A, x_acc)
        attention_ffn_block(nc, A, x_acc)


def ssm_block(nc, A, x_acc):
    acs_pos = nc.dram_tensor("acs_pos", [3, HEADS, T], BF16).ap()
    acs_neg = nc.dram_tensor("acs_neg", [3, HEADS, T], BF16).ap()
    exp_acs = nc.dram_tensor("exp_acs", [HEADS, NB, P], F32).ap()

    with ExitStack() as ctx:
        def sb(name, shape, dt=F32):
            return ctx.enter_context(nc.sbuf_tensor(name, shape, dt))

        def sem(name):
            return ctx.enter_context(nc.semaphore(name))

        def bank(name):
            return ctx.enter_context(nc.psum_tensor(name, [P, 512], F32))

        proj_ps = [bank("proj_ps0"), bank("proj_ps1")]
        tr_ps = bank("tr_ps")
        dif_ps = [bank("dif_ps0"), bank("dif_ps1")]
        y_ps = bank("y_ps")
        st_ps = bank("st_ps")
        off_ps = bank("off_ps")

        out_ps = [dif_ps[0], dif_ps[1], tr_ps, st_ps]

        ident = sb("ident", [P, P])
        causal = sb("causal", [P, P])
        ones = sb("ones", [P, P])
        norm_w = sb("norm_w", [P, KD])
        conv_w = sb("conv_w", [P, TILES + 2 * GROUPS, KC])
        conv_b = sb("conv_b", [P, TILES + 2 * GROUPS])
        d_skip = sb("d_skip", [P, TILES])
        gnorm = sb("gnorm", [P, TILES])
        dt_bias = sb("dt_bias", [P, 1])
        a_log = sb("a_log", [P, 1])
        x_tok = sb("x_tok", [P, TT, D])
        hT = sb("hT", [P, KD, T])
        dt_tok = sb("dt_tok", [P, TT, HEADS])
        dec_tok = sb("dec_tok", [P, NB, HEADS])
        w_ring = sb("w_ring", [P, WR, 2, KD, P])
        w_bc = sb("w_bc", [P, 2, KD, P])
        w_out = sb("w_out", [P, U, D])
        dif_l = sb("dif_l", [P, HG // 4, T], BF16)
        dif_r = sb("dif_r", [P, HG // 4, T], BF16)
        e_bc = sb("e_bc", [P, U, NB, P])
        bT = sb("bT", [P, T])
        cT = sb("cT", [P, T])
        b_tok = sb("b_tok", [P, NB, P])
        cb = sb("cb", [P, T])
        m_mat = sb("m_mat", [P, HG, T])
        conv_acc = sb("conv_acc", [P, 2, T])
        hid = sb("hid", [P, 2, T])
        gate = sb("gate", [P, 2, T])
        hc = sb("hc", [P, 2, TT, P])
        hcd = sb("hcd", [P, 2, NB, P])
        state = sb("state", [P, 2, NB, P])
        y_tmp = sb("y_tmp", [P, 2, T])
        off_tmp = sb("off_tmp", [P, 2, NB, P])
        yg = sb("yg", [P, U, T])
        sq = sb("sq", [P, T])
        sq_sum = sb("sq_sum", [P, T])
        mean_sq = sb("mean_sq", [P, TT])
        rstd_g = sb("rstd_g", [P, TT])
        minus_half = sb("minus_half", [P, 8])
        ss = sb("ss", [P, TT])
        rs = sb("rs", [P, TT])
        lead = sb("lead", [P, 8])
        bn6 = sb("bn6", [P, TT, 6])
        mv = sb("mv", [P, TT, 2])
        a_neg = sb("a_neg", [P, 1])
        a_exp = sb("a_exp", [P, 1])

        x_norm = m_mat[:, 0:4, :]
        dt_u = m_mat[:, 4, :]
        dt_abs = m_mat[:, 5, :]
        dt_e = m_mat[:, 6, :]
        dt_den = m_mat[:, 7, :]
        dt_z = m_mat[:, 8, :]
        dt_z2 = m_mat[:, 9, :]
        dt_s = m_mat[:, 10, :]
        dtT = m_mat[:, 11, :]
        acs = m_mat[:, 12, :]
        rest = m_mat[:, 13, :]
        decT = yg[:, 0, 0:NB * P]
        eT = yg[:, 1, 0:NB * P]
        aT = yg[:, 2, :]
        rest2 = yg[:, 3, :]
        parts = sb("parts", [P, 3, T], BF16)
        nparts = sb("nparts", [P, 3, T], BF16)
        w_dt = yg[:, 4, :].rearrange("p (k o) -> p k o", k=KD)
        sq_junk = yg[:, 5, :]

        s_const = sem("s_const"); s_chan = sem("s_chan"); s_x = sem("s_x"); s_wdt = sem("s_wdt")
        w_loaded = [sem(f"w_loaded{i}") for i in range(WR)]
        wbc_loaded = sem("wbc_loaded"); dif_loaded = sem("dif_loaded")
        e_loaded = sem("e_loaded"); wo_loaded = sem("wo_loaded")
        scratch_out = sem("scratch_out");
        act_step = sem("act_step"); vec_step = sem("vec_step"); pool_step = sem("pool_step")
        pe_step = sem("pe_step")
        proj_ready = sem("proj_ready"); dif_ready = sem("dif_ready"); clamped = sem("clamped"); exp_done = sem("exp_done")
        tap_done = sem("tap_done"); conv_step = sem("conv_step"); conv_done = sem("conv_done")
        hid_ready = sem("hid_ready"); gate_done = sem("gate_done")
        tr_ready = sem("tr_ready"); hc_done = sem("hc_done"); hcd_done = sem("hcd_done")
        cb_ready = sem("cb_ready"); cb_done = sem("cb_done"); m_done = sem("m_done")
        st_ready = sem("st_ready"); st_copied = sem("st_copied")
        yd_ready = sem("yd_ready"); off_ready = sem("off_ready"); comb_done = sem("comb_done")
        yg_done = sem("yg_done"); gated = sem("gated"); sq_done = sem("sq_done")
        wo_scaled = sem("wo_scaled"); ss_ready = sem("ss_ready"); ms_done = sem("ms_done")
        rstd_ready = sem("rstd_ready"); out_ready = sem("out_ready"); out_added = sem("out_added")
        block = ctx.enter_context(nc.Block())

        PB, PCc, PG = 1, 2, 2 + 2 * U
        def p_hid(u):
            return 3 + 2 * u
        def p_gate(u):
            return 4 + 2 * u

        CONSTS = 10

        @block.sync
        def _(sp):
            sp.dma_start(x_tok[:], A["x"]).then_inc(s_x, 16)
            for dst, src in ((ident, "ident"), (causal, "causal"), (norm_w, "norm_w"), (dt_bias, "dt_bias"),
                             (a_log, "a_log")):
                sp.dma_start(dst[:], A[src]).then_inc(s_const, 16)
            sp.dma_start(w_dt, A["w_dt"]).then_inc(s_wdt, 16)

            def load_w(g, u):
                sp.dma_start(w_ring[:, u % WR], A["w_main"][bass.ds(g * U + u, 1)].rearrange(
                    "a p j k o -> (a p) j k o")).then_inc(w_loaded[u % WR], 16)

            def load_bc(g):
                sp.dma_start(w_bc[:], A["w_bc"][bass.ds(g, 1)].rearrange(
                    "a p j k o -> (a p) j k o")).then_inc(wbc_loaded, 16)

            def load_dif(g):
                for r in range(4):
                    for dst, src, row in ((dif_l, acs_neg, 3), (dif_r, acs_pos, 0)):
                        sp.dma_start(dst[32 * r + row:32 * r + row + 3],
                                     src[:, bass.ds(g * HG + r, HG // 4, 4), :]).then_inc(dif_loaded, 16)

            def load_e(g):
                for half in range(2):
                    src = exp_acs[bass.ds(g * HG + half, U, 2)]
                    sp.dma_start(e_bc[half * HD:(half + 1) * HD],
                                 src.unsqueeze(0).to_broadcast([HD, U, NB, P])).then_inc(e_loaded, 16)

            def load_wo(g):
                sp.dma_start(w_out[:], A["w_out"][bass.ds(g, 1)].rearrange(
                    "a p u o -> (a p) u o")).then_inc(wo_loaded, 16)

            load_bc(0)
            for u in range(WR):
                load_w(0, u)
            for dst, src in ((conv_w, "conv_w"), (conv_b, "conv_b"), (d_skip, "d_skip"), (gnorm, "gnorm")):
                sp.dma_start(dst[:], A[src]).then_inc(s_chan, 16)
            load_wo(0)
            sp.wait_ge(vec_step, V["parts"])
            sp.dma_start(acs_pos.rearrange("k h t -> h k t"), parts[:]).then_inc(scratch_out, 16)
            sp.dma_start(acs_neg.rearrange("k h t -> h k t"), nparts[:]).then_inc(scratch_out, 16)
            sp.wait_ge(act_step, S["eT"])
            sp.dma_start(exp_acs.rearrange("h b t -> h (b t)"), eT).then_inc(scratch_out, 16)
            sp.wait_ge(scratch_out, 48)
            sp.wait_ge(pool_step, 3)
            load_dif(0)
            load_e(0)
            with sp.Fori(0, GROUPS - 1) as g:
                sp.wait_ge(proj_ready, PG * g + PCc)
                load_bc(g + 1)
                sp.wait_ge(dif_ready, HG * g + HG)
                load_dif(g + 1)
                for u in range(WR, U):
                    sp.wait_ge(proj_ready, PG * g + p_gate(u - WR))
                    load_w(g, u)
                for u in range(WR):
                    sp.wait_ge(proj_ready, PG * g + p_gate(u + WR))
                    load_w(g + 1, u)
                sp.wait_ge(comb_done, U * g + U + 1)
                load_e(g + 1)
                sp.wait_ge(out_ready, TT * g + TT)
                load_wo(g + 1)
            g = GROUPS - 1
            for u in range(WR, U):
                sp.wait_ge(proj_ready, PG * g + p_gate(u - WR))
                load_w(g, u)
            sp.wait_ge(vec_step, V["ln"])

        @block.gpsimd
        def _(pool):
            nc.gpsimd.memset(dif_l[:], 1.0).then_inc(pool_step, 1)
            nc.gpsimd.memset(dif_r[:], 1.0).then_inc(pool_step, 1)
            nc.gpsimd.memset(minus_half[:], -0.5).then_inc(pool_step, 1)
            pool.wait_ge(pool_step, 3)
            pool.wait_ge(vec_step, V["ms"])
            nc.gpsimd.tensor_tensor(rs[:], ss[:], minus_half[:, 0:TT], ALU.pow).then_inc(pool_step, 1)
            nc.gpsimd.memset(lead[:, 5:6], 0.0).then_inc(gated, 1)
            with pool.Fori(0, GROUPS) as g:
                def decay(u):
                    pool.wait_ge(hc_done, (U + 1) * g + 2 + u)
                    for hh in range(2):
                        ins = nc.gpsimd.tensor_tensor(
                            hcd[:, u % 2, :, hh * HD:(hh + 1) * HD], hc[:, u % 2, 0:TT:2, hh * HD:(hh + 1) * HD],
                            dec_tok[:, :, bass.ds(g * HG + 2 * u + hh, 1)].to_broadcast([P, NB, HD]), ALU.mult)
                    ins.then_inc(hcd_done, 1)

                def mix(u):
                    if u % 2 == 0:
                        pool.wait_ge(exp_done, HG // 4 * g + u // 2 + 1)
                    for h in (2 * u, 2 * u + 1):
                        nc.gpsimd.tensor_tensor(m_mat[:, h, :], m_mat[:, h, :], cb[:], ALU.mult).then_inc(m_done, 1)

                def gated_y(u):
                    pool.wait_ge(comb_done, U * g + u + 1 + 1)
                    late = y_tmp[:, u % 2, :].rearrange("p (b c t) -> p b c t", b=NB, c=2)[:, :, 1, :]
                    nc.gpsimd.tensor_tensor(late, late, off_tmp[:, u % 2], ALU.add).then_inc(yg_done, 1)
                    pool.wait_ge(gate_done, U * g + u + 1 + 1)
                    pool.wait_ge(yg_done, U * g + u + 1)
                    nc.gpsimd.tensor_tensor(yg[:, u, :], y_tmp[:, u % 2, :], gate[:, u % 2, :],
                                            ALU.mult).then_inc(gated, 1)
                    pool.wait_ge(gated, U * g + u + 1 + 1)
                    if u == 0:
                        nc.gpsimd.tensor_tensor(sq_sum[:], yg[:, u, :], yg[:, u, :], ALU.mult).then_inc(sq_done, 2)
                    else:
                        pool.wait_ge(sq_done, 2 * U * g + 2 * u)
                        nc.gpsimd.tensor_tensor(sq[:], yg[:, u, :], yg[:, u, :], ALU.mult).then_inc(sq_done, 1)
                        pool.wait_ge(sq_done, 2 * U * g + 2 * u + 1)
                        nc.gpsimd.tensor_tensor(sq_sum[:], sq_sum[:], sq[:], ALU.add).then_inc(sq_done, 1)

                pool.wait_ge(cb_done, g + 1)
                mix(0)
                decay(0)
                for u in range(1, U):
                    mix(u)
                    decay(u)
                    gated_y(u - 1)
                gated_y(U - 1)
                pool.wait_ge(ms_done, g + 1 + 1)
                nc.gpsimd.tensor_tensor(rstd_g[:], mean_sq[:], minus_half[:, 0:TT], ALU.pow).then_inc(rstd_ready, 1)
            pool.wait_ge(vec_step, V["var"])
            nc.gpsimd.tensor_tensor(rs[:], ss[:], minus_half[:, 0:TT], ALU.pow).then_inc(pool_step, 1)

        @block.scalar
        def _(act):
            act.wait_ge(s_x, 16)
            for t in range(TT):
                nc.scalar.activation(sq_junk, x_tok[:, t, :], ACT.Square, accum_out=ss[:, t:t + 1]).then_inc(act_step, 1)
                if t < TT - 1:
                    act.wait_ge(act_step, t + 1)
            act.wait_ge(s_const, 5 * 16)
            nc.scalar.activation(a_exp[:], a_log[:], ACT.Exp).then_inc(act_step, 1)
            act.wait_ge(pe_step, E["dt"])
            act.wait_ge(vec_step, V["u"])
            nc.scalar.activation(dt_abs, dt_u, ACT.Abs).then_inc(act_step, 1)
            act.wait_ge(act_step, 6)
            nc.scalar.activation(dt_e, dt_abs, ACT.Exp, scale=-1.0).then_inc(act_step, 1)
            act.wait_ge(vec_step, V["acs"])
            for b in range(NB):
                last = acs[:, b * EB + P - 1:b * EB + P]
                nc.scalar.activation(decT[:, b * P:(b + 1) * P], acs[:, b * EB:b * EB + P], ACT.Exp, bias=last,
                                     scale=-1.0).then_inc(act_step, 1)
            nc.scalar.activation(eT.rearrange("p (b t) -> p b t", b=NB),
                                 acs.rearrange("p (b t) -> p b t", b=NB)[:, :, P:2 * P], ACT.Exp).then_inc(act_step, 1)
            act.wait_ge(s_chan, 4 * 16)
            for k, s in enumerate((hid_ready, gate_done)):
                nc.scalar.copy(lead[:, 3 + k:4 + k], ones[:, 0:1]).then_inc(s, 1)
            with act.Fori(0, GROUPS) as g:
                def tap(n, wait, slot, col, ps):
                    act.wait_ge(proj_ready, PG * g + wait)
                    if n == 0:
                        act.wait_ge(vec_step, V["start"])
                    act.wait_ge(hid_ready, (U + 2) * g + max(n - 1, 0) + 1)
                    nc.scalar.activation(conv_acc[:, slot, :], ps[:], ACT.Identity, bias=conv_b[:, col],
                                         scale=conv_w[:, col, KC - 1]).then_inc(tap_done, 1)

                def exps(j):
                    act.wait_ge(clamped, HG * g + 4 * j + 4)
                    nc.scalar.activation(m_mat[:, 4 * j:4 * j + 4, :], m_mat[:, 4 * j:4 * j + 4, :], ACT.Exp
                                         ).then_inc(exp_done, 1)

                def silu(n, dst, slot):
                    act.wait_ge(conv_done, (U + 2) * g + n + 1 + 1)
                    nc.scalar.activation(dst, conv_acc[:, slot, :], ACT.Silu).then_inc(hid_ready, 1)

                def silu_gate(u):
                    act.wait_ge(proj_ready, PG * g + p_gate(u))
                    if u < 2:
                        act.wait_ge(gated, U * g + 1)
                    else:
                        act.wait_ge(gated, U * g + u - 1 + 1)
                    nc.scalar.activation(gate[:, u % 2, :], proj_ps[1][:], ACT.Silu).then_inc(gate_done, 1)

                def state_copy(u):
                    act.wait_ge(st_ready, U * g + u + 1)
                    nc.scalar.copy(state[:, u % 2], st_ps[:, 0:NB * P].rearrange("p (b t) -> p b t", b=NB)
                                   ).then_inc(st_copied, 1)

                def scale_wo(u):
                    if u == 0:
                        act.wait_ge(wo_loaded, 16 * g + 16)
                    nc.scalar.activation(w_out[:, u, :], w_out[:, u, :], ACT.Copy,
                                         scale=gnorm[:, bass.ds(g * U + u, 1)]).then_inc(wo_scaled, 1)

                def hid_tile(u):
                    if u < 2:
                        act.wait_ge(comb_done, U * g + 1)
                    else:
                        act.wait_ge(comb_done, U * g + u - 1 + 1)
                    silu(2 + u, hid[:, u % 2, :], u % 2)

                tap(0, PB, 0, bass.ds(TILES + g, 1), proj_ps[0])
                exps(0)
                tap(1, PCc, 1, bass.ds(TILES + GROUPS + g, 1), proj_ps[1])
                exps(1)
                exps(2)
                silu(0, bT[:], 0)
                tap(2, p_hid(0), 0, bass.ds(g * U, 1), proj_ps[0])
                exps(3)
                silu(1, cT[:], 1)
                hid_tile(0)
                silu_gate(0)
                scale_wo(0)
                for u in range(1, U):
                    tap(2 + u, p_hid(u), u % 2, bass.ds(g * U + u, 1), proj_ps[0])
                    hid_tile(u)
                    silu_gate(u)
                    state_copy(u - 1)
                    scale_wo(u)
                state_copy(U - 1)

        @block.vector
        def _(dve):
            n = [0]

            def step(ins, name=None):
                n[0] += 1
                ins.then_inc(vec_step, 1)
                if name:
                    assert V[name] == n[0], (name, n[0])
                dve.wait_ge(vec_step, n[0])

            step(nc.vector.memset(ones[:], 1.0))
            dve.wait_ge(act_step, 4)
            step(nc.vector.tensor_scalar(ss[:], ss[:], 1.0 / D, EPS, ALU.mult, ALU.add), "ms")
            dve.wait_ge(pool_step, 4)
            for t in range(TT):
                step(nc.vector.tensor_scalar(x_norm[:, t, :], x_tok[:, t, :], rs[:, t:t + 1], None, ALU.mult),
                     "xn" if t == TT - 1 else None)
            step(nc.vector.tensor_scalar(x_acc[:], x_tok[:], 2.0, None, ALU.mult))
            dve.wait_ge(s_const, 5 * 16)
            for k in range(KD):
                dve.wait_ge(pe_step, k + 1)
                step(nc.vector.tensor_scalar(hT[:, k, :], proj_ps[k % 2][:], norm_w[:, k:k + 1], None, ALU.mult),
                     "hT%d" % k)
            dve.wait_ge(pe_step, E["dt"])
            step(nc.vector.tensor_scalar(dt_u, proj_ps[0][:], dt_bias[:], None, ALU.add), "u")
            dve.wait_ge(act_step, 7)
            step(nc.vector.tensor_scalar(dt_den, dt_e, 2.0, None, ALU.add))
            step(nc.vector.reciprocal(dt_den, dt_den))
            step(nc.vector.tensor_tensor(dt_z, dt_e, dt_den, ALU.mult))
            step(nc.vector.tensor_tensor(dt_z2, dt_z, dt_z, ALU.mult))
            step(nc.vector.tensor_scalar(dt_s, dt_z2, 2.0 / 17, None, ALU.mult))
            for k in range(15, 1, -2):
                step(nc.vector.scalar_tensor_tensor(dt_s, dt_s, 2.0 / k, dt_z2, ALU.add, ALU.mult))
            step(nc.vector.scalar_tensor_tensor(dt_s, dt_s, 2.0, dt_z, ALU.add, ALU.mult))
            step(nc.vector.scalar_tensor_tensor(dtT, dt_u, 0.0, dt_s, ALU.max, ALU.add), "dtT")
            dve.wait_ge(act_step, 5)
            step(nc.vector.tensor_scalar(a_neg[:], a_exp[:], -1.0, None, ALU.mult))
            step(nc.vector.tensor_scalar(aT, dtT, a_neg[:], None, ALU.mult))
            for c in range(TT):
                step(nc.vector.tensor_tensor_scan(acs[:, c * P:(c + 1) * P], ones[:], aT[:, c * P:(c + 1) * P],
                                                  0.0, ALU.mult, ALU.add), "acs" if c == TT - 1 else None)
            step(nc.vector.tensor_copy(parts[:, 0, :], acs))
            step(nc.vector.tensor_tensor(rest, acs, parts[:, 0, :], ALU.subtract))
            step(nc.vector.tensor_copy(parts[:, 1, :], rest))
            step(nc.vector.tensor_tensor(rest2, rest, parts[:, 1, :], ALU.subtract))
            step(nc.vector.tensor_copy(parts[:, 2, :], rest2))
            step(nc.vector.tensor_scalar(nparts[:], parts[:], -1.0, None, ALU.mult), "parts")
            dve.wait_ge(pe_step, E["dt_tr"])
            step(nc.vector.tensor_copy(dt_tok[:], tr_ps[:].rearrange("p (c h) -> p c h", c=TT)))
            dve.wait_ge(pe_step, E["dec_tr"])
            step(nc.vector.tensor_copy(dec_tok[:], st_ps[:, 0:NB * P].rearrange("p (b h) -> p b h", b=NB)), "start")
            nc.vector.memset(rstd_g[:], 0.0).then_inc(out_added, TT)
            for k, s in enumerate((conv_done, comb_done, ms_done)):
                nc.vector.memset(lead[:, k:k + 1], 0.0).then_inc(s, 1)
            dve.wait_ge(s_chan, 4 * 16)

            with dve.Fori(0, GROUPS) as g:
                def conv(n, slot, col, ps):
                    dve.wait_ge(tap_done, (U + 2) * g + n + 1)
                    acc = conv_acc[:, slot, :].rearrange("p (b t) -> p b t", b=NB)
                    src = ps[:].rearrange("p (b t) -> p b t", b=NB)
                    for k in range(1, KC):
                        ins = nc.vector.scalar_tensor_tensor(
                            acc[:, :, k:], src[:, :, :SEQ - k], conv_w[:, col, KC - 1 - k], acc[:, :, k:],
                            ALU.mult, ALU.add)
                        if k < KC - 1:
                            ins.then_inc(conv_step, 1)
                            dve.wait_ge(conv_step, (KC - 2) * ((U + 2) * g + n) + k)
                        else:
                            ins.then_inc(conv_done, 1)

                def to_tokens(u):
                    dve.wait_ge(tr_ready, (U + 1) * g + 2 + u)
                    nc.vector.tensor_tensor(
                        hc[:, u % 2].rearrange("p c (h d) -> p c h d", h=2),
                        tr_ps[:].rearrange("p (c h d) -> p c h d", c=TT, h=2),
                        dt_tok[:, :, bass.ds(g * HG + 2 * u, 2)].unsqueeze(3).to_broadcast([P, TT, 2, HD]),
                        ALU.mult).then_inc(hc_done, 1)

                def clamp(h0, h1):
                    for h in range(h0, h1):
                        dve.wait_ge(dif_ready, HG * g + h + 1)
                        nc.vector.tensor_scalar(m_mat[:, h, :], dif_ps[h % 2][:], 0.0, None, ALU.min
                                                ).then_inc(clamped, 1)

                def combine(u):
                    dve.wait_ge(yd_ready, U * g + u + 1)
                    if u < 2:
                        dve.wait_ge(gated, U * g + 1)
                    else:
                        dve.wait_ge(gated, U * g + u - 1 + 1)
                    nc.vector.scalar_tensor_tensor(y_tmp[:, u % 2, :], hid[:, u % 2, :],
                                                   d_skip[:, bass.ds(g * U + u, 1)], y_ps[:], ALU.mult, ALU.add)
                    dve.wait_ge(off_ready, U * g + u + 1)
                    nc.vector.tensor_tensor(off_tmp[:, u % 2], off_ps[:, 0:NB * P].rearrange("p (b t) -> p b t", b=NB),
                                            e_bc[:, u], ALU.mult).then_inc(comb_done, 1)

                clamp(0, 6)
                conv(0, 0, bass.ds(TILES + g, 1), proj_ps[0])
                clamp(6, 10)
                conv(1, 1, bass.ds(TILES + GROUPS + g, 1), proj_ps[1])
                clamp(10, 14)
                conv(2, 0, bass.ds(g * U, 1), proj_ps[0])
                clamp(14, 16)
                dve.wait_ge(tr_ready, (U + 1) * g + 1)
                nc.vector.tensor_copy(b_tok[:], tr_ps[:, 0:NB * P].rearrange("p (b t) -> p b t", b=NB)
                                      ).then_inc(hc_done, 1)
                dve.wait_ge(cb_ready, g + 1)
                nc.vector.tensor_tensor(cb[:].rearrange("p (c t) -> p c t", c=TT),
                                        y_ps[:].rearrange("p (c t) -> p c t", c=TT),
                                        causal[:].unsqueeze(1).to_broadcast([P, TT, P]), ALU.mult
                                        ).then_inc(cb_done, 1)
                dve.wait_ge(e_loaded, 32 * g + 32)
                for u in range(1, U):
                    conv(2 + u, u % 2, bass.ds(g * U + u, 1), proj_ps[0])
                    to_tokens(u - 1)
                    combine(u - 1)
                to_tokens(U - 1)
                combine(U - 1)
                dve.wait_ge(ss_ready, g + 1)
                nc.vector.tensor_scalar(mean_sq[:], off_ps[:, 0:TT], 1.0 / GCH, EPS, ALU.mult, ALU.add
                                        ).then_inc(ms_done, 1)
                dve.wait_ge(rstd_ready, g + 1)
                for t in range(TT):
                    dve.wait_ge(out_ready, TT * g + t + 1)
                    dve.wait_ge(out_added, TT * g + t + 1)
                    nc.vector.scalar_tensor_tensor(x_acc[:, t, :], out_ps[t][:], rstd_g[:, t:t + 1], x_acc[:, t, :],
                                                   ALU.mult, ALU.add).then_inc(out_added, 1)
            dve.wait_ge(out_added, TT * (GROUPS + 1))
            for t in range(TT):
                step(nc.vector.bn_stats(bn6[:, t, :], x_acc[:, t, :]))
            for t in range(TT):
                step(nc.vector.bn_aggr(mv[:, t, :], bn6[:, t, :]))
            step(nc.vector.tensor_scalar(ss[:], mv[:, :, 1], EPS, None, ALU.add), "var")
            dve.wait_ge(pool_step, 5)
            for t in range(TT):
                step(nc.vector.tensor_scalar(x_acc[:, t, :], x_acc[:, t, :], mv[:, t, 0:1], rs[:, t:t + 1],
                                             ALU.subtract, ALU.mult), "ln" if t == TT - 1 else None)

        @block.tensor
        def _(pe):
            pe.wait_ge(vec_step, V["xn"])
            pe.wait_ge(s_const, 5 * 16)
            for k in range(KD):
                if k >= 2:
                    pe.wait_ge(vec_step, V["hT%d" % (k - 2)])
                for t in range(TT):
                    ins = nc.tensor.transpose(proj_ps[k % 2][:, t * P:(t + 1) * P],
                                              x_norm[:, t, k * P:(k + 1) * P], ident[:])
                ins.then_inc(pe_step, 1)
            pe.wait_ge(vec_step, V["hT%d" % (KD - 1)])
            pe.wait_ge(s_wdt, 16)
            for k in range(KD):
                ins = nc.tensor.matmul(proj_ps[0][:], w_dt[:, k, :], hT[:, k, :], start=k == 0, stop=k == KD - 1)
            ins.then_inc(pe_step, 1)
            pe.wait_ge(vec_step, V["dtT"])
            for c in range(TT):
                ins = nc.tensor.transpose(tr_ps[:, c * P:(c + 1) * P], dtT[:, c * P:(c + 1) * P], ident[:])
            ins.then_inc(pe_step, 1)
            pe.wait_ge(act_step, 9)
            for b in range(NB):
                ins = nc.tensor.transpose(st_ps[:, b * P:(b + 1) * P], decT[:, b * P:(b + 1) * P], ident[:])
            ins.then_inc(pe_step, 1)
            pe.wait_ge(vec_step, V["start"])
            with pe.Fori(0, GROUPS) as g:
                def project(ps, w, ks, last):
                    for k in ks:
                        ins = nc.tensor.matmul(ps[:], w[:, k, :], hT[:, k, :], start=k == 0, stop=k == KD - 1)
                    if last:
                        ins.then_inc(proj_ready, 1)

                def hid_proj(u, ks=range(KD)):
                    if 0 in ks:
                        pe.wait_ge(w_loaded[u % WR], 16 * (2 * g + u // WR + 1))
                        pe.wait_ge(conv_done, (U + 2) * g + (u + 2 if u else 1) + 1)
                    project(proj_ps[0], w_ring[:, u % WR, 0], ks, KD - 1 in ks)

                def gate_proj(u, ks=range(KD)):
                    if 0 in ks:
                        if u == 0:
                            pe.wait_ge(conv_done, (U + 2) * g + 2 + 1)
                        else:
                            pe.wait_ge(gate_done, U * g + u + 1)
                    project(proj_ps[1], w_ring[:, u % WR, 1], ks, KD - 1 in ks)

                def difs(h0, h1):
                    for h in range(h0, h1):
                        if h >= 2:
                            pe.wait_ge(clamped, HG * g + h - 1)
                        r, j = 32 * (h % 4), h // 4
                        for c in range(TT):
                            cols = slice(c * P, (c + 1) * P)
                            ins = nc.tensor.matmul(dif_ps[h % 2][:, cols], dif_l[r:r + 6, j, cols],
                                                   dif_r[r:r + 6, j, cols], start=True, stop=True)
                        ins.then_inc(dif_ready, 1)

                def transposes(u):
                    pe.wait_ge(hid_ready, (U + 2) * g + 3 + u + 1)
                    pe.wait_ge(hc_done, (U + 1) * g + 1 + u)
                    for c in range(TT):
                        cols = slice(c * P, (c + 1) * P)
                        ins = nc.tensor.transpose(tr_ps[:, cols], hid[:, u % 2, cols], ident[:])
                    ins.then_inc(tr_ready, 1)

                def states(u):
                    pe.wait_ge(hcd_done, U * g + u + 1)
                    if u == 0:
                        pe.wait_ge(out_added, TT * g + TT)
                    else:
                        pe.wait_ge(st_copied, U * g + u)
                    for b in range(NB):
                        ins = nc.tensor.matmul(st_ps[:, b * P:(b + 1) * P], b_tok[:, b, :], hcd[:, u % 2, b, :],
                                               start=True, stop=True)
                    ins.then_inc(st_ready, 1)

                def outputs(u):
                    if u == 0:
                        pe.wait_ge(cb_done, g + 1)
                    else:
                        pe.wait_ge(comb_done, U * g + u + 1)
                    pe.wait_ge(m_done, HG * g + 2 * u + 2)
                    for hh in range(2):
                        rows = slice(hh * HD, (hh + 1) * HD)
                        for c in range(TT):
                            cols = slice(c * P, (c + 1) * P)
                            ins = nc.tensor.matmul(y_ps[rows, cols], hc[:, u % 2, c, rows],
                                                   m_mat[:, 2 * u + hh, cols], start=True, stop=True)
                    ins.then_inc(yd_ready, 1)
                    pe.wait_ge(st_copied, U * g + u + 1)
                    if u == 0:
                        pe.wait_ge(ms_done, g + 1)
                    for b in range(NB):
                        late = slice(b * EB + P, (b + 1) * EB)
                        ins = nc.tensor.matmul(off_ps[:, b * P:(b + 1) * P], state[:, u % 2, b, :], cT[:, late],
                                               start=True, stop=True)
                    ins.then_inc(off_ready, 1)

                def out_proj(t, ks):
                    for k in ks:
                        ins = nc.tensor.matmul(out_ps[t][:], yg[:, k, t * P:(t + 1) * P], w_out[:, k, :],
                                               start=k == 0, stop=k == U - 1)
                    if U - 1 in ks:
                        ins.then_inc(out_ready, 1)

                pe.wait_ge(dif_loaded, 128 * g + 128)
                pe.wait_ge(out_added, TT * g + 2)
                difs(0, 2)
                pe.wait_ge(wbc_loaded, 16 * g + 16)
                pe.wait_ge(conv_done, (U + 2) * g + 1)
                project(proj_ps[0], w_bc[:, 0], (0, 1), False)
                difs(2, 4)
                project(proj_ps[0], w_bc[:, 0], (2, 3), True)
                difs(4, 6)
                pe.wait_ge(gate_done, U * g + 1)
                project(proj_ps[1], w_bc[:, 1], (0, 1), False)
                difs(6, 8)
                project(proj_ps[1], w_bc[:, 1], (2, 3), True)
                difs(8, 10)
                hid_proj(0, (0, 1))
                difs(10, 12)
                hid_proj(0, (2, 3))
                difs(12, 14)
                gate_proj(0, (0, 1))
                difs(14, 16)
                gate_proj(0, (2, 3))
                pe.wait_ge(hid_ready, (U + 2) * g + 2 + 1)
                pe.wait_ge(out_added, TT * g + 3)
                for b in range(NB):
                    ins = nc.tensor.transpose(tr_ps[:, b * P:(b + 1) * P], bT[:, b * EB:b * EB + P], ident[:])
                ins.then_inc(tr_ready, 1)
                pe.wait_ge(comb_done, U * g + 1)
                for c in range(TT):
                    cols = slice(c * P, (c + 1) * P)
                    ins = nc.tensor.matmul(y_ps[:, cols], bT[:, cols], cT[:, cols], start=True, stop=True)
                ins.then_inc(cb_ready, 1)
                for u in range(1, U):
                    hid_proj(u)
                    transposes(u - 1)
                    gate_proj(u)
                    states(u - 1)
                    outputs(u - 1)
                transposes(U - 1)
                pe.wait_ge(clamped, HG * g + HG)
                pe.wait_ge(wo_scaled, U * g + U - 1)
                pe.wait_ge(gated, U * g + 6 + 1)
                out_proj(0, range(0, 6))
                states(U - 1)
                outputs(U - 1)
                pe.wait_ge(wo_scaled, U * g + U)
                pe.wait_ge(gated, U * g + U - 1 + 1)
                out_proj(0, (6,))
                out_proj(1, range(0, 7))
                pe.wait_ge(sq_done, 2 * U * g + 2 * U)
                pe.wait_ge(comb_done, U * g + U + 1)
                for t in range(TT):
                    ins = nc.tensor.matmul(off_ps[:, t:t + 1], sq_sum[:, t * P:(t + 1) * P], ones[:, 0:1],
                                           start=True, stop=True)
                ins.then_inc(ss_ready, 1)
                out_proj(0, (7,))
                out_proj(1, (7,))
                pe.wait_ge(hc_done, (U + 1) * g + U + 1)
                out_proj(2, range(U))
                pe.wait_ge(st_copied, U * g + U)
                out_proj(3, range(U))




def attention_ffn_block(nc, A, x_acc):
    k_hi_d = nc.dram_tensor("k_hi_d", [P, CT], F32R).ap()
    k_lo_d = nc.dram_tensor("k_lo_d", [P, CT], F32R).ap()
    q_hi_d = nc.dram_tensor("q_hi_d", [KD, P, T], F32R).ap()
    q_lo_d = nc.dram_tensor("q_lo_d", [KD, P, T], F32R).ap()
    k_stack = nc.dram_tensor("k_stack", [KVH, 3 * AD, CT], F32R).ap().bitcast(F32)
    q_stack = nc.dram_tensor("q_stack", [2, KVH * REP // 2, 3 * AD, T], F32R).ap().bitcast(F32)

    with ExitStack() as ctx:
        def sb(name, shape, dt=F32):
            return ctx.enter_context(nc.sbuf_tensor(name, shape, dt))

        def sem(name):
            return ctx.enter_context(nc.semaphore(name))

        max_ps = ctx.enter_context(nc.psum_tensor("max_ps", [P, 2, 512], F32))
        sc_ps = [ctx.enter_context(nc.psum_tensor(f"sc_ps{i}", [P, 2, 512], F32)) for i in range(2)]
        pv_ps = ctx.enter_context(nc.psum_tensor("pv_ps", [P, 512], F32))
        odd_ps = ctx.enter_context(nc.psum_tensor("odd_ps", [P, 512], F32))
        banks = [max_ps[:, 0, :], max_ps[:, 1, :], sc_ps[0][:, 0, :], sc_ps[0][:, 1, :],
                 sc_ps[1][:, 0, :], sc_ps[1][:, 1, :], pv_ps[:], odd_ps[:]]

        ident = sb("ident2", [P, P])
        ctxT = sb("ctxT", [P, KD, CT])
        wk = sb("wk", [P, KD, KVW])
        wv = sb("wv", [P, KD, KVW])
        wq = sb("wq", [P, KD, D])
        wo = sb("wo", [P, KD, D])
        w1 = sb("w1", [P, NE, KD, D])
        w2 = sb("w2", [P, NE, KD, D])
        b1 = sb("b1", [P, NE, KD])
        b2 = sb("b2", [P, NE, D])
        gate_w = sb("gate_w", [P, KD, NE])
        gate_r = sb("gate_r", [P, NE])
        gate_b = sb("gate_b", [P, NE])
        vision = sb("vision", [P, P])
        text = sb("text", [P, P])
        every = sb("every", [P, P])
        first = sb("first", [P, P])
        k_hi = sb("k_hi", [P, CT], F32R)
        k_lo = sb("k_lo", [P, CT], F32R)
        v_tok = sb("v_tok", [P, CT // P, KVH, 2 * AD])
        x1T = sb("x1T", [P, KD, T])
        q_hi = sb("q_hi", [P, KD, T], F32R)
        q_lo = sb("q_lo", [P, KD, T], F32R)
        k_st = [sb(f"k_st{i}", [P, CT], F32R) for i in range(RING)]
        q_st = [sb(f"q_st{i}", [P, REP // 2, T], F32R) for i in range(RING)]
        nmax = sb("nmax", [P, RING, TT, REP])
        m_hi = sb("m_hi", [REP, RING, T], F32R)
        m_lo = sb("m_lo", [REP, RING, T], F32R)
        probs = sb("probs", [P, 2, 2 * 512])
        rden = sb("rden", [P, TT, REP])
        v_kv = [sb(f"v_kv{i}", [P, CT // P, 2 * AD]) for i in range(RING)]
        pv = sb("pv", [P, T])
        attn = sb("attn", [P, TT, D])
        attnT = x1T
        x2T = attn
        actT = [ctxT[:, :, 0:T], ctxT[:, :, T:2 * T]]
        bn6 = sb("bn6b", [P, TT, 6])
        mv = sb("mvb", [P, TT, 2])
        var = sb("varb", [P, TT])
        rs = sb("rsb", [P, TT])
        minus_half = sb("minus_halfb", [P, 8])
        lead = sb("leadb", [P, 8])
        asum = sb("asum", [P, TT])
        strength = sb("strength", [P, NB, 2])
        ratio = sb("ratio", [P, NB])
        lg = sb("lg", [P, TT, NE])
        lmax = sb("lmax", [P, TT])
        pe_ = sb("pe_", [P, TT, NE])
        lsum = sb("lsum", [P, TT])
        sel = sb("sel", [P, TT, 2, NE])
        keep = sb("keep", [P, TT])
        v1 = sb("v1", [P, TT])
        v2 = sb("v2", [P, TT])
        coef = sb("coef", [P, TT, NE])
        coef2 = sb("coef2", [P, TT, NE])
        sel_b = sb("sel_b", [P, NB, 2, NE])

        ctx_in = sem("ctx_in"); wkv_in = sem("wkv_in"); const_in = sem("const_in"); wq_in = sem("wq_in")
        wo_in = sem("wo_in"); w1_in = sem("w1_in"); w2_in = sem("w2_in"); small_in = sem("small_in")
        k_out = sem("k_out"); stacked = sem("stacked"); q_out = sem("q_out"); out_done = sem("out_done2")
        k_done = sem("k_done"); v_done = sem("v_done"); xT_ready = sem("xT_ready"); xT_done = sem("xT_done")
        q_ready = sem("q_ready"); q_hi_done = sem("q_hi_done"); q_lo_done = sem("q_lo_done")
        k_ready = sem("k_ready"); v_ready = sem("v_ready"); k_hi_done = sem("k_hi_done")
        ones_set = sem("ones_set"); halves_set = sem("halves_set")
        st_in = [sem(f"st_in{i}") for i in range(RING)]
        row_in = [sem(f"row_in{i}") for i in range(RING)]
        smax_ready = sem("smax_ready"); smax_done = sem("smax_done"); mT_ready = sem("mT_ready")
        m_hi_done = sem("m_hi_done"); m_lo_done = sem("m_lo_done")
        sc_ready = sem("sc_ready"); probs_done = sem("probs_done"); pv_ready = sem("pv_ready")
        pv_done = sem("pv_done"); v_slot = sem("v_slot"); pvT_ready = sem("pvT_ready")
        rden_done = sem("rden_done"); attn_done = sem("attn_done")
        aT_ready = sem("aT_ready"); aT_done = sem("aT_done"); o_ready = sem("o_ready")
        ln_step = sem("ln_step"); pow_done = sem("pow_done"); x2_done = sem("x2_done")
        x2T_ready = sem("x2T_ready"); x2T_done = sem("x2T_done")
        asum_done = sem("asum_done"); str_ready = sem("str_ready"); lg_ready = sem("lg_ready")
        soft_in = sem("soft_in"); soft_out = sem("soft_out"); sel_done = sem("sel_done"); sel_ready = sem("sel_ready")
        chain = sem("chain"); pre_ready = sem("pre_ready"); act_done = sem("act_done")
        moe_ready = sem("moe_ready"); moe_done = sem("moe_done"); ln_done = sem("ln_done")
        block = ctx.enter_context(nc.Block())
        HALF = KVH // 2

        @block.sync
        def _(sp):
            sp.dma_start(ident[:], A["ident"]).then_inc(const_in, 16)
            sp.dma_start(wk[:], A["wk"]).then_inc(wkv_in, 16)
            sp.dma_start(ctxT[:], A["ctxT"]).then_inc(ctx_in, 16)
            sp.dma_start(wv[:], A["wv"]).then_inc(wkv_in, 16)
            sp.dma_start(wq[:], A["wq"]).then_inc(wq_in, 16)
            sp.wait_ge(k_hi_done, NB)
            sp.wait_ge(k_done, NB)
            sp.dma_start(k_hi_d.bitcast(F32), k_hi[:].bitcast(F32)).then_inc(k_out, 16)
            sp.dma_start(k_lo_d.bitcast(F32), k_lo[:].bitcast(F32)).then_inc(k_out, 16)
            sp.wait_ge(q_hi_done, KD)
            sp.wait_ge(q_lo_done, KD)
            sp.dma_start(q_hi_d.rearrange("j p t -> p j t").bitcast(F32), q_hi[:].bitcast(F32)).then_inc(q_out, 16)
            sp.dma_start(q_lo_d.rearrange("j p t -> p j t").bitcast(F32), q_lo[:].bitcast(F32)).then_inc(q_out, 16)
            sp.wait_ge(k_out, 32)
            for j, ks in enumerate((k_hi_d, k_lo_d, k_hi_d)):
                sp.dma_start(k_stack[:, AD * j:AD * (j + 1), :],
                             ks.bitcast(F32).rearrange("(k d) t -> k d t", d=AD)).then_inc(stacked, 16)
            sp.wait_ge(q_out, 32)
            for j, qs in enumerate((q_hi_d, q_hi_d, q_lo_d)):
                rows = qs.bitcast(F32).rearrange("j p t -> (j p) t").rearrange(
                    "(m par d) t -> par m d t", par=2, d=AD)
                for par in range(2):
                    sp.dma_start(q_stack[par, :, AD * j:AD * (j + 1)], rows[par]).then_inc(stacked, 16)
            sp.wait_ge(stacked, 9 * 16)
            sp.wait_ge(ones_set, RING)

            def load_stacks(kv):
                for par in range(2):
                    rows = slice(64 * par, 64 * par + 3 * AD)
                    sp.dma_start(k_st[kv % RING][rows].bitcast(F32), k_stack[kv]).then_inc(st_in[kv % RING], 16)
                    sp.dma_start(q_st[kv % RING][rows].bitcast(F32),
                                 q_stack[par, kv * REP // 2:(kv + 1) * REP // 2].rearrange("m r t -> r m t")
                                 ).then_inc(st_in[kv % RING], 16)

            def load_rows(kv):
                s = kv % RING
                sp.wait_ge(m_lo_done, kv + 1 + 1)
                for h in range(REP):
                    for row, src in ((3 * AD, m_hi), (3 * AD + 1, m_lo)):
                        r = 64 * (h % 2) + row
                        sp.dma_start(q_st[s][r:r + 1, h // 2, :].bitcast(F32),
                                     src[h:h + 1, s, :].bitcast(F32)).then_inc(row_in[s], 16)

            for kv in range(RING):
                load_stacks(kv)
            sp.dma_start(wo[:], A["wo"]).then_inc(wo_in, 16)
            for name, dst in (("vision", vision), ("text", text), ("first", first), ("every", every),
                              ("b1", b1), ("gate_w", gate_w)):
                sp.dma_start(dst[:], A[name]).then_inc(small_in, 16)
            sp.dma_start(gate_r[:], A["gate_r"].partition_broadcast(P)).then_inc(small_in, 16)
            sp.dma_start(gate_b[:], A["gate_b"].partition_broadcast(P)).then_inc(small_in, 16)
            sp.dma_start(b2[:], A["b2"].partition_broadcast(P)).then_inc(small_in, 16)
            sp.dma_start(w1[:], A["w1"]).then_inc(w1_in, 16)
            sp.dma_start(w2[:], A["w2"]).then_inc(w2_in, 16)
            load_rows(0)
            for kv in range(1, KVH):
                load_rows(kv)
                if kv + 2 < KVH:
                    sp.wait_ge(sc_ready, 8 * kv)
                    load_stacks(kv + 2)

            sp.wait_ge(ln_done, TT)
            sp.dma_start(A["out"], x_acc[:]).then_inc(out_done, 16)
            sp.wait_ge(out_done, 16)

        @block.gpsimd
        def _(pool):
            nc.gpsimd.memset(minus_half[:], -0.5).then_inc(halves_set, 1)
            pool.wait_ge(halves_set, 1)
            pool.wait_ge(v_done, 3)

            def fill_v(kv, s):
                nc.gpsimd.tensor_copy(v_kv[s][:], v_tok[:, :, bass.ds(kv, 1), :].rearrange("p c a d -> p c (a d)")
                                      ).then_inc(v_slot, 1)

            for kv in range(RING):
                fill_v(kv, kv)
            for kv in range(RING, KVH):
                pool.wait_ge(pv_ready, kv - RING + 1)
                fill_v(kv, kv % RING)
            for n in range(2):
                pool.wait_ge(ln_step, 9 * n + 9)
                nc.gpsimd.tensor_tensor(rs[:], var[:], minus_half[:, 0:TT], ALU.pow).then_inc(pow_done, 1)

        @block.scalar
        def _(act):
            act.wait_ge(halves_set, 1)
            for b in range(NB):
                act.wait_ge(k_ready, b + 1)
                nc.scalar.copy(k_hi[:, b * CS:(b + 1) * CS], banks[b]).then_inc(k_hi_done, 1)
            for j in range(KD):
                act.wait_ge(q_ready, j + 1)
                nc.scalar.mul(q_hi[:, j, :], banks[j], SCALE).then_inc(q_hi_done, 1)

            def max_row(kv, s):
                act.wait_ge(mT_ready, kv + 1)
                nc.scalar.copy(m_hi[:, s, :], odd_ps[0:REP, :]).then_inc(m_hi_done, 1)

            def exps(kv, n):
                act.wait_ge(sc_ready, 8 * kv + n + 1)
                nc.scalar.activation(probs[:, n % 2, :], sc_ps[n % 2][:].rearrange("p a k -> p (a k)"), ACT.Exp
                                     ).then_inc(probs_done, 1)

            nc.scalar.copy(lead[:, 4:5], minus_half[:, 0:1]).then_inc(probs_done, 2)
            nc.scalar.copy(lead[:, 5:6], minus_half[:, 0:1]).then_inc(pv_done, 1)
            max_row(0, 0)

            def head(kv, s, more=True):
                for n in range(8):
                    exps(kv, n)
                    if n == 4 and more:
                        max_row(kv + 1, (s + 1) % RING)
                act.wait_ge(pv_ready, kv + 1)
                nc.scalar.copy(pv[:], pv_ps[:]).then_inc(pv_done, 1)

            with act.Fori(0, 2) as i:
                for s in range(RING):
                    head(RING * i + s, s)
            head(KVH - 2, 0)
            head(KVH - 1, 1, False)
            act.wait_ge(soft_in, 1)
            nc.scalar.activation(pe_[:], lg[:], ACT.Exp).then_inc(soft_out, 1)
            act.wait_ge(small_in, 9 * 16)
            for e, func in enumerate((ACT.Tanh, ACT.Gelu, ACT.Silu)):
                for f in range(KD):
                    act.wait_ge(pre_ready, KD * e + f + 1)
                    nc.scalar.activation(actT[e % 2][:, f, :], banks[f], func, bias=b1[:, e, f:f + 1]
                                         ).then_inc(act_done, 1)

        @block.vector
        def _(dve):
            for s in range(RING):
                nc.vector.memset(k_st[s][:].bitcast(F32), 1.0).then_inc(ones_set, 1)
            nc.vector.memset(v_tok[:, :, :, AD:2 * AD], 1.0).then_inc(v_done, 1)
            for k, s in enumerate((attn_done, smax_done, m_lo_done)):
                nc.vector.memset(lead[:, k:k + 1], 0.0).then_inc(s, 1)
            for b in range(NB):
                dve.wait_ge(k_hi_done, b + 1)
                cols = slice(b * CS, (b + 1) * CS)
                nc.vector.tensor_tensor(k_lo[:, cols], banks[b], k_hi[:, cols].bitcast(F32), ALU.subtract
                                        ).then_inc(k_done, 1)
            for h in range(2):
                dve.wait_ge(v_ready, h + 1)
                nc.vector.tensor_copy(v_tok[:, 4 * h:4 * h + 4, :, 0:AD],
                                      banks[2 + h].rearrange("p (c k d) -> p c k d", c=4, k=KVH)).then_inc(v_done, 1)
            for k in range(KD):
                dve.wait_ge(xT_ready, k + 1)
                nc.vector.tensor_copy(x1T[:, k, :], banks[4 + k]).then_inc(xT_done, 1)
            for j in range(KD):
                dve.wait_ge(q_hi_done, j + 1)
                nc.vector.scalar_tensor_tensor(q_lo[:, j, :], banks[j], SCALE, q_hi[:, j, :].bitcast(F32),
                                               ALU.mult, ALU.subtract).then_inc(q_lo_done, 1)

            def row_max(kv, s, n):
                dve.wait_ge(smax_ready, 8 * kv + n + 1)
                t, m = n // 2, n % 2
                nc.vector.tensor_reduce(nmax[:, s, t, 2 * m:2 * m + 2], max_ps[:], AX.X, ALU.max, negate=True
                                        ).then_inc(smax_done, 1)

            def max_row(kv, s):
                dve.wait_ge(m_hi_done, kv + 1)
                nc.vector.tensor_tensor(m_lo[:, s, :], odd_ps[0:REP, :], m_hi[:, s, :].bitcast(F32), ALU.subtract
                                        ).then_inc(m_lo_done, 1)

            def normalise(kv):
                dve.wait_ge(pvT_ready, kv + 1)
                out = odd_ps[:].rearrange("p (t h d) -> p t h d", t=TT, h=REP)
                nc.vector.reciprocal(rden[:], out[:, :, :, AD]).then_inc(rden_done, 1)
                dve.wait_ge(rden_done, kv + 1)
                nc.vector.tensor_tensor(
                    attn[:, :, bass.ds(kv * REP * AD, REP * AD)].rearrange("p t (h d) -> p t h d", h=REP),
                    out[:, :, :, 0:AD], rden[:].unsqueeze(3).to_broadcast([P, TT, REP, AD]),
                    ALU.mult).then_inc(attn_done, 1)

            def head(kv, s, rest, ahead):
                if rest:
                    for n in range(5, 8):
                        row_max(kv + 1, (s + 1) % RING, n)
                if ahead:
                    row_max(kv + 2, (s + 2) % RING, 0)
                if rest:
                    max_row(kv + 1, (s + 1) % RING)
                if ahead:
                    for n in range(1, 5):
                        row_max(kv + 2, (s + 2) % RING, n)
                normalise(kv)

            for n in range(8):
                row_max(0, 0, n)
            max_row(0, 0)
            for n in range(5):
                row_max(1, 1, n)
            with dve.Fori(0, 2) as i:
                for s in range(RING):
                    head(RING * i + s, s, True, True)
            head(KVH - 2, 0, True, False)
            head(KVH - 1, 1, False, False)
            for k in range(KD):
                dve.wait_ge(aT_ready, k + 1)
                nc.vector.tensor_copy(attnT[:, k, :], banks[k]).then_inc(aT_done, 1)

            def layernorm(n, done):
                at = 9 * n
                for t in range(TT):
                    nc.vector.bn_stats(bn6[:, t, :], x_acc[:, t, :]).then_inc(ln_step, 1)
                for t in range(TT):
                    dve.wait_ge(ln_step, at + TT)
                    nc.vector.bn_aggr(mv[:, t, :], bn6[:, t, :]).then_inc(ln_step, 1)
                dve.wait_ge(ln_step, at + 2 * TT)
                nc.vector.tensor_scalar(var[:], mv[:, :, 1], EPS, None, ALU.add).then_inc(ln_step, 1)
                dve.wait_ge(pow_done, n + 1)
                for t in range(TT):
                    nc.vector.tensor_scalar(x_acc[:, t, :], x_acc[:, t, :], mv[:, t, 0:1], rs[:, t:t + 1],
                                            ALU.subtract, ALU.mult).then_inc(done, 1)

            c = [0]

            def link(ins):
                c[0] += 1
                ins.then_inc(chain, 1)
                dve.wait_ge(chain, c[0])

            for t in range(TT):
                dve.wait_ge(o_ready, t + 1)
                link(nc.vector.tensor_tensor(x_acc[:, t, :], x_acc[:, t, :], banks[4 + t], ALU.add))
            layernorm(0, x2_done)
            dve.wait_ge(x2_done, TT)
            nc.vector.tensor_reduce(asum[:], x_acc[:], AX.X, ALU.add, apply_absolute_value=True).then_inc(asum_done, 1)
            for k in range(KD):
                dve.wait_ge(x2T_ready, k + 1)
                nc.vector.tensor_copy(x2T[:, k, :], banks[k]).then_inc(x2T_done, 1)

            dve.wait_ge(str_ready, 1)
            dve.wait_ge(small_in, 9 * 16)
            sums = odd_ps[:, 0:2 * NB].rearrange("p (b s) -> p b s", b=NB)
            link(nc.vector.tensor_scalar(strength[:, :, 0], sums[:, :, 0], 1.0 / (VIS * D), 1e-8, ALU.mult, ALU.add))
            link(nc.vector.tensor_scalar(strength[:, :, 1], sums[:, :, 1], 1.0 / ((SEQ - VIS) * D), None, ALU.mult))
            link(nc.vector.reciprocal(ratio[:], strength[:, :, 0]))
            link(nc.vector.tensor_tensor(ratio[:], ratio[:], strength[:, :, 1], ALU.mult))
            dve.wait_ge(lg_ready, 1)
            logits = odd_ps[:, 16:16 + TT * NE].rearrange("p (t e) -> p t e", t=TT)
            link(nc.vector.tensor_tensor(lg[:], logits, gate_b[:].unsqueeze(1).to_broadcast([P, TT, NE]), ALU.add))
            for t in range(TT):
                link(nc.vector.scalar_tensor_tensor(lg[:, t, :], gate_r[:], ratio[:, t // 2:t // 2 + 1], lg[:, t, :],
                                                    ALU.mult, ALU.add))
            link(nc.vector.tensor_reduce(lmax[:], lg[:], AX.X, ALU.max))
            link(nc.vector.tensor_tensor(lg[:], lg[:], lmax[:].unsqueeze(2).to_broadcast([P, TT, NE]), ALU.subtract))
            nc.vector.memset(keep[:], 0.0).then_inc(soft_in, 1)
            dve.wait_ge(soft_out, 1)
            link(nc.vector.tensor_reduce(lsum[:], pe_[:], AX.X, ALU.add))
            link(nc.vector.reciprocal(lsum[:], lsum[:]))
            link(nc.vector.tensor_tensor(pe_[:], pe_[:], lsum[:].unsqueeze(2).to_broadcast([P, TT, NE]), ALU.mult))
            for i, best in enumerate((v1, v2)):
                s = sel[:, :, i, :]
                link(nc.vector.tensor_reduce(best[:], pe_[:], AX.X, ALU.max))
                link(nc.vector.tensor_tensor(s, pe_[:], best[:].unsqueeze(2).to_broadcast([P, TT, NE]), ALU.is_ge))
                link(nc.vector.tensor_scalar(keep[:], s[:, :, 0], -1.0, 1.0, ALU.mult, ALU.add))
                link(nc.vector.tensor_tensor(s[:, :, 1], s[:, :, 1], keep[:], ALU.mult))
                link(nc.vector.tensor_tensor(s[:, :, 2], keep[:], s[:, :, 1], ALU.subtract))
                if i == 0:
                    link(nc.vector.scalar_tensor_tensor(pe_[:], s, -2.0, pe_[:], ALU.mult, ALU.add))
            link(nc.vector.scalar_tensor_tensor(lsum[:], v1[:], 1e-8, v2[:], ALU.add, ALU.add))
            link(nc.vector.reciprocal(lsum[:], lsum[:]))
            link(nc.vector.tensor_tensor(v1[:], v1[:], lsum[:], ALU.mult))
            nc.vector.tensor_tensor(v2[:], v2[:], lsum[:], ALU.mult).then_inc(sel_done, 1)
            dve.wait_ge(sel_done, 1)
            dve.wait_ge(sel_ready, 1)
            link(nc.vector.tensor_copy(sel_b[:].rearrange("p b i e -> p (b i e)"), odd_ps[:, 64:64 + NB * 2 * NE]))
            for t in range(TT):
                link(nc.vector.tensor_scalar(coef[:, t, :], sel_b[:, t // 2, 0, :], v1[:, t:t + 1], None, ALU.mult))
                link(nc.vector.scalar_tensor_tensor(coef[:, t, :], sel_b[:, t // 2, 1, :], v2[:, t:t + 1],
                                                    coef[:, t, :], ALU.mult, ALU.add))
            for e in range(NE):
                for t in range(TT):
                    link(nc.vector.scalar_tensor_tensor(x_acc[:, t, :], b2[:, e, :], coef[:, t, e:e + 1],
                                                        x_acc[:, t, :], ALU.mult, ALU.add))
            for e in range(NE):
                for t in range(TT):
                    dve.wait_ge(moe_ready, TT * e + t + 1)
                    if e:
                        dve.wait_ge(moe_done, TT * (e - 1) + t + 1)
                    nc.vector.scalar_tensor_tensor(x_acc[:, t, :], banks[4 + t], coef[:, t, e:e + 1], x_acc[:, t, :],
                                                   ALU.mult, ALU.add).then_inc(moe_done, 1)
            dve.wait_ge(moe_done, TT * NE)
            layernorm(1, ln_done)

        @block.tensor
        def _(pe):
            pe.wait_ge(wkv_in, 32)
            pe.wait_ge(ctx_in, 16)
            for b in range(NB):
                for k in range(KD):
                    ins = nc.tensor.matmul(banks[b], wk[:, k, :], ctxT[:, k, b * CS:(b + 1) * CS],
                                           start=k == 0, stop=k == KD - 1)
                ins.then_inc(k_ready, 1)
            for h in range(2):
                for c in range(4):
                    for k in range(KD):
                        t = 4 * h + c
                        ins = nc.tensor.matmul(banks[2 + h][:, c * P:(c + 1) * P], ctxT[:, k, t * P:(t + 1) * P],
                                               wv[:, k, :], start=k == 0, stop=k == KD - 1)
                ins.then_inc(v_ready, 1)

            def turn(src, ready, first_bank):
                for k in range(KD):
                    for t in range(TT):
                        ins = nc.tensor.transpose(banks[first_bank + k][:, t * P:(t + 1) * P],
                                                  src[:, t, k * P:(k + 1) * P], ident[:])
                    ins.then_inc(ready, 1)

            pe.wait_ge(const_in, 16)
            turn(x_acc, xT_ready, 4)
            pe.wait_ge(xT_done, KD)
            pe.wait_ge(wq_in, 16)
            pe.wait_ge(k_done, NB)
            for j in range(KD):
                if j == 2:
                    pe.wait_ge(v_done, 3)
                for k in range(KD):
                    ins = nc.tensor.matmul(banks[j], wq[:, k, j * P:(j + 1) * P], x1T[:, k, :],
                                           start=k == 0, stop=k == KD - 1)
                ins.then_inc(q_ready, 1)
            pe.wait_ge(q_lo_done, KD)

            def row_scores(kv, s, n, visit):
                t, m = n // 2, n % 2
                if n == 0:
                    pe.wait_ge(st_in[s], 16 * 4 * visit)
                pe.wait_ge(smax_done, 8 * kv + n + 1)
                for par in range(2):
                    rows = slice(64 * par, 64 * par + 3 * AD)
                    ins = nc.tensor.matmul(max_ps[:, par, :], q_st[s][rows, m, t * P:(t + 1) * P],
                                           k_st[s][rows, (t // 2) * CS:(t // 2 + 1) * CS], start=True, stop=True)
                ins.then_inc(smax_ready, 1)

            def max_rows(kv, s):
                pe.wait_ge(smax_done, 8 * kv + 8 + 1)
                pe.wait_ge(m_lo_done, kv + 1)
                if not (isinstance(kv, int) and kv < 1):
                    pe.wait_ge(attn_done, kv - 1 + 1)
                for t in range(TT):
                    ins = nc.tensor.transpose(odd_ps[0:REP, t * P:(t + 1) * P], nmax[:, s, t, :], ident[:])
                ins.then_inc(mT_ready, 1)

            def scores(kv, s, n, visit):
                b, c = divmod(n, CS // P)
                if n == 0:
                    pe.wait_ge(row_in[s], 16 * 8 * visit)
                pe.wait_ge(probs_done, 8 * kv + n - 1 + 2)
                for m in range(REP // 2):
                    for par in range(2):
                        rows = slice(64 * par, 64 * par + 3 * AD + 2)
                        ins = nc.tensor.matmul(sc_ps[n % 2][:, par, m * SEQ:(m + 1) * SEQ],
                                               k_st[s][rows, b * CS + c * P:b * CS + (c + 1) * P],
                                               q_st[s][rows, m, b * SEQ:(b + 1) * SEQ], start=True, stop=True)
                ins.then_inc(sc_ready, 1)

            def values(kv, s, n):
                b, c = divmod(n, CS // P)
                pe.wait_ge(probs_done, 8 * kv + n + 1 + 2)
                if n == 0:
                    pe.wait_ge(v_slot, kv + 1)
                    pe.wait_ge(pv_done, kv + 1)
                for h in range(REP):
                    at = (2 * (h % 2) + h // 2) * SEQ
                    ins = nc.tensor.matmul(pv_ps[32 * h:32 * h + 2 * AD, b * SEQ:(b + 1) * SEQ],
                                           v_kv[s][:, b * (CS // P) + c, :], probs[:, n % 2, at:at + SEQ],
                                           start=c == 0, stop=c == CS // P - 1)
                if n == 7:
                    ins.then_inc(pv_ready, 1)

            def turn_pv(kv):
                pe.wait_ge(pv_done, kv + 1 + 1)
                pe.wait_ge(m_lo_done, min(kv + 2, KVH) + 1 if isinstance(kv, int) else kv + 3)
                pe.wait_ge(attn_done, kv + 1)
                for t in range(TT):
                    ins = nc.tensor.transpose(odd_ps[:, t * P:(t + 1) * P], pv[:, t * P:(t + 1) * P], ident[:])
                ins.then_inc(pvT_ready, 1)

            for n in range(8):
                row_scores(0, 0, n, 1)
            max_rows(0, 0)
            for n in range(5):
                row_scores(1, 1, n, 1)

            def head(kv, s, visit, rest=True, ahead=True):
                s1, s2 = (s + 1) % RING, (s + 2) % RING
                scores(kv, s, 0, visit)
                for n in range(8):
                    if rest and n == 4:
                        max_rows(kv + 1, s1)
                    if rest and n < 3:
                        row_scores(kv + 1, s1, n + 5, None)
                    if ahead and n >= 3:
                        row_scores(kv + 2, s2, n - 3, visit + (s > 0))
                    if n < 7:
                        scores(kv, s, n + 1, visit)
                    values(kv, s, n)
                turn_pv(kv)

            with pe.Fori(0, 2) as i:
                for s in range(RING):
                    head(RING * i + s, s, i + 1)
            head(KVH - 2, 0, 3, True, False)
            head(KVH - 1, 1, 3, False, False)
            pe.wait_ge(attn_done, KVH + 1)
            turn(attn, aT_ready, 0)
            pe.wait_ge(wo_in, 16)
            pe.wait_ge(aT_done, KD)
            for t in range(TT):
                for k in range(KD):
                    ins = nc.tensor.matmul(banks[4 + t], attnT[:, k, t * P:(t + 1) * P], wo[:, k, :],
                                           start=k == 0, stop=k == KD - 1)
                ins.then_inc(o_ready, 1)
            pe.wait_ge(small_in, 9 * 16)
            pe.wait_ge(chain, TT)
            pe.wait_ge(asum_done, 1)
            for b in range(NB):
                for i, parts in enumerate(((vision,), (text, every))):
                    for j, mask in enumerate(parts):
                        at = 2 * b + i
                        ins = nc.tensor.matmul(odd_ps[:, at:at + 1], mask[:], asum[:, 2 * b + j:2 * b + j + 1],
                                               start=j == 0, stop=j == len(parts) - 1)
            ins.then_inc(str_ready, 1)
            turn(x_acc, x2T_ready, 0)
            pe.wait_ge(x2T_done, KD)
            pe.wait_ge(chain, TT + 4)
            for t in range(TT):
                for k in range(KD):
                    at = 16 + NE * t
                    ins = nc.tensor.matmul(odd_ps[:, at:at + NE], x2T[:, k, t * P:(t + 1) * P], gate_w[:, k, :],
                                           start=k == 0, stop=k == KD - 1)
            ins.then_inc(lg_ready, 1)

            def up(e):
                for f in range(KD):
                    if e:
                        pe.wait_ge(act_done, KD * (e - 1) + f + 1)
                    for k in range(KD):
                        ins = nc.tensor.matmul(banks[f], w1[:, e, k, f * P:(f + 1) * P], x2T[:, k, :],
                                               start=k == 0, stop=k == KD - 1)
                    ins.then_inc(pre_ready, 1)

            def down(e):
                pe.wait_ge(act_done, KD * (e + 1))
                for t in range(TT):
                    if e:
                        pe.wait_ge(moe_done, TT * (e - 1) + t + 1)
                    for f in range(KD):
                        ins = nc.tensor.matmul(banks[4 + t], actT[e % 2][:, f, t * P:(t + 1) * P], w2[:, e, f, :],
                                               start=f == 0, stop=f == KD - 1)
                    ins.then_inc(moe_ready, 1)

            pe.wait_ge(w1_in, 16)
            up(0)
            pe.wait_ge(sel_done, 1)
            for b in range(NB):
                at = 64 + 2 * NE * b
                ins = nc.tensor.matmul(odd_ps[:, at:at + 2 * NE], first[:],
                                       sel[:, 2 * b].rearrange("p i e -> p (i e)"), start=True, stop=True)
            ins.then_inc(sel_ready, 1)
            pe.wait_ge(w2_in, 16)
            pe.wait_ge(chain, SEL_B)
            up(1)
            down(0)
            up(2)
            down(1)
            down(2)


V = {"ms": 2, "xn": 6, "hT0": 8, "hT1": 9, "hT2": 10, "hT3": 11, "u": 12, "dtT": 26, "acs": 32, "parts": 38,
     "start": 40, "var": 49, "ln": 53}
S = {"eT": 10}
E = {"dt": 5, "dt_tr": 6, "dec_tr": 7}


def kernel(**inputs):
    import numpy as np
    import concourse.bacc as bacc
    from concourse.bass_utils import run_bass_kernel_spmd

    w = {k: np.asarray(v) for k, v in inputs.items()}

    def columns(vec, n):
        return np.ascontiguousarray(vec.reshape(n, P).T)

    def weight_tiles(rows):
        n = rows.shape[0] // P
        return rows.reshape(n, P, KD, P).transpose(0, 3, 2, 1)

    wi = w["L0_attn_in_proj_w"]
    parts = {}
    gate_w, hid_w = weight_tiles(wi[:DIN]), weight_tiles(wi[DIN:2 * DIN])
    b_w = weight_tiles(wi[2 * DIN:2 * DIN + GROUPS * NST])
    c_w = weight_tiles(wi[2 * DIN + GROUPS * NST:2 * DIN + 2 * GROUPS * NST])
    parts["w_main"] = np.stack([hid_w, gate_w], axis=2)
    parts["w_bc"] = np.stack([b_w, c_w], axis=2)
    parts["w_dt"] = weight_tiles(wi[2 * DIN + 2 * GROUPS * NST:])[0]
    parts["w_out"] = w["L0_attn_out_proj_w"].T.reshape(GROUPS, U, P, D).transpose(0, 2, 1, 3)
    parts["x"] = w["x"].reshape(TT, P, D).transpose(1, 0, 2)
    nch = TILES + 2 * GROUPS
    parts["conv_w"] = w["L0_attn_conv_w"].reshape(nch, P, KC).transpose(1, 0, 2)
    parts["conv_b"] = columns(w["L0_attn_conv_b"], nch)
    parts["norm_w"] = columns(w["L0_attn_norm_w"], KD)
    parts["gnorm"] = columns(w["L0_attn_gnorm_w"], TILES)
    parts["d_skip"] = columns(np.repeat(w["L0_attn_Dp"], HD), TILES)
    parts["dt_bias"] = w["L0_attn_dt_bias"].reshape(HEADS, 1)
    parts["a_log"] = w["L0_attn_A_log"].reshape(HEADS, 1)
    parts["ident"] = np.eye(P, dtype=np.float32)
    parts["causal"] = np.triu(np.ones((P, P), np.float32))

    def rows_k(m):
        return m.reshape(-1, P, m.shape[-1]).transpose(1, 0, 2)

    parts["ctxT"] = rows_k(w["ctx_4096"].reshape(CT, D).T)
    parts["wk"], parts["wv"] = rows_k(w["L0_xattn_Wk"]), rows_k(w["L0_xattn_Wv"])
    parts["wq"], parts["wo"] = rows_k(w["L0_xattn_Wq"]), rows_k(w["L0_xattn_Wo"])
    parts["w1"] = w["L0_ffn_w1"].reshape(NE, KD, P, D).transpose(2, 0, 1, 3)
    parts["w2"] = w["L0_ffn_w2"].reshape(NE, KD, P, D).transpose(2, 0, 1, 3)
    parts["b1"] = w["L0_ffn_b1"].reshape(NE, KD, P).transpose(2, 0, 1)
    parts["b2"] = w["L0_ffn_b2"]
    parts["gate_w"] = rows_k(w["L0_ffn_gate_w"][:D])
    parts["gate_r"] = w["L0_ffn_gate_w"][D]
    parts["gate_b"] = w["L0_ffn_gate_b"]
    token = np.arange(P).reshape(P, 1) * np.ones((1, P))
    parts["vision"] = (token < VIS).astype(np.float32)
    parts["text"] = (token >= VIS).astype(np.float32)
    parts["every"] = np.ones((P, P), np.float32)
    parts["first"] = (token == 0).astype(np.float32)

    nc = bacc.Bacc("TRN2", target_bir_lowering=False, num_devices=1)
    arrays, aps = {}, {}
    for name, a in parts.items():
        arrays["in_" + name] = np.ascontiguousarray(a)
        aps[name] = nc.dram_tensor("in_" + name, a.shape, F32, kind="ExternalInput").ap()
    aps["out"] = nc.dram_tensor("out_dram", [P, TT, D], F32, kind="ExternalOutput").ap()
    decoder_program(nc, aps)
    r = run_bass_kernel_spmd(nc, [arrays], core_ids=[0])
    got = np.asarray(r.results[0]["out_dram"]).reshape(P, TT, D)
    return np.ascontiguousarray(got.transpose(1, 0, 2).reshape(NB, SEQ, D))
```

```python
from contextlib import ExitStack

import concourse.bass as bass
from concourse import mybir

ALU = mybir.AluOpType
ACT = mybir.ActivationFunctionType
AX = mybir.AxisListType
F32 = mybir.dt.float32
BF16 = mybir.dt.bfloat16
F32R = mybir.dt.float32r

P = 128
NB, SEQ, D = 2, 256, 512
T = NB * SEQ
TT = T // P
KD = D // P
HEADS, HD, GROUPS, NST = 128, 64, 8, 128
DIN = HEADS * HD
TILES = DIN // P
U = TILES // GROUPS
HG = HEADS // GROUPS
KC = 4
GCH = DIN // GROUPS
EPS = 1e-5
EB = SEQ
CS = 512
CT = NB * CS
AH, KVH, AD = 32, 8, 16
REP = AH // KVH
KVW = KVH * AD
SCALE = AD ** -0.5
NE = 3
VIS = int(SEQ * 0.3)
SEL_B = 35
RING = 3
PAIRS = U + 1
WR = 3
BIG = 1e38


def decoder_program(nc, A):
    with ExitStack() as ctx:
        x_acc = ctx.enter_context(nc.sbuf_tensor("x_acc", [P, TT, D], F32))
        ssm_block(nc, A, x_acc)
        attention_ffn_block(nc, A, x_acc)


def ssm_block(nc, A, x_acc):
    acs_pos = nc.dram_tensor("acs_pos", [3, HEADS, T], BF16).ap()
    acs_neg = nc.dram_tensor("acs_neg", [3, HEADS, T], BF16).ap()
    exp_acs = nc.dram_tensor("exp_acs", [HEADS, NB, P], F32).ap()

    with ExitStack() as ctx:
        def sb(name, shape, dt=F32):
            return ctx.enter_context(nc.sbuf_tensor(name, shape, dt))

        def sem(name):
            return ctx.enter_context(nc.semaphore(name))

        def bank(name):
            return ctx.enter_context(nc.psum_tensor(name, [P, 512], F32))

        proj_ps = [bank("proj_ps0"), bank("proj_ps1")]
        tr_ps = bank("tr_ps")
        dif_ps = [bank("dif_ps0"), bank("dif_ps1")]
        y_ps = bank("y_ps")
        st_ps = bank("st_ps")
        off_ps = bank("off_ps")

        out_ps = [dif_ps[0], dif_ps[1], tr_ps, st_ps]

        ident = sb("ident", [P, P])
        causal = sb("causal", [P, P])
        ones = sb("ones", [P, P])
        norm_w = sb("norm_w", [P, KD])
        conv_w = sb("conv_w", [P, TILES + 2 * GROUPS, KC])
        conv_b = sb("conv_b", [P, TILES + 2 * GROUPS])
        d_skip = sb("d_skip", [P, TILES])
        gnorm = sb("gnorm", [P, TILES])
        dt_bias = sb("dt_bias", [P, 1])
        a_log = sb("a_log", [P, 1])
        h_hi = sb("h_hi", [P, KD, T], F32R)
        h_lo = sb("h_lo", [P, KD, T], F32R)
        ident_b = sb("ident_b", [P, P], BF16)
        above = sb("above", [P, TT, P], BF16)
        dt_tok = sb("dt_tok", [P, TT, HEADS])
        dec_tok = sb("dec_tok", [P, NB, HEADS])
        w_raw = sb("w_raw", [P, WR, 2, KD, P])
        w_hi = sb("w_hi", [P, WR, KD, P], F32R)
        w_lo = sb("w_lo", [P, WR, KD, P], F32R)
        wo_raw = sb("wo_raw", [P, 2, 2, D])
        wo_hi = sb("wo_hi", [P, U, D], F32R)
        wo_lo = sb("wo_lo", [P, U, D], F32R)
        dif_l = sb("dif_l", [P, HG // 4, T], BF16)
        dif_r = sb("dif_r", [P, HG // 4, T], BF16)
        e_bc = sb("e_bc", [P, 2, 2, NB, P])
        bT = sb("bT", [P, T])
        cT = sb("cT", [P, T])
        b_tok = sb("b_tok", [P, NB, P])
        cb = sb("cb", [P, T])
        m_mat = sb("m_mat", [P, HG, T])
        conv_acc = sb("conv_acc", [P, 2, T])
        hid = sb("hid", [P, 2, T])
        gate = sb("gate", [P, 2, T])
        hc = sb("hc", [P, 2, TT, P])
        hcd = sb("hcd", [P, 2, NB, P])
        state = sb("state", [P, 2, NB, P])
        y_tmp = sb("y_tmp", [P, 2, T])
        off_tmp = sb("off_tmp", [P, 2, NB, P])
        y_hi = sb("y_hi", [P, U, T], F32R)
        y_lo = sb("y_lo", [P, U, T], F32R)
        sq_sum = sb("sq_sum", [P, T])
        mean_sq = sb("mean_sq", [P, TT])
        rstd_g = sb("rstd_g", [P, TT])
        minus_half = sb("minus_half", [P, 8])
        ss = sb("ss", [P, TT])
        rs = sb("rs", [P, TT])
        lead = sb("lead", [P, 8])
        lead_act = sb("lead_act", [P, 2])
        bn6 = sb("bn6", [P, TT, 6])
        mv = sb("mv", [P, TT, 2])
        a_neg = sb("a_neg", [P, 1])
        a_exp = sb("a_exp", [P, 1])

        sq = bT

        x_norm = m_mat[:, 0:4, :]
        dt_u = m_mat[:, 4, :]
        dt_abs = m_mat[:, 5, :]
        dt_e = m_mat[:, 6, :]
        dt_den = m_mat[:, 7, :]
        dt_z = m_mat[:, 8, :]
        dt_z2 = m_mat[:, 9, :]
        dt_s = m_mat[:, 10, :]
        dtT = m_mat[:, 11, :]
        acs = m_mat[:, 12, :]
        rest = m_mat[:, 13, :]
        decT = m_mat[:, 14, 0:NB * P]
        eT = m_mat[:, 14, NB * P:2 * NB * P]
        aT = m_mat[:, 15, :]
        rest2 = y_tmp[:, 1, :]
        sq_junk = y_tmp[:, 0, :]
        w_dt = gate[:, 0, :].rearrange("p (k o) -> p k o", k=KD)
        hT = [conv_acc[:, 0, :], conv_acc[:, 1, :], hid[:, 0, :], hid[:, 1, :]]
        x_tok = wo_raw[:].rearrange("p a b d -> p (a b) d")
        all_parts = m_mat[:, 0:3, :].rearrange("p k t -> p (k t)").bitcast(BF16).rearrange(
            "p (k t) -> p k t", k=6)
        parts, nparts = all_parts[:, 0:3, :], all_parts[:, 3:6, :]

        h_split = sem("h_split"); h_low = sem("h_low"); s_const = sem("s_const"); s_chan = sem("s_chan"); s_x = sem("s_x"); s_wdt = sem("s_wdt")
        w_loaded = [sem(f"w_loaded{i}") for i in range(WR)]
        w_hi_done = sem("w_hi_done"); w_lo_done = sem("w_lo_done")
        dif_loaded = sem("dif_loaded")
        e_loaded = [sem(f"e_loaded{i}") for i in range(2)]; wo_loaded = [sem(f"wo_loaded{i}") for i in range(2)]
        scratch_out = sem("scratch_out");
        act_step = sem("act_step"); vec_step = sem("vec_step"); pool_step = sem("pool_step")
        pe_step = sem("pe_step")
        proj_ready = sem("proj_ready"); dif_ready = sem("dif_ready"); exp_done = sem("exp_done")
        tap_done = sem("tap_done"); conv_step = sem("conv_step"); conv_done = sem("conv_done")
        hid_ready = sem("hid_ready"); gate_done = sem("gate_done")
        tr_ready = sem("tr_ready"); hc_done = sem("hc_done"); hcd_done = sem("hcd_done")
        cb_ready = sem("cb_ready"); cb_done = sem("cb_done"); m_done = sem("m_done")
        st_ready = sem("st_ready"); st_copied = sem("st_copied")
        yd_ready = sem("yd_ready"); off_ready = sem("off_ready"); comb_done = sem("comb_done"); within_done = sem("within_done")
        y_added = sem("y_added"); y_hi_done = sem("y_hi_done"); y_lo_done = sem("y_lo_done"); gated = sem("gated"); sq_done = sem("sq_done")
        squared = sem("squared"); wo_hi_done = sem("wo_hi_done"); wo_lo_done = sem("wo_lo_done"); ss_ready = sem("ss_ready"); ms_done = sem("ms_done")
        rstd_ready = sem("rstd_ready"); out_ready = sem("out_ready"); out_added = sem("out_added")
        block = ctx.enter_context(nc.Block())

        HV = 2 * PAIRS
        def hid_half(u):
            return 2 + 2 * u
        def gate_half(u):
            return 3 + 2 * u

        @block.sync
        def _(sp):
            sp.dma_start(x_tok[:], A["x"]).then_inc(s_x, 16)
            for dst, src in ((ident, "ident"), (causal, "causal"), (norm_w, "norm_w"), (dt_bias, "dt_bias"),
                             (a_log, "a_log")):
                sp.dma_start(dst[:], A[src]).then_inc(s_const, 16)
            sp.dma_start(w_dt, A["w_dt"]).then_inc(s_wdt, 16)

            def load_w(g, j):
                sp.dma_start(w_raw[:, j % WR], A["w_main"][bass.ds(g * PAIRS + j, 1)].rearrange(
                    "a p j k o -> (a p) j k o")).then_inc(w_loaded[j % WR], 16)

            def load_dif(g):
                for r in range(4):
                    for dst, src, row in ((dif_l, acs_neg, 3), (dif_r, acs_pos, 0)):
                        sp.dma_start(dst[32 * r + row:32 * r + row + 3],
                                     src[:, bass.ds(g * HG + r, HG // 4, 4), :]).then_inc(dif_loaded, 16)

            def load_e(g, q):
                for half in range(2):
                    src = exp_acs[bass.ds(g * HG + 4 * q + half, 2, 2)]
                    sp.dma_start(e_bc[half * HD:(half + 1) * HD, q % 2],
                                 src.unsqueeze(0).to_broadcast([HD, 2, NB, P])).then_inc(e_loaded[q % 2], 16)

            def load_wo(g, q):
                sp.dma_start(wo_raw[:, q % 2], A["w_out"][bass.ds(g * (U // 2) + q, 1)].rearrange(
                    "a p u o -> (a p) u o")).then_inc(wo_loaded[q % 2], 16)

            for j in range(WR):
                load_w(0, j)
            for dst, src in ((ident_b, "ident_b"), (above, "above"), (conv_w, "conv_w"), (conv_b, "conv_b"), (d_skip, "d_skip"), 
                             (gnorm, "gnorm")):
                sp.dma_start(dst[:], A[src]).then_inc(s_chan, 16)
            sp.wait_ge(vec_step, V["x2"])
            load_wo(0, 0)
            load_wo(0, 1)
            sp.wait_ge(vec_step, V["parts"])
            sp.dma_start(acs_pos.rearrange("k h t -> h k t"), parts[:]).then_inc(scratch_out, 16)
            sp.dma_start(acs_neg.rearrange("k h t -> h k t"), nparts[:]).then_inc(scratch_out, 16)
            sp.wait_ge(act_step, S["eT"])
            sp.dma_start(exp_acs.rearrange("h b t -> h (b t)"), eT).then_inc(scratch_out, 16)
            sp.wait_ge(scratch_out, 48)
            sp.wait_ge(pool_step, 3)
            load_dif(0)
            load_e(0, 0)
            load_e(0, 1)

            def refill_w(g, j, ahead=0):
                sp.wait_ge(w_lo_done, HV * (g + ahead) + 2 * (j - WR) + 2)
                load_w(g + ahead, j)

            def refill_wo(g, q, ahead=0):
                sp.wait_ge(wo_lo_done, U * (g + ahead) + 2 * (q - 2) + 2)
                load_wo(g + ahead, q)

            def refill_e(g, q, ahead=0):
                sp.wait_ge(comb_done, U * (g + ahead) + 2 * (q - 2) + 2 + 1)
                load_e(g + ahead, q)

            def group(g, last):
                refill_w(g, 3)
                if not last:
                    sp.wait_ge(dif_ready, HG * g + HG)
                    load_dif(g + 1)
                for j in (4, 5, 6):
                    refill_w(g, j)
                refill_wo(g, 2)
                refill_w(g, 7)
                refill_wo(g, 3)
                refill_w(g, 8)
                refill_e(g, 2)
                refill_w(g, 0, 1)
                refill_e(g, 3)
                if not last:
                    refill_wo(g, 0, 1)
                refill_w(g, 1, 1)
                refill_w(g, 2, 1)
                if not last:
                    refill_wo(g, 1, 1)
                    refill_e(g, 0, 1)
                    refill_e(g, 1, 1)

            with sp.Fori(0, GROUPS - 1) as g:
                group(g, False)
            group(GROUPS - 1, True)
            sp.wait_ge(vec_step, V["ln"])

        @block.gpsimd
        def _(pool):
            nc.gpsimd.memset(dif_l[:], 1.0).then_inc(pool_step, 1)
            nc.gpsimd.memset(dif_r[:], 1.0).then_inc(pool_step, 1)
            nc.gpsimd.memset(minus_half[:], -0.5).then_inc(pool_step, 1)
            pool.wait_ge(pool_step, 3)
            pool.wait_ge(vec_step, V["ms"])
            nc.gpsimd.tensor_tensor(rs[:], ss[:], minus_half[:, 0:TT], ALU.pow).then_inc(pool_step, 1)
            with pool.Fori(0, GROUPS) as g:
                def decay(u):
                    pool.wait_ge(hc_done, (U + 1) * g + 2 + u)
                    for hh in range(2):
                        ins = nc.gpsimd.tensor_tensor(
                            hcd[:, u % 2, :, hh * HD:(hh + 1) * HD], hc[:, u % 2, 0:TT:2, hh * HD:(hh + 1) * HD],
                            dec_tok[:, :, bass.ds(g * HG + 2 * u + hh, 1)].to_broadcast([P, NB, HD]), ALU.mult)
                    ins.then_inc(hcd_done, 1)

                def gated_y(u):
                    pool.wait_ge(comb_done, U * g + u + 1 + 1)
                    late = y_tmp[:, u % 2, :].rearrange("p (b c t) -> p b c t", b=NB, c=2)[:, :, 1, :]
                    nc.gpsimd.tensor_tensor(late, late, off_tmp[:, u % 2], ALU.add).then_inc(y_added, 1)
                    pool.wait_ge(gate_done, U * g + u + 1 + 1)
                    pool.wait_ge(y_added, U * g + u + 1)
                    nc.gpsimd.tensor_tensor(y_tmp[:, u % 2, :], y_tmp[:, u % 2, :], gate[:, u % 2, :],
                                            ALU.mult).then_inc(gated, 1)

                def low_y(u):
                    pool.wait_ge(y_hi_done, U * g + u + 1)
                    nc.gpsimd.tensor_tensor(y_lo[:, u, :], y_tmp[:, u % 2, :], y_hi[:, u, :].bitcast(F32),
                                            ALU.subtract).then_inc(y_lo_done, 1)
                    pool.wait_ge(squared, U * g + u + 1)
                    if u:
                        pool.wait_ge(sq_done, U * g + u + 1)
                        nc.gpsimd.tensor_tensor(sq_sum[:], sq_sum[:], sq[:], ALU.add).then_inc(sq_done, 1)
                    else:
                        nc.gpsimd.tensor_tensor(sq_sum[:].rearrange("p (c t) -> p c t", c=TT),
                                                sq[:].rearrange("p (c t) -> p c t", c=TT),
                                                ones[:].unsqueeze(1).to_broadcast([P, TT, P]), ALU.mult
                                                ).then_inc(sq_done, 1)

                decay(0)
                for u in range(2, U):
                    decay(u - 1)
                    gated_y(u - 2)
                    low_y(u - 2)
                decay(U - 1)
                gated_y(U - 2)
                low_y(U - 2)
                gated_y(U - 1)
                low_y(U - 1)
                pool.wait_ge(ms_done, g + 1 + 1)
                nc.gpsimd.tensor_tensor(rstd_g[:], mean_sq[:], minus_half[:, 0:TT], ALU.pow).then_inc(rstd_ready, 1)
            pool.wait_ge(vec_step, V["var"])
            nc.gpsimd.tensor_tensor(rs[:], ss[:], minus_half[:, 0:TT], ALU.pow).then_inc(pool_step, 1)

        @block.scalar
        def _(act):
            act.wait_ge(s_x, 16)
            for t in range(TT):
                nc.scalar.activation(sq_junk, x_tok[:, t, :], ACT.Square, accum_out=ss[:, t:t + 1]).then_inc(act_step, 1)
                if t < TT - 1:
                    act.wait_ge(act_step, t + 1)
            act.wait_ge(s_const, 5 * 16)
            nc.scalar.activation(a_exp[:], a_log[:], ACT.Exp).then_inc(act_step, 1)
            act.wait_ge(pe_step, E["dt"])
            act.wait_ge(vec_step, V["u"])
            nc.scalar.activation(dt_abs, dt_u, ACT.Abs).then_inc(act_step, 1)
            act.wait_ge(act_step, 6)
            nc.scalar.activation(dt_e, dt_abs, ACT.Exp, scale=-1.0).then_inc(act_step, 1)
            act.wait_ge(vec_step, V["acs"])
            for b in range(NB):
                last = acs[:, b * EB + P - 1:b * EB + P]
                nc.scalar.activation(decT[:, b * P:(b + 1) * P], acs[:, b * EB:b * EB + P], ACT.Exp, bias=last,
                                     scale=-1.0).then_inc(act_step, 1)
            nc.scalar.activation(eT.rearrange("p (b t) -> p b t", b=NB),
                                 acs.rearrange("p (b t) -> p b t", b=NB)[:, :, P:2 * P], ACT.Exp).then_inc(act_step, 1)
            act.wait_ge(s_chan, 6 * 16)
            for k, s in enumerate((hid_ready, gate_done)):
                nc.scalar.copy(lead_act[:, k:k + 1], ones[:, 0:1]).then_inc(s, 1)
            for k in range(KD):
                act.wait_ge(vec_step, V["hT%d" % k])
                nc.scalar.copy(h_hi[:, k, :], hT[k]).then_inc(h_split, 1)

            def split_hi(g, n, ahead=0):
                j = n // 2
                act.wait_ge(w_loaded[j % WR], 16 * (PAIRS // WR * (g + ahead) + j // WR + 1))
                act.wait_ge(proj_ready, HV * (g + ahead) + n + 1)
                nc.scalar.copy(w_hi[:, n % WR].rearrange("p k o -> p (k o)"),
                               w_raw[:, j % WR, n % 2].rearrange("p k o -> p (k o)")).then_inc(w_hi_done, 1)

            act.wait_ge(vec_step, V["start"])
            for n in range(WR):
                split_hi(0, n)
            with act.Fori(0, GROUPS) as g:
                def tap(n, col, ps):
                    act.wait_ge(proj_ready, HV * g + (hid_half(n - 2) if n >= 2 else n) + 1 + WR)
                    act.wait_ge(hid_ready, (U + 2) * g + max(n - 1, 0) + 1)
                    nc.scalar.activation(conv_acc[:, n % 2, :], ps[:], ACT.Identity, bias=conv_b[:, col],
                                         scale=conv_w[:, col, KC - 1]).then_inc(tap_done, 1)

                def exps(h0, h1):
                    for h in range(h0, h1):
                        act.wait_ge(dif_ready, HG * g + h + 1)
                        nc.scalar.activation(m_mat[:, h, :], dif_ps[h % 2][:], ACT.Exp).then_inc(exp_done, 1)

                def silu(n, dst):
                    act.wait_ge(conv_done, (U + 2) * g + n + 1 + 1)
                    nc.scalar.activation(dst, conv_acc[:, n % 2, :], ACT.Silu).then_inc(hid_ready, 1)

                def hid_tile(u):
                    act.wait_ge(comb_done, U * g + max(u - 1, 0) + 1)
                    silu(2 + u, hid[:, u % 2, :])

                def silu_gate(u):
                    act.wait_ge(proj_ready, HV * g + gate_half(u) + 1 + WR)
                    if u >= 2:
                        act.wait_ge(gated, U * g + u - 1)
                    else:
                        act.wait_ge(y_lo_done, U * g + 1)
                    nc.scalar.activation(gate[:, u % 2, :], proj_ps[1][:], ACT.Silu).then_inc(gate_done, 1)

                def state_copy(u):
                    act.wait_ge(st_ready, U * g + u + 1)
                    nc.scalar.copy(state[:, u % 2], st_ps[:, 0:NB * P].rearrange("p (b t) -> p b t", b=NB)
                                   ).then_inc(st_copied, 1)

                def scale_wo(u):
                    if u % 2 == 0:
                        act.wait_ge(wo_loaded[u // 2 % 2], 16 * (2 * g + u // 4 + 1))
                    nc.scalar.activation(wo_hi[:, u, :], wo_raw[:, u // 2 % 2, u % 2, :], ACT.Copy,
                                         scale=gnorm[:, bass.ds(g * U + u, 1)]).then_inc(wo_hi_done, 1)

                def high_y(u):
                    act.wait_ge(gated, U * g + u + 1)
                    nc.scalar.copy(y_hi[:, u, :], y_tmp[:, u % 2, :]).then_inc(y_hi_done, 1)
                    act.wait_ge(sq_done, U * g + u + 1)
                    nc.scalar.activation(sq[:], y_tmp[:, u % 2, :], ACT.Square).then_inc(squared, 1)

                exps(0, 6)
                tap(0, bass.ds(TILES + g, 1), proj_ps[0])
                split_hi(g, gate_half(0))
                exps(6, 12)
                tap(1, bass.ds(TILES + GROUPS + g, 1), proj_ps[1])
                split_hi(g, hid_half(1))
                exps(12, 16)
                act.wait_ge(sq_done, U * g + 1)
                silu(0, bT[:])
                silu(1, cT[:])
                tap(2, bass.ds(g * U, 1), proj_ps[0])
                split_hi(g, gate_half(1))
                hid_tile(0)
                silu_gate(0)
                scale_wo(0)
                for u in range(1, U):
                    if u >= 2:
                        state_copy(u - 2)
                    if u < U - 1:
                        split_hi(g, hid_half(u + 1))
                    else:
                        split_hi(g, 0, 1)
                    tap(2 + u, bass.ds(g * U + u, 1), proj_ps[0])
                    if u < U - 1:
                        split_hi(g, gate_half(u + 1))
                    else:
                        split_hi(g, 1, 1)
                    hid_tile(u)
                    if u >= 2:
                        high_y(u - 2)
                    silu_gate(u)
                    scale_wo(u)
                state_copy(U - 2)
                split_hi(g, 2, 1)
                high_y(U - 2)
                state_copy(U - 1)
                high_y(U - 1)

        @block.vector
        def _(dve):
            n = [0]

            def step(ins, name=None):
                n[0] += 1
                ins.then_inc(vec_step, 1)
                if name:
                    assert V[name] == n[0], (name, n[0])
                dve.wait_ge(vec_step, n[0])

            step(nc.vector.memset(ones[:], 1.0))
            dve.wait_ge(act_step, 4)
            step(nc.vector.tensor_scalar(ss[:], ss[:], 1.0 / D, EPS, ALU.mult, ALU.add), "ms")
            dve.wait_ge(pool_step, 4)
            for t in range(TT):
                step(nc.vector.tensor_scalar(x_norm[:, t, :], x_tok[:, t, :], rs[:, t:t + 1], None, ALU.mult),
                     "xn" if t == TT - 1 else None)
            step(nc.vector.tensor_scalar(x_acc[:], x_tok[:], 2.0, None, ALU.mult), "x2")
            dve.wait_ge(s_const, 5 * 16)
            for k in range(KD):
                dve.wait_ge(pe_step, k + 1)
                step(nc.vector.tensor_scalar(hT[k], proj_ps[k % 2][:], norm_w[:, k:k + 1], None, ALU.mult),
                     "hT%d" % k)
            dve.wait_ge(pe_step, E["dt"])
            step(nc.vector.tensor_scalar(dt_u, proj_ps[0][:], dt_bias[:], None, ALU.add), "u")
            dve.wait_ge(act_step, 7)
            step(nc.vector.tensor_scalar(dt_den, dt_e, 2.0, None, ALU.add))
            step(nc.vector.reciprocal(dt_den, dt_den))
            step(nc.vector.tensor_tensor(dt_z, dt_e, dt_den, ALU.mult))
            step(nc.vector.tensor_tensor(dt_z2, dt_z, dt_z, ALU.mult))
            step(nc.vector.tensor_scalar(dt_s, dt_z2, 2.0 / 17, None, ALU.mult))
            for k in range(15, 1, -2):
                step(nc.vector.scalar_tensor_tensor(dt_s, dt_s, 2.0 / k, dt_z2, ALU.add, ALU.mult))
            step(nc.vector.scalar_tensor_tensor(dt_s, dt_s, 2.0, dt_z, ALU.add, ALU.mult))
            step(nc.vector.scalar_tensor_tensor(dtT, dt_u, 0.0, dt_s, ALU.max, ALU.add), "dtT")
            dve.wait_ge(act_step, 5)
            step(nc.vector.tensor_scalar(a_neg[:], a_exp[:], -1.0, None, ALU.mult))
            step(nc.vector.tensor_scalar(aT, dtT, a_neg[:], None, ALU.mult))
            for c in range(TT):
                step(nc.vector.tensor_tensor_scan(acs[:, c * P:(c + 1) * P], ones[:], aT[:, c * P:(c + 1) * P],
                                                  0.0, ALU.mult, ALU.add), "acs" if c == TT - 1 else None)
            step(nc.vector.tensor_copy(parts[:, 0, :], acs))
            step(nc.vector.tensor_tensor(rest, acs, parts[:, 0, :], ALU.subtract))
            step(nc.vector.tensor_copy(parts[:, 1, :], rest))
            step(nc.vector.tensor_tensor(rest2, rest, parts[:, 1, :], ALU.subtract))
            step(nc.vector.tensor_copy(parts[:, 2, :], rest2))
            step(nc.vector.tensor_scalar(nparts[:], parts[:], -1.0, None, ALU.mult), "parts")
            dve.wait_ge(pe_step, E["dt_tr"])
            step(nc.vector.tensor_copy(dt_tok[:], tr_ps[:].rearrange("p (c h) -> p c h", c=TT)))
            dve.wait_ge(pe_step, E["dec_tr"])
            step(nc.vector.tensor_copy(dec_tok[:], st_ps[:, 0:NB * P].rearrange("p (b h) -> p b h", b=NB)), "start")
            nc.vector.memset(rstd_g[:], 0.0).then_inc(out_added, TT)
            for k, s in enumerate((conv_done, comb_done, ms_done, y_lo_done)):
                nc.vector.memset(lead[:, k:k + 1], 0.0).then_inc(s, 1)
            nc.vector.memset(lead[:, 6:7], 0.0).then_inc(proj_ready, WR)
            nc.vector.memset(lead[:, 7:8], 0.0).then_inc(sq_done, 1)
            for k in range(KD):
                dve.wait_ge(h_split, k + 1)
                nc.vector.tensor_tensor(h_lo[:, k, :], hT[k], h_hi[:, k, :].bitcast(F32), ALU.subtract
                                        ).then_inc(h_low, 1)

            def split_lo(g, n, ahead=0):
                dve.wait_ge(w_hi_done, HV * (g + ahead) + n + 1)
                nc.vector.tensor_tensor(w_lo[:, n % WR].rearrange("p k o -> p (k o)"),
                                        w_raw[:, n // 2 % WR, n % 2].rearrange("p k o -> p (k o)"),
                                        w_hi[:, n % WR].rearrange("p k o -> p (k o)").bitcast(F32), ALU.subtract
                                        ).then_inc(w_lo_done, 1)

            for first in range(WR):
                split_lo(0, first)
            dve.wait_ge(s_chan, 6 * 16)

            with dve.Fori(0, GROUPS) as g:
                def conv(n, col, ps, between=()):
                    dve.wait_ge(tap_done, (U + 2) * g + n + 1)
                    acc = conv_acc[:, n % 2, :].rearrange("p (b t) -> p b t", b=NB)
                    src = ps[:].rearrange("p (b t) -> p b t", b=NB)
                    for k in range(1, KC):
                        ins = nc.vector.scalar_tensor_tensor(
                            acc[:, :, k:], src[:, :, :SEQ - k], conv_w[:, col, KC - 1 - k], acc[:, :, k:],
                            ALU.mult, ALU.add)
                        if k < KC - 1:
                            ins.then_inc(conv_step, 1)
                            if between:
                                between[k - 1]()
                            dve.wait_ge(conv_step, (KC - 2) * ((U + 2) * g + n) + k)
                        else:
                            ins.then_inc(conv_done, 1)

                def to_tokens(u):
                    dve.wait_ge(tr_ready, (U + 1) * g + 2 + u)
                    nc.vector.tensor_tensor(
                        hc[:, u % 2].rearrange("p c (h d) -> p c h d", h=2),
                        tr_ps[:].rearrange("p (c h d) -> p c h d", c=TT, h=2),
                        dt_tok[:, :, bass.ds(g * HG + 2 * u, 2)].unsqueeze(3).to_broadcast([P, TT, 2, HD]),
                        ALU.mult).then_inc(hc_done, 1)

                def mix_head(h):
                    dve.wait_ge(exp_done, HG * g + h + 1)
                    nc.vector.tensor_tensor(m_mat[:, h, :], m_mat[:, h, :], cb[:], ALU.mult).then_inc(m_done, 1)

                def within(u):
                    dve.wait_ge(yd_ready, U * g + u + 1)
                    dve.wait_ge(y_lo_done, U * g + max(u - 1, 0) + 1)
                    dve.wait_ge(sq_done, U * g + max(u - 1, 0) + 1)
                    nc.vector.scalar_tensor_tensor(y_tmp[:, u % 2, :], hid[:, u % 2, :],
                                                   d_skip[:, bass.ds(g * U + u, 1)], y_ps[:], ALU.mult, ALU.add
                                                   ).then_inc(within_done, 1)

                def carried(u):
                    dve.wait_ge(e_loaded[u // 2 % 2], 32 * (2 * g + u // 4 + 1))
                    dve.wait_ge(off_ready, U * g + u + 1)
                    dve.wait_ge(within_done, U * g + u + 1)
                    nc.vector.tensor_tensor(off_tmp[:, u % 2], off_ps[:, 0:NB * P].rearrange("p (b t) -> p b t", b=NB),
                                            e_bc[:, u // 2 % 2, u % 2], ALU.mult).then_inc(comb_done, 1)

                def low_wo(u):
                    dve.wait_ge(wo_hi_done, U * g + u + 1)
                    nc.vector.scalar_tensor_tensor(wo_lo[:, u, :], wo_raw[:, u // 2 % 2, u % 2, :],
                                                   gnorm[:, bass.ds(g * U + u, 1)], wo_hi[:, u, :].bitcast(F32),
                                                   ALU.mult, ALU.subtract).then_inc(wo_lo_done, 1)

                conv(0, bass.ds(TILES + g, 1), proj_ps[0])
                split_lo(g, gate_half(0))
                conv(1, bass.ds(TILES + GROUPS + g, 1), proj_ps[1])
                split_lo(g, hid_half(1))
                conv(2, bass.ds(g * U, 1), proj_ps[0])
                dve.wait_ge(tr_ready, (U + 1) * g + 1)
                nc.vector.tensor_copy(b_tok[:], tr_ps[:, 0:NB * P].rearrange("p (b t) -> p b t", b=NB)
                                      ).then_inc(hc_done, 1)
                dve.wait_ge(cb_ready, g + 1)
                nc.vector.tensor_tensor(cb[:].rearrange("p (c t) -> p c t", c=TT),
                                        y_ps[:].rearrange("p (c t) -> p c t", c=TT),
                                        causal[:].unsqueeze(1).to_broadcast([P, TT, P]), ALU.mult
                                        ).then_inc(cb_done, 1)
                dve.wait_ge(cb_done, g + 1)
                split_lo(g, gate_half(1))
                mix_head(0)
                mix_head(1)
                low_wo(0)
                for u in range(1, U):
                    to_tokens(u - 1)
                    if u < U - 1:
                        split_lo(g, hid_half(u + 1))
                    else:
                        split_lo(g, 0, 1)
                    conv(2 + u, bass.ds(g * U + u, 1), proj_ps[0],
                         (lambda: carried(u - 2) if u >= 2 else None, lambda: mix_head(2 * u)))
                    mix_head(2 * u + 1)
                    if u < U - 1:
                        split_lo(g, gate_half(u + 1))
                    else:
                        split_lo(g, 1, 1)
                    within(u - 1)
                    low_wo(u)
                to_tokens(U - 1)
                carried(U - 2)
                split_lo(g, 2, 1)
                within(U - 1)
                carried(U - 1)
                dve.wait_ge(ss_ready, g + 1)
                nc.vector.tensor_scalar(mean_sq[:], off_ps[:, 0:TT], 1.0 / GCH, EPS, ALU.mult, ALU.add
                                        ).then_inc(ms_done, 1)
                dve.wait_ge(rstd_ready, g + 1)
                for t in range(TT):
                    dve.wait_ge(out_ready, TT * g + t + 1)
                    dve.wait_ge(out_added, TT * g + t + 1)
                    nc.vector.scalar_tensor_tensor(x_acc[:, t, :], out_ps[t][:], rstd_g[:, t:t + 1], x_acc[:, t, :],
                                                   ALU.mult, ALU.add).then_inc(out_added, 1)
            dve.wait_ge(out_added, TT * (GROUPS + 1))
            for t in range(TT):
                step(nc.vector.bn_stats(bn6[:, t, :], x_acc[:, t, :]))
            for t in range(TT):
                step(nc.vector.bn_aggr(mv[:, t, :], bn6[:, t, :]))
            step(nc.vector.tensor_scalar(ss[:], mv[:, :, 1], EPS, None, ALU.add), "var")
            dve.wait_ge(pool_step, 5)
            for t in range(TT):
                step(nc.vector.tensor_scalar(x_acc[:, t, :], x_acc[:, t, :], mv[:, t, 0:1], rs[:, t:t + 1],
                                             ALU.subtract, ALU.mult), "ln" if t == TT - 1 else None)

        @block.tensor
        def _(pe):
            pe.wait_ge(vec_step, V["xn"])
            pe.wait_ge(s_const, 5 * 16)
            for k in range(KD):
                if k >= 2:
                    pe.wait_ge(vec_step, V["hT%d" % (k - 2)])
                for t in range(TT):
                    ins = nc.tensor.transpose(proj_ps[k % 2][:, t * P:(t + 1) * P],
                                              x_norm[:, t, k * P:(k + 1) * P], ident[:])
                ins.then_inc(pe_step, 1)
            pe.wait_ge(vec_step, V["hT%d" % (KD - 1)])
            pe.wait_ge(s_wdt, 16)
            for k in range(KD):
                ins = nc.tensor.matmul(proj_ps[0][:], w_dt[:, k, :], hT[k], start=k == 0, stop=k == KD - 1)
            ins.then_inc(pe_step, 1)
            pe.wait_ge(vec_step, V["dtT"])
            for c in range(TT):
                ins = nc.tensor.transpose(tr_ps[:, c * P:(c + 1) * P], dtT[:, c * P:(c + 1) * P], ident[:])
            ins.then_inc(pe_step, 1)
            pe.wait_ge(act_step, 9)
            for b in range(NB):
                ins = nc.tensor.transpose(st_ps[:, b * P:(b + 1) * P], decT[:, b * P:(b + 1) * P], ident[:])
            ins.then_inc(pe_step, 1)
            pe.wait_ge(vec_step, V["start"])
            pe.wait_ge(h_low, KD)
            pe.wait_ge(s_chan, 6 * 16)
            with pe.Fori(0, GROUPS) as g:
                def project(n, ks=range(KD)):
                    ps = proj_ps[n % 2]
                    if 0 in ks:
                        pe.wait_ge(w_lo_done, HV * g + n + 1)
                        if n == 0:
                            pe.wait_ge(conv_done, (U + 2) * g + 1)
                        elif n == 1:
                            pe.wait_ge(gate_done, U * g + 1)
                        elif n == 3:
                            pe.wait_ge(conv_done, (U + 2) * g + 2 + 1)
                        elif n % 2:
                            pe.wait_ge(gate_done, U * g + (n - 3) // 2 + 1)
                        else:
                            u = (n - 2) // 2
                            pe.wait_ge(conv_done, (U + 2) * g + (u + 2 if u else 1) + 1)
                    for k in ks:
                        for i, (w, h) in enumerate(((w_hi, h_hi), (w_hi, h_lo), (w_lo, h_hi))):
                            ins = nc.tensor.matmul(ps[:], w[:, n % WR, k, :], h[:, k, :], start=k == 0 and i == 0,
                                                   stop=k == KD - 1 and i == 2)
                    if KD - 1 in ks:
                        ins.then_inc(proj_ready, 1)

                def difs(h0, h1):
                    for h in range(h0, h1):
                        if h >= 2:
                            pe.wait_ge(exp_done, HG * g + h - 1)
                        r, j = 32 * (h % 4), h // 4
                        nc.tensor.matmul(dif_ps[h % 2][:], ident_b[:], above[:].rearrange("p c t -> p (c t)"),
                                         start=True, stop=False)
                        for c in range(TT):
                            cols = slice(c * P, (c + 1) * P)
                            ins = nc.tensor.matmul(dif_ps[h % 2][:, cols], dif_l[r:r + 6, j, cols],
                                                   dif_r[r:r + 6, j, cols], start=False, stop=c == TT - 1)
                        ins.then_inc(dif_ready, 1)

                def transposes(u):
                    pe.wait_ge(hid_ready, (U + 2) * g + 3 + u + 1)
                    pe.wait_ge(hc_done, (U + 1) * g + 1 + u)
                    for c in range(TT):
                        cols = slice(c * P, (c + 1) * P)
                        ins = nc.tensor.transpose(tr_ps[:, cols], hid[:, u % 2, cols], ident[:])
                    ins.then_inc(tr_ready, 1)

                def states(u):
                    pe.wait_ge(hcd_done, U * g + u + 1)
                    if u == 0:
                        pe.wait_ge(out_added, TT * g + TT)
                    else:
                        pe.wait_ge(st_copied, U * g + u)
                    for b in range(NB):
                        ins = nc.tensor.matmul(st_ps[:, b * P:(b + 1) * P], b_tok[:, b, :], hcd[:, u % 2, b, :],
                                               start=True, stop=True)
                    ins.then_inc(st_ready, 1)

                def within(u):
                    if u == 0:
                        pe.wait_ge(cb_done, g + 1)
                    else:
                        pe.wait_ge(within_done, U * g + u)
                    pe.wait_ge(hc_done, (U + 1) * g + 2 + u)
                    pe.wait_ge(m_done, HG * g + 2 * u + 2)
                    for c in range(TT):
                        cols = slice(c * P, (c + 1) * P)
                        for hh in range(2):
                            rows = slice(hh * HD, (hh + 1) * HD)
                            ins = nc.tensor.matmul(y_ps[rows, cols], hc[:, u % 2, c, rows],
                                                   m_mat[:, 2 * u + hh, cols], start=True, stop=True)
                    ins.then_inc(yd_ready, 1)

                def carried(u):
                    pe.wait_ge(st_copied, U * g + u + 1)
                    if u == 0:
                        pe.wait_ge(ms_done, g + 1)
                    else:
                        pe.wait_ge(comb_done, U * g + u + 1)
                    for b in range(NB):
                        late = slice(b * EB + P, (b + 1) * EB)
                        ins = nc.tensor.matmul(off_ps[:, b * P:(b + 1) * P], state[:, u % 2, b, :], cT[:, late],
                                               start=True, stop=True)
                    ins.then_inc(off_ready, 1)

                def out_proj(t, ks):
                    for k in ks:
                        for i, (y, w) in enumerate(((y_hi, wo_hi), (y_hi, wo_lo), (y_lo, wo_hi))):
                            ins = nc.tensor.matmul(out_ps[t][:], y[:, k, t * P:(t + 1) * P], w[:, k, :],
                                                   start=k == 0 and i == 0, stop=k == U - 1 and i == 2)
                    if U - 1 in ks:
                        ins.then_inc(out_ready, 1)

                pe.wait_ge(dif_loaded, 128 * g + 128)
                pe.wait_ge(out_added, TT * g + 2)
                for n in range(2):
                    difs(6 * n, 6 * n + 3)
                    project(n, (0, 1))
                    difs(6 * n + 3, 6 * n + 6)
                    project(n, (2, 3))
                difs(12, 16)
                project(hid_half(0))
                project(gate_half(0), (0, 1))
                pe.wait_ge(hid_ready, (U + 2) * g + 1 + 1)
                pe.wait_ge(out_added, TT * g + 3)
                for b in range(NB):
                    ins = nc.tensor.transpose(tr_ps[:, b * P:(b + 1) * P], bT[:, b * EB:b * EB + P], ident[:])
                ins.then_inc(tr_ready, 1)
                project(gate_half(0), (2, 3))
                pe.wait_ge(hid_ready, (U + 2) * g + 2 + 1)
                pe.wait_ge(comb_done, U * g + 1)
                for c in range(TT):
                    cols = slice(c * P, (c + 1) * P)
                    ins = nc.tensor.matmul(y_ps[:, cols], bT[:, cols], cT[:, cols], start=True, stop=True)
                ins.then_inc(cb_ready, 1)
                for u in range(1, U):
                    project(hid_half(u), (0, 1))
                    transposes(u - 1)
                    project(hid_half(u), (2, 3))
                    if u >= 2:
                        carried(u - 2)
                    project(gate_half(u))
                    within(u - 1)
                    states(u - 1)
                pe.wait_ge(y_lo_done, U * g + 4 + 1)
                out_proj(0, range(0, 4))
                transposes(U - 1)
                out_proj(1, range(0, 4))
                carried(U - 2)
                within(U - 1)
                states(U - 1)
                pe.wait_ge(wo_lo_done, U * g + U)
                pe.wait_ge(y_lo_done, U * g + U - 2 + 1)
                out_proj(0, (4, 5))
                out_proj(1, (4, 5))
                carried(U - 1)
                pe.wait_ge(y_lo_done, U * g + U - 1 + 1)
                out_proj(0, (6,))
                out_proj(1, (6,))
                pe.wait_ge(hc_done, (U + 1) * g + U + 1)
                out_proj(2, range(7))
                out_proj(3, range(7))
                pe.wait_ge(sq_done, U * g + U + 1)
                pe.wait_ge(comb_done, U * g + U + 1)
                for t in range(TT):
                    ins = nc.tensor.matmul(off_ps[:, t:t + 1], sq_sum[:, t * P:(t + 1) * P], ones[:, 0:1],
                                           start=True, stop=True)
                ins.then_inc(ss_ready, 1)
                pe.wait_ge(y_lo_done, U * g + U + 1)
                for t in range(TT):
                    out_proj(t, (7,))




def attention_ffn_block(nc, A, x_acc):
    k_hi_d = nc.dram_tensor("k_hi_d", [P, CT], F32R).ap()
    k_lo_d = nc.dram_tensor("k_lo_d", [P, CT], F32R).ap()
    q_hi_d = nc.dram_tensor("q_hi_d", [KD, P, T], F32R).ap()
    q_lo_d = nc.dram_tensor("q_lo_d", [KD, P, T], F32R).ap()
    k_stack = nc.dram_tensor("k_stack", [KVH, 3 * AD, CT], F32R).ap().bitcast(F32)
    q_stack = nc.dram_tensor("q_stack", [2, KVH * REP // 2, 3 * AD, T], F32R).ap().bitcast(F32)

    with ExitStack() as ctx:
        def sb(name, shape, dt=F32):
            return ctx.enter_context(nc.sbuf_tensor(name, shape, dt))

        def sem(name):
            return ctx.enter_context(nc.semaphore(name))

        max_ps = ctx.enter_context(nc.psum_tensor("max_ps", [P, 2, 512], F32))
        sc_ps = [ctx.enter_context(nc.psum_tensor(f"sc_ps{i}", [P, 2, 512], F32)) for i in range(2)]
        pv_ps = ctx.enter_context(nc.psum_tensor("pv_ps", [P, 512], F32))
        odd_ps = ctx.enter_context(nc.psum_tensor("odd_ps", [P, 512], F32))
        banks = [max_ps[:, 0, :], max_ps[:, 1, :], sc_ps[0][:, 0, :], sc_ps[0][:, 1, :],
                 sc_ps[1][:, 0, :], sc_ps[1][:, 1, :], pv_ps[:], odd_ps[:]]

        ident = sb("ident2", [P, P])
        ctxT = sb("ctxT", [P, KD, CT])
        wk = sb("wk", [P, KD, KVW])
        wv = sb("wv", [P, KD, KVW])
        wq = sb("wq", [P, KD, D])
        wo = sb("wo", [P, KD, D])
        w1 = sb("w1", [P, NE, KD, D])
        w2 = sb("w2", [P, NE, KD, D])
        b1 = sb("b1", [P, NE, KD])
        b2 = sb("b2", [P, NE, D])
        gate_w = sb("gate_w", [P, KD, NE])
        gate_r = sb("gate_r", [P, NE])
        gate_b = sb("gate_b", [P, NE])
        vision = sb("vision", [P, P])
        text = sb("text", [P, P])
        every = sb("every", [P, P])
        first = sb("first", [P, P])
        k_hi = sb("k_hi", [P, CT], F32R)
        k_lo = sb("k_lo", [P, CT], F32R)
        v_tok = sb("v_tok", [P, CT // P, KVH, 2 * AD])
        x1T = sb("x1T", [P, KD, T])
        q_hi = sb("q_hi", [P, KD, T], F32R)
        q_lo = sb("q_lo", [P, KD, T], F32R)
        k_st = [sb(f"k_st{i}", [P, CT], F32R) for i in range(RING)]
        q_st = [sb(f"q_st{i}", [P, REP // 2, T], F32R) for i in range(RING)]
        nmax = sb("nmax", [P, RING, TT, REP])
        m_hi = sb("m_hi", [REP, RING, T], F32R)
        m_lo = sb("m_lo", [REP, RING, T], F32R)
        probs = sb("probs", [P, 2, 2 * 512])
        rden = sb("rden", [P, TT, REP])
        v_kv = [sb(f"v_kv{i}", [P, CT // P, 2 * AD]) for i in range(RING)]
        pv = sb("pv", [P, T])
        attn = sb("attn", [P, TT, D])
        attnT = x1T
        x2T = attn
        actT = [ctxT[:, :, 0:T], ctxT[:, :, T:2 * T]]
        bn6 = sb("bn6b", [P, TT, 6])
        mv = sb("mvb", [P, TT, 2])
        var = sb("varb", [P, TT])
        rs = sb("rsb", [P, TT])
        minus_half = sb("minus_halfb", [P, 8])
        lead = sb("leadb", [P, 8])
        asum = sb("asum", [P, TT])
        strength = sb("strength", [P, NB, 2])
        ratio = sb("ratio", [P, NB])
        lg = sb("lg", [P, TT, NE])
        lmax = sb("lmax", [P, TT])
        pe_ = sb("pe_", [P, TT, NE])
        lsum = sb("lsum", [P, TT])
        sel = sb("sel", [P, TT, 2, NE])
        keep = sb("keep", [P, TT])
        v1 = sb("v1", [P, TT])
        v2 = sb("v2", [P, TT])
        coef = sb("coef", [P, TT, NE])
        coef2 = sb("coef2", [P, TT, NE])
        sel_b = sb("sel_b", [P, NB, 2, NE])

        ctx_in = sem("ctx_in"); wkv_in = sem("wkv_in"); const_in = sem("const_in"); wq_in = sem("wq_in")
        wo_in = sem("wo_in"); w1_in = sem("w1_in"); w2_in = sem("w2_in"); small_in = sem("small_in")
        k_out = sem("k_out"); stacked = sem("stacked"); q_out = sem("q_out"); out_done = sem("out_done2")
        k_done = sem("k_done"); v_done = sem("v_done"); xT_ready = sem("xT_ready"); xT_done = sem("xT_done")
        q_ready = sem("q_ready"); q_hi_done = sem("q_hi_done"); q_lo_done = sem("q_lo_done")
        k_ready = sem("k_ready"); v_ready = sem("v_ready"); k_hi_done = sem("k_hi_done")
        ones_set = sem("ones_set"); halves_set = sem("halves_set")
        st_in = [sem(f"st_in{i}") for i in range(RING)]
        row_in = [sem(f"row_in{i}") for i in range(RING)]
        smax_ready = sem("smax_ready"); smax_done = sem("smax_done"); mT_ready = sem("mT_ready")
        m_hi_done = sem("m_hi_done"); m_lo_done = sem("m_lo_done")
        sc_ready = sem("sc_ready"); probs_done = sem("probs_done"); pv_ready = sem("pv_ready")
        pv_done = sem("pv_done"); v_slot = sem("v_slot"); pvT_ready = sem("pvT_ready")
        rden_done = sem("rden_done"); attn_done = sem("attn_done")
        aT_ready = sem("aT_ready"); aT_done = sem("aT_done"); o_ready = sem("o_ready")
        ln_step = sem("ln_step"); pow_done = sem("pow_done"); x2_done = sem("x2_done")
        x2T_ready = sem("x2T_ready"); x2T_done = sem("x2T_done")
        asum_done = sem("asum_done"); str_ready = sem("str_ready"); lg_ready = sem("lg_ready")
        soft_in = sem("soft_in"); soft_out = sem("soft_out"); sel_done = sem("sel_done"); sel_ready = sem("sel_ready")
        chain = sem("chain"); pre_ready = sem("pre_ready"); act_done = sem("act_done")
        moe_ready = sem("moe_ready"); moe_done = sem("moe_done"); ln_done = sem("ln_done")
        block = ctx.enter_context(nc.Block())
        HALF = KVH // 2

        @block.sync
        def _(sp):
            sp.dma_start(ident[:], A["ident"]).then_inc(const_in, 16)
            sp.dma_start(wk[:], A["wk"]).then_inc(wkv_in, 16)
            sp.dma_start(ctxT[:], A["ctxT"]).then_inc(ctx_in, 16)
            sp.dma_start(wv[:], A["wv"]).then_inc(wkv_in, 16)
            sp.dma_start(wq[:], A["wq"]).then_inc(wq_in, 16)
            sp.wait_ge(k_hi_done, NB)
            sp.wait_ge(k_done, NB)
            sp.dma_start(k_hi_d.bitcast(F32), k_hi[:].bitcast(F32)).then_inc(k_out, 16)
            sp.dma_start(k_lo_d.bitcast(F32), k_lo[:].bitcast(F32)).then_inc(k_out, 16)
            sp.wait_ge(q_hi_done, KD)
            sp.wait_ge(q_lo_done, KD)
            sp.dma_start(q_hi_d.rearrange("j p t -> p j t").bitcast(F32), q_hi[:].bitcast(F32)).then_inc(q_out, 16)
            sp.dma_start(q_lo_d.rearrange("j p t -> p j t").bitcast(F32), q_lo[:].bitcast(F32)).then_inc(q_out, 16)
            sp.wait_ge(k_out, 32)
            for j, ks in enumerate((k_hi_d, k_lo_d, k_hi_d)):
                sp.dma_start(k_stack[:, AD * j:AD * (j + 1), :],
                             ks.bitcast(F32).rearrange("(k d) t -> k d t", d=AD)).then_inc(stacked, 16)
            sp.wait_ge(q_out, 32)
            for j, qs in enumerate((q_hi_d, q_hi_d, q_lo_d)):
                rows = qs.bitcast(F32).rearrange("j p t -> (j p) t").rearrange(
                    "(m par d) t -> par m d t", par=2, d=AD)
                for par in range(2):
                    sp.dma_start(q_stack[par, :, AD * j:AD * (j + 1)], rows[par]).then_inc(stacked, 16)
            sp.wait_ge(stacked, 9 * 16)
            sp.wait_ge(ones_set, RING)

            def load_stacks(kv):
                for par in range(2):
                    rows = slice(64 * par, 64 * par + 3 * AD)
                    sp.dma_start(k_st[kv % RING][rows].bitcast(F32), k_stack[kv]).then_inc(st_in[kv % RING], 16)
                    sp.dma_start(q_st[kv % RING][rows].bitcast(F32),
                                 q_stack[par, kv * REP // 2:(kv + 1) * REP // 2].rearrange("m r t -> r m t")
                                 ).then_inc(st_in[kv % RING], 16)

            def load_rows(kv):
                s = kv % RING
                sp.wait_ge(m_lo_done, kv + 1 + 1)
                for h in range(REP):
                    for row, src in ((3 * AD, m_hi), (3 * AD + 1, m_lo)):
                        r = 64 * (h % 2) + row
                        sp.dma_start(q_st[s][r:r + 1, h // 2, :].bitcast(F32),
                                     src[h:h + 1, s, :].bitcast(F32)).then_inc(row_in[s], 16)

            for kv in range(RING):
                load_stacks(kv)
            sp.dma_start(wo[:], A["wo"]).then_inc(wo_in, 16)
            for name, dst in (("vision", vision), ("text", text), ("first", first), ("every", every),
                              ("b1", b1), ("gate_w", gate_w)):
                sp.dma_start(dst[:], A[name]).then_inc(small_in, 16)
            sp.dma_start(gate_r[:], A["gate_r"].partition_broadcast(P)).then_inc(small_in, 16)
            sp.dma_start(gate_b[:], A["gate_b"].partition_broadcast(P)).then_inc(small_in, 16)
            sp.dma_start(b2[:], A["b2"].partition_broadcast(P)).then_inc(small_in, 16)
            sp.dma_start(w1[:], A["w1"]).then_inc(w1_in, 16)
            sp.dma_start(w2[:], A["w2"]).then_inc(w2_in, 16)
            load_rows(0)
            for kv in range(1, KVH):
                load_rows(kv)
                if kv + 2 < KVH:
                    sp.wait_ge(sc_ready, 8 * kv)
                    load_stacks(kv + 2)

            sp.wait_ge(ln_done, TT)
            sp.dma_start(A["out"], x_acc[:]).then_inc(out_done, 16)
            sp.wait_ge(out_done, 16)

        @block.gpsimd
        def _(pool):
            nc.gpsimd.memset(minus_half[:], -0.5).then_inc(halves_set, 1)
            pool.wait_ge(halves_set, 1)
            pool.wait_ge(v_done, 3)

            def fill_v(kv, s):
                nc.gpsimd.tensor_copy(v_kv[s][:], v_tok[:, :, bass.ds(kv, 1), :].rearrange("p c a d -> p c (a d)")
                                      ).then_inc(v_slot, 1)

            for kv in range(RING):
                fill_v(kv, kv)
            for kv in range(RING, KVH):
                pool.wait_ge(pv_ready, kv - RING + 1)
                fill_v(kv, kv % RING)
            for n in range(2):
                pool.wait_ge(ln_step, 9 * n + 9)
                nc.gpsimd.tensor_tensor(rs[:], var[:], minus_half[:, 0:TT], ALU.pow).then_inc(pow_done, 1)

        @block.scalar
        def _(act):
            act.wait_ge(halves_set, 1)
            for b in range(NB):
                act.wait_ge(k_ready, b + 1)
                nc.scalar.copy(k_hi[:, b * CS:(b + 1) * CS], banks[b]).then_inc(k_hi_done, 1)
            for j in range(KD):
                act.wait_ge(q_ready, j + 1)
                nc.scalar.mul(q_hi[:, j, :], banks[j], SCALE).then_inc(q_hi_done, 1)

            def max_row(kv, s):
                act.wait_ge(mT_ready, kv + 1)
                nc.scalar.copy(m_hi[:, s, :], odd_ps[0:REP, :]).then_inc(m_hi_done, 1)

            def exps(kv, n):
                act.wait_ge(sc_ready, 8 * kv + n + 1)
                nc.scalar.activation(probs[:, n % 2, :], sc_ps[n % 2][:].rearrange("p a k -> p (a k)"), ACT.Exp
                                     ).then_inc(probs_done, 1)

            nc.scalar.copy(lead[:, 4:5], minus_half[:, 0:1]).then_inc(probs_done, 2)
            nc.scalar.copy(lead[:, 5:6], minus_half[:, 0:1]).then_inc(pv_done, 1)
            max_row(0, 0)

            def head(kv, s, more=True):
                for n in range(8):
                    exps(kv, n)
                    if n == 4 and more:
                        max_row(kv + 1, (s + 1) % RING)
                act.wait_ge(pv_ready, kv + 1)
                nc.scalar.copy(pv[:], pv_ps[:]).then_inc(pv_done, 1)

            with act.Fori(0, 2) as i:
                for s in range(RING):
                    head(RING * i + s, s)
            head(KVH - 2, 0)
            head(KVH - 1, 1, False)
            act.wait_ge(soft_in, 1)
            nc.scalar.activation(pe_[:], lg[:], ACT.Exp).then_inc(soft_out, 1)
            act.wait_ge(small_in, 9 * 16)
            for e, func in enumerate((ACT.Tanh, ACT.Gelu, ACT.Silu)):
                for f in range(KD):
                    act.wait_ge(pre_ready, KD * e + f + 1)
                    nc.scalar.activation(actT[e % 2][:, f, :], banks[f], func, bias=b1[:, e, f:f + 1]
                                         ).then_inc(act_done, 1)

        @block.vector
        def _(dve):
            for s in range(RING):
                nc.vector.memset(k_st[s][:].bitcast(F32), 1.0).then_inc(ones_set, 1)
            nc.vector.memset(v_tok[:, :, :, AD:2 * AD], 1.0).then_inc(v_done, 1)
            for k, s in enumerate((attn_done, smax_done, m_lo_done)):
                nc.vector.memset(lead[:, k:k + 1], 0.0).then_inc(s, 1)
            for b in range(NB):
                dve.wait_ge(k_hi_done, b + 1)
                cols = slice(b * CS, (b + 1) * CS)
                nc.vector.tensor_tensor(k_lo[:, cols], banks[b], k_hi[:, cols].bitcast(F32), ALU.subtract
                                        ).then_inc(k_done, 1)
            for h in range(2):
                dve.wait_ge(v_ready, h + 1)
                nc.vector.tensor_copy(v_tok[:, 4 * h:4 * h + 4, :, 0:AD],
                                      banks[2 + h].rearrange("p (c k d) -> p c k d", c=4, k=KVH)).then_inc(v_done, 1)
            for k in range(KD):
                dve.wait_ge(xT_ready, k + 1)
                nc.vector.tensor_copy(x1T[:, k, :], banks[4 + k]).then_inc(xT_done, 1)
            for j in range(KD):
                dve.wait_ge(q_hi_done, j + 1)
                nc.vector.scalar_tensor_tensor(q_lo[:, j, :], banks[j], SCALE, q_hi[:, j, :].bitcast(F32),
                                               ALU.mult, ALU.subtract).then_inc(q_lo_done, 1)

            def row_max(kv, s, n):
                dve.wait_ge(smax_ready, 8 * kv + n + 1)
                t, m = n // 2, n % 2
                nc.vector.tensor_reduce(nmax[:, s, t, 2 * m:2 * m + 2], max_ps[:], AX.X, ALU.max, negate=True
                                        ).then_inc(smax_done, 1)

            def max_row(kv, s):
                dve.wait_ge(m_hi_done, kv + 1)
                nc.vector.tensor_tensor(m_lo[:, s, :], odd_ps[0:REP, :], m_hi[:, s, :].bitcast(F32), ALU.subtract
                                        ).then_inc(m_lo_done, 1)

            def normalise(kv):
                dve.wait_ge(pvT_ready, kv + 1)
                out = odd_ps[:].rearrange("p (t h d) -> p t h d", t=TT, h=REP)
                nc.vector.reciprocal(rden[:], out[:, :, :, AD]).then_inc(rden_done, 1)
                dve.wait_ge(rden_done, kv + 1)
                nc.vector.tensor_tensor(
                    attn[:, :, bass.ds(kv * REP * AD, REP * AD)].rearrange("p t (h d) -> p t h d", h=REP),
                    out[:, :, :, 0:AD], rden[:].unsqueeze(3).to_broadcast([P, TT, REP, AD]),
                    ALU.mult).then_inc(attn_done, 1)

            def head(kv, s, rest, ahead):
                if rest:
                    for n in range(5, 8):
                        row_max(kv + 1, (s + 1) % RING, n)
                if ahead:
                    row_max(kv + 2, (s + 2) % RING, 0)
                if rest:
                    max_row(kv + 1, (s + 1) % RING)
                if ahead:
                    for n in range(1, 5):
                        row_max(kv + 2, (s + 2) % RING, n)
                normalise(kv)

            for n in range(8):
                row_max(0, 0, n)
            max_row(0, 0)
            for n in range(5):
                row_max(1, 1, n)
            with dve.Fori(0, 2) as i:
                for s in range(RING):
                    head(RING * i + s, s, True, True)
            head(KVH - 2, 0, True, False)
            head(KVH - 1, 1, False, False)
            for k in range(KD):
                dve.wait_ge(aT_ready, k + 1)
                nc.vector.tensor_copy(attnT[:, k, :], banks[k]).then_inc(aT_done, 1)

            def layernorm(n, done):
                at = 9 * n
                for t in range(TT):
                    nc.vector.bn_stats(bn6[:, t, :], x_acc[:, t, :]).then_inc(ln_step, 1)
                for t in range(TT):
                    dve.wait_ge(ln_step, at + TT)
                    nc.vector.bn_aggr(mv[:, t, :], bn6[:, t, :]).then_inc(ln_step, 1)
                dve.wait_ge(ln_step, at + 2 * TT)
                nc.vector.tensor_scalar(var[:], mv[:, :, 1], EPS, None, ALU.add).then_inc(ln_step, 1)
                dve.wait_ge(pow_done, n + 1)
                for t in range(TT):
                    nc.vector.tensor_scalar(x_acc[:, t, :], x_acc[:, t, :], mv[:, t, 0:1], rs[:, t:t + 1],
                                            ALU.subtract, ALU.mult).then_inc(done, 1)

            c = [0]

            def link(ins):
                c[0] += 1
                ins.then_inc(chain, 1)
                dve.wait_ge(chain, c[0])

            for t in range(TT):
                dve.wait_ge(o_ready, t + 1)
                link(nc.vector.tensor_tensor(x_acc[:, t, :], x_acc[:, t, :], banks[4 + t], ALU.add))
            layernorm(0, x2_done)
            dve.wait_ge(x2_done, TT)
            nc.vector.tensor_reduce(asum[:], x_acc[:], AX.X, ALU.add, apply_absolute_value=True).then_inc(asum_done, 1)
            for k in range(KD):
                dve.wait_ge(x2T_ready, k + 1)
                nc.vector.tensor_copy(x2T[:, k, :], banks[k]).then_inc(x2T_done, 1)

            dve.wait_ge(str_ready, 1)
            dve.wait_ge(small_in, 9 * 16)
            sums = odd_ps[:, 0:2 * NB].rearrange("p (b s) -> p b s", b=NB)
            link(nc.vector.tensor_scalar(strength[:, :, 0], sums[:, :, 0], 1.0 / (VIS * D), 1e-8, ALU.mult, ALU.add))
            link(nc.vector.tensor_scalar(strength[:, :, 1], sums[:, :, 1], 1.0 / ((SEQ - VIS) * D), None, ALU.mult))
            link(nc.vector.reciprocal(ratio[:], strength[:, :, 0]))
            link(nc.vector.tensor_tensor(ratio[:], ratio[:], strength[:, :, 1], ALU.mult))
            dve.wait_ge(lg_ready, 1)
            logits = odd_ps[:, 16:16 + TT * NE].rearrange("p (t e) -> p t e", t=TT)
            link(nc.vector.tensor_tensor(lg[:], logits, gate_b[:].unsqueeze(1).to_broadcast([P, TT, NE]), ALU.add))
            for t in range(TT):
                link(nc.vector.scalar_tensor_tensor(lg[:, t, :], gate_r[:], ratio[:, t // 2:t // 2 + 1], lg[:, t, :],
                                                    ALU.mult, ALU.add))
            link(nc.vector.tensor_reduce(lmax[:], lg[:], AX.X, ALU.max))
            link(nc.vector.tensor_tensor(lg[:], lg[:], lmax[:].unsqueeze(2).to_broadcast([P, TT, NE]), ALU.subtract))
            nc.vector.memset(keep[:], 0.0).then_inc(soft_in, 1)
            dve.wait_ge(soft_out, 1)
            link(nc.vector.tensor_reduce(lsum[:], pe_[:], AX.X, ALU.add))
            link(nc.vector.reciprocal(lsum[:], lsum[:]))
            link(nc.vector.tensor_tensor(pe_[:], pe_[:], lsum[:].unsqueeze(2).to_broadcast([P, TT, NE]), ALU.mult))
            for i, best in enumerate((v1, v2)):
                s = sel[:, :, i, :]
                link(nc.vector.tensor_reduce(best[:], pe_[:], AX.X, ALU.max))
                link(nc.vector.tensor_tensor(s, pe_[:], best[:].unsqueeze(2).to_broadcast([P, TT, NE]), ALU.is_ge))
                link(nc.vector.tensor_scalar(keep[:], s[:, :, 0], -1.0, 1.0, ALU.mult, ALU.add))
                link(nc.vector.tensor_tensor(s[:, :, 1], s[:, :, 1], keep[:], ALU.mult))
                link(nc.vector.tensor_tensor(s[:, :, 2], keep[:], s[:, :, 1], ALU.subtract))
                if i == 0:
                    link(nc.vector.scalar_tensor_tensor(pe_[:], s, -2.0, pe_[:], ALU.mult, ALU.add))
            link(nc.vector.scalar_tensor_tensor(lsum[:], v1[:], 1e-8, v2[:], ALU.add, ALU.add))
            link(nc.vector.reciprocal(lsum[:], lsum[:]))
            link(nc.vector.tensor_tensor(v1[:], v1[:], lsum[:], ALU.mult))
            nc.vector.tensor_tensor(v2[:], v2[:], lsum[:], ALU.mult).then_inc(sel_done, 1)
            dve.wait_ge(sel_done, 1)
            dve.wait_ge(sel_ready, 1)
            link(nc.vector.tensor_copy(sel_b[:].rearrange("p b i e -> p (b i e)"), odd_ps[:, 64:64 + NB * 2 * NE]))
            for t in range(TT):
                link(nc.vector.tensor_scalar(coef[:, t, :], sel_b[:, t // 2, 0, :], v1[:, t:t + 1], None, ALU.mult))
                link(nc.vector.scalar_tensor_tensor(coef[:, t, :], sel_b[:, t // 2, 1, :], v2[:, t:t + 1],
                                                    coef[:, t, :], ALU.mult, ALU.add))
            for e in range(NE):
                for t in range(TT):
                    link(nc.vector.scalar_tensor_tensor(x_acc[:, t, :], b2[:, e, :], coef[:, t, e:e + 1],
                                                        x_acc[:, t, :], ALU.mult, ALU.add))
            for e in range(NE):
                for t in range(TT):
                    dve.wait_ge(moe_ready, TT * e + t + 1)
                    if e:
                        dve.wait_ge(moe_done, TT * (e - 1) + t + 1)
                    nc.vector.scalar_tensor_tensor(x_acc[:, t, :], banks[4 + t], coef[:, t, e:e + 1], x_acc[:, t, :],
                                                   ALU.mult, ALU.add).then_inc(moe_done, 1)
            dve.wait_ge(moe_done, TT * NE)
            layernorm(1, ln_done)

        @block.tensor
        def _(pe):
            pe.wait_ge(wkv_in, 32)
            pe.wait_ge(ctx_in, 16)
            for b in range(NB):
                for k in range(KD):
                    ins = nc.tensor.matmul(banks[b], wk[:, k, :], ctxT[:, k, b * CS:(b + 1) * CS],
                                           start=k == 0, stop=k == KD - 1)
                ins.then_inc(k_ready, 1)
            for h in range(2):
                for c in range(4):
                    for k in range(KD):
                        t = 4 * h + c
                        ins = nc.tensor.matmul(banks[2 + h][:, c * P:(c + 1) * P], ctxT[:, k, t * P:(t + 1) * P],
                                               wv[:, k, :], start=k == 0, stop=k == KD - 1)
                ins.then_inc(v_ready, 1)

            def turn(src, ready, first_bank):
                for k in range(KD):
                    for t in range(TT):
                        ins = nc.tensor.transpose(banks[first_bank + k][:, t * P:(t + 1) * P],
                                                  src[:, t, k * P:(k + 1) * P], ident[:])
                    ins.then_inc(ready, 1)

            pe.wait_ge(const_in, 16)
            turn(x_acc, xT_ready, 4)
            pe.wait_ge(xT_done, KD)
            pe.wait_ge(wq_in, 16)
            pe.wait_ge(k_done, NB)
            for j in range(KD):
                if j == 2:
                    pe.wait_ge(v_done, 3)
                for k in range(KD):
                    ins = nc.tensor.matmul(banks[j], wq[:, k, j * P:(j + 1) * P], x1T[:, k, :],
                                           start=k == 0, stop=k == KD - 1)
                ins.then_inc(q_ready, 1)
            pe.wait_ge(q_lo_done, KD)

            def row_scores(kv, s, n, visit):
                t, m = n // 2, n % 2
                if n == 0:
                    pe.wait_ge(st_in[s], 16 * 4 * visit)
                pe.wait_ge(smax_done, 8 * kv + n + 1)
                for par in range(2):
                    rows = slice(64 * par, 64 * par + 3 * AD)
                    ins = nc.tensor.matmul(max_ps[:, par, :], q_st[s][rows, m, t * P:(t + 1) * P],
                                           k_st[s][rows, (t // 2) * CS:(t // 2 + 1) * CS], start=True, stop=True)
                ins.then_inc(smax_ready, 1)

            def max_rows(kv, s):
                pe.wait_ge(smax_done, 8 * kv + 8 + 1)
                pe.wait_ge(m_lo_done, kv + 1)
                if not (isinstance(kv, int) and kv < 1):
                    pe.wait_ge(attn_done, kv - 1 + 1)
                for t in range(TT):
                    ins = nc.tensor.transpose(odd_ps[0:REP, t * P:(t + 1) * P], nmax[:, s, t, :], ident[:])
                ins.then_inc(mT_ready, 1)

            def scores(kv, s, n, visit):
                b, c = divmod(n, CS // P)
                if n == 0:
                    pe.wait_ge(row_in[s], 16 * 8 * visit)
                pe.wait_ge(probs_done, 8 * kv + n - 1 + 2)
                for m in range(REP // 2):
                    for par in range(2):
                        rows = slice(64 * par, 64 * par + 3 * AD + 2)
                        ins = nc.tensor.matmul(sc_ps[n % 2][:, par, m * SEQ:(m + 1) * SEQ],
                                               k_st[s][rows, b * CS + c * P:b * CS + (c + 1) * P],
                                               q_st[s][rows, m, b * SEQ:(b + 1) * SEQ], start=True, stop=True)
                ins.then_inc(sc_ready, 1)

            def values(kv, s, n):
                b, c = divmod(n, CS // P)
                pe.wait_ge(probs_done, 8 * kv + n + 1 + 2)
                if n == 0:
                    pe.wait_ge(v_slot, kv + 1)
                    pe.wait_ge(pv_done, kv + 1)
                for h in range(REP):
                    at = (2 * (h % 2) + h // 2) * SEQ
                    ins = nc.tensor.matmul(pv_ps[32 * h:32 * h + 2 * AD, b * SEQ:(b + 1) * SEQ],
                                           v_kv[s][:, b * (CS // P) + c, :], probs[:, n % 2, at:at + SEQ],
                                           start=c == 0, stop=c == CS // P - 1)
                if n == 7:
                    ins.then_inc(pv_ready, 1)

            def turn_pv(kv):
                pe.wait_ge(pv_done, kv + 1 + 1)
                pe.wait_ge(m_lo_done, min(kv + 2, KVH) + 1 if isinstance(kv, int) else kv + 3)
                pe.wait_ge(attn_done, kv + 1)
                for t in range(TT):
                    ins = nc.tensor.transpose(odd_ps[:, t * P:(t + 1) * P], pv[:, t * P:(t + 1) * P], ident[:])
                ins.then_inc(pvT_ready, 1)

            for n in range(8):
                row_scores(0, 0, n, 1)
            max_rows(0, 0)
            for n in range(5):
                row_scores(1, 1, n, 1)

            def head(kv, s, visit, rest=True, ahead=True):
                s1, s2 = (s + 1) % RING, (s + 2) % RING
                scores(kv, s, 0, visit)
                for n in range(8):
                    if rest and n == 4:
                        max_rows(kv + 1, s1)
                    if rest and n < 3:
                        row_scores(kv + 1, s1, n + 5, None)
                    if ahead and n >= 3:
                        row_scores(kv + 2, s2, n - 3, visit + (s > 0))
                    if n < 7:
                        scores(kv, s, n + 1, visit)
                    values(kv, s, n)
                turn_pv(kv)

            with pe.Fori(0, 2) as i:
                for s in range(RING):
                    head(RING * i + s, s, i + 1)
            head(KVH - 2, 0, 3, True, False)
            head(KVH - 1, 1, 3, False, False)
            pe.wait_ge(attn_done, KVH + 1)
            turn(attn, aT_ready, 0)
            pe.wait_ge(wo_in, 16)
            pe.wait_ge(aT_done, KD)
            for t in range(TT):
                for k in range(KD):
                    ins = nc.tensor.matmul(banks[4 + t], attnT[:, k, t * P:(t + 1) * P], wo[:, k, :],
                                           start=k == 0, stop=k == KD - 1)
                ins.then_inc(o_ready, 1)
            pe.wait_ge(small_in, 9 * 16)
            pe.wait_ge(chain, TT)
            pe.wait_ge(asum_done, 1)
            for b in range(NB):
                for i, parts in enumerate(((vision,), (text, every))):
                    for j, mask in enumerate(parts):
                        at = 2 * b + i
                        ins = nc.tensor.matmul(odd_ps[:, at:at + 1], mask[:], asum[:, 2 * b + j:2 * b + j + 1],
                                               start=j == 0, stop=j == len(parts) - 1)
            ins.then_inc(str_ready, 1)
            turn(x_acc, x2T_ready, 0)
            pe.wait_ge(x2T_done, KD)
            pe.wait_ge(chain, TT + 4)
            for t in range(TT):
                for k in range(KD):
                    at = 16 + NE * t
                    ins = nc.tensor.matmul(odd_ps[:, at:at + NE], x2T[:, k, t * P:(t + 1) * P], gate_w[:, k, :],
                                           start=k == 0, stop=k == KD - 1)
            ins.then_inc(lg_ready, 1)

            def up(e):
                for f in range(KD):
                    if e:
                        pe.wait_ge(act_done, KD * (e - 1) + f + 1)
                    for k in range(KD):
                        ins = nc.tensor.matmul(banks[f], w1[:, e, k, f * P:(f + 1) * P], x2T[:, k, :],
                                               start=k == 0, stop=k == KD - 1)
                    ins.then_inc(pre_ready, 1)

            def down(e):
                pe.wait_ge(act_done, KD * (e + 1))
                for t in range(TT):
                    if e:
                        pe.wait_ge(moe_done, TT * (e - 1) + t + 1)
                    for f in range(KD):
                        ins = nc.tensor.matmul(banks[4 + t], actT[e % 2][:, f, t * P:(t + 1) * P], w2[:, e, f, :],
                                               start=f == 0, stop=f == KD - 1)
                    ins.then_inc(moe_ready, 1)

            pe.wait_ge(w1_in, 16)
            up(0)
            pe.wait_ge(sel_done, 1)
            for b in range(NB):
                at = 64 + 2 * NE * b
                ins = nc.tensor.matmul(odd_ps[:, at:at + 2 * NE], first[:],
                                       sel[:, 2 * b].rearrange("p i e -> p (i e)"), start=True, stop=True)
            ins.then_inc(sel_ready, 1)
            pe.wait_ge(w2_in, 16)
            pe.wait_ge(chain, SEL_B)
            up(1)
            down(0)
            up(2)
            down(1)
            down(2)


V = {"ms": 2, "xn": 6, "x2": 7, "hT0": 8, "hT1": 9, "hT2": 10, "hT3": 11, "u": 12, "dtT": 26, "acs": 32, "parts": 38,
     "start": 40, "var": 49, "ln": 53}
S = {"eT": 10}
E = {"dt": 5, "dt_tr": 6, "dec_tr": 7}


def kernel(**inputs):
    import numpy as np
    import concourse.bacc as bacc
    from concourse.bass_utils import run_bass_kernel_spmd

    w = {k: np.asarray(v) for k, v in inputs.items()}

    def columns(vec, n):
        return np.ascontiguousarray(vec.reshape(n, P).T)

    def weight_tiles(rows):
        n = rows.shape[0] // P
        return rows.reshape(n, P, KD, P).transpose(0, 3, 2, 1)

    wi = w["L0_attn_in_proj_w"]
    parts = {}
    gate_w, hid_w = weight_tiles(wi[:DIN]), weight_tiles(wi[DIN:2 * DIN])
    b_w = weight_tiles(wi[2 * DIN:2 * DIN + GROUPS * NST])
    c_w = weight_tiles(wi[2 * DIN + GROUPS * NST:2 * DIN + 2 * GROUPS * NST])
    main = np.stack([hid_w, gate_w], axis=2).reshape(GROUPS, U, P, 2, KD, P)
    bc = np.stack([b_w, c_w], axis=2)[:, None]
    pairs = np.concatenate([bc, main], axis=1).reshape(GROUPS * PAIRS, P, 2, KD, P)
    parts["w_main"] = np.concatenate([pairs, np.zeros((PAIRS,) + pairs.shape[1:], np.float32)])
    parts["w_dt"] = weight_tiles(wi[2 * DIN + 2 * GROUPS * NST:])[0]
    parts["w_out"] = w["L0_attn_out_proj_w"].T.reshape(GROUPS * U // 2, 2, P, D).transpose(0, 2, 1, 3)
    parts["x"] = w["x"].reshape(TT, P, D).transpose(1, 0, 2)
    nch = TILES + 2 * GROUPS
    parts["conv_w"] = w["L0_attn_conv_w"].reshape(nch, P, KC).transpose(1, 0, 2)
    parts["conv_b"] = columns(w["L0_attn_conv_b"], nch)
    parts["norm_w"] = columns(w["L0_attn_norm_w"], KD)
    parts["gnorm"] = columns(w["L0_attn_gnorm_w"], TILES)
    parts["d_skip"] = columns(np.repeat(w["L0_attn_Dp"], HD), TILES)
    parts["dt_bias"] = w["L0_attn_dt_bias"].reshape(HEADS, 1)
    parts["a_log"] = w["L0_attn_A_log"].reshape(HEADS, 1)
    parts["ident"] = np.eye(P, dtype=np.float32)
    import ml_dtypes
    parts["ident_b"] = np.eye(P).astype(ml_dtypes.bfloat16)
    parts["above"] = np.ascontiguousarray(np.broadcast_to(
        (np.tril(np.ones((P, P)), -1) * -BIG)[:, None], (P, TT, P))).astype(ml_dtypes.bfloat16)
    parts["causal"] = np.triu(np.ones((P, P), np.float32))

    def rows_k(m):
        return m.reshape(-1, P, m.shape[-1]).transpose(1, 0, 2)

    parts["ctxT"] = rows_k(w["ctx_4096"].reshape(CT, D).T)
    parts["wk"], parts["wv"] = rows_k(w["L0_xattn_Wk"]), rows_k(w["L0_xattn_Wv"])
    parts["wq"], parts["wo"] = rows_k(w["L0_xattn_Wq"]), rows_k(w["L0_xattn_Wo"])
    parts["w1"] = w["L0_ffn_w1"].reshape(NE, KD, P, D).transpose(2, 0, 1, 3)
    parts["w2"] = w["L0_ffn_w2"].reshape(NE, KD, P, D).transpose(2, 0, 1, 3)
    parts["b1"] = w["L0_ffn_b1"].reshape(NE, KD, P).transpose(2, 0, 1)
    parts["b2"] = w["L0_ffn_b2"]
    parts["gate_w"] = rows_k(w["L0_ffn_gate_w"][:D])
    parts["gate_r"] = w["L0_ffn_gate_w"][D]
    parts["gate_b"] = w["L0_ffn_gate_b"]
    token = np.arange(P).reshape(P, 1) * np.ones((1, P))
    parts["vision"] = (token < VIS).astype(np.float32)
    parts["text"] = (token >= VIS).astype(np.float32)
    parts["every"] = np.ones((P, P), np.float32)
    parts["first"] = (token == 0).astype(np.float32)

    nc = bacc.Bacc("TRN2", target_bir_lowering=False, num_devices=1)
    arrays, aps = {}, {}
    for name, a in parts.items():
        arrays["in_" + name] = np.ascontiguousarray(a)
        aps[name] = nc.dram_tensor("in_" + name, a.shape, mybir.dt.from_np(a.dtype), kind="ExternalInput").ap()
    aps["out"] = nc.dram_tensor("out_dram", [P, TT, D], F32, kind="ExternalOutput").ap()
    decoder_program(nc, aps)
    r = run_bass_kernel_spmd(nc, [arrays], core_ids=[0])
    got = np.asarray(r.results[0]["out_dram"]).reshape(P, TT, D)
    return np.ascontiguousarray(got.transpose(1, 0, 2).reshape(NB, SEQ, D))
```

```python
from contextlib import ExitStack

import concourse.bass as bass
from concourse import mybir

ALU = mybir.AluOpType
ACT = mybir.ActivationFunctionType
AX = mybir.AxisListType
F32 = mybir.dt.float32
BF16 = mybir.dt.bfloat16
F32R = mybir.dt.float32r

P = 128
NB, SEQ, D = 2, 256, 512
T = NB * SEQ
TT = T // P
KD = D // P
HEADS, HD, GROUPS, NST = 128, 64, 8, 128
DIN = HEADS * HD
TILES = DIN // P
U = TILES // GROUPS
HG = HEADS // GROUPS
KC = 4
GCH = DIN // GROUPS
EPS = 1e-5
EB = SEQ
CS = 512
CT = NB * CS
AH, KVH, AD = 32, 8, 16
REP = AH // KVH
KVW = KVH * AD
SCALE = AD ** -0.5
NE = 3
VIS = int(SEQ * 0.3)
SEL_B = 35
RING = 3
PAIRS = U + 1
WR = 3
BIG = 1e38


def decoder_program(nc, A):
    with ExitStack() as ctx:
        x_acc = ctx.enter_context(nc.sbuf_tensor("x_acc", [P, TT, D], F32))
        early = EarlyInputs(nc, ctx)
        ssm_block(nc, A, x_acc, early)
        attention_ffn_block(nc, A, x_acc, early)


class EarlyInputs:
    def __init__(self, nc, ctx):
        self.space = ctx.enter_context(nc.sbuf_tensor("early_space", [P, HG * T], F32))
        self.loaded = ctx.enter_context(nc.semaphore("early_loaded"))
        at = 0

        def place(width):
            nonlocal at
            part = self.space[:, at:at + KD * width].rearrange("p (k o) -> p k o", k=KD)
            at += KD * width
            return part

        self.ctxT, self.wk, self.wv, self.wq = place(CT), place(KVW), place(KVW), place(D)


def ssm_block(nc, A, x_acc, early):
    acs_pos = nc.dram_tensor("acs_pos", [3, HEADS, T], BF16).ap()
    acs_neg = nc.dram_tensor("acs_neg", [3, HEADS, T], BF16).ap()
    exp_acs = nc.dram_tensor("exp_acs", [HEADS, NB, P], F32).ap()

    with ExitStack() as ctx:
        def sb(name, shape, dt=F32):
            return ctx.enter_context(nc.sbuf_tensor(name, shape, dt))

        def sem(name):
            return ctx.enter_context(nc.semaphore(name))

        def bank(name):
            return ctx.enter_context(nc.psum_tensor(name, [P, 512], F32))

        proj_ps = [bank("proj_ps0"), bank("proj_ps1")]
        tr_ps = bank("tr_ps")
        dif_ps = [bank("dif_ps0"), bank("dif_ps1")]
        y_ps = bank("y_ps")
        st_ps = bank("st_ps")
        off_ps = bank("off_ps")

        dif_ring = [dif_ps[0], dif_ps[1], y_ps, off_ps]
        out_ps = [dif_ps[0], dif_ps[1], tr_ps, st_ps]

        ident = sb("ident", [P, P])
        causal = sb("causal", [P, P])
        ones = sb("ones", [P, P])
        norm_w = sb("norm_w", [P, KD])
        conv_w = sb("conv_w", [P, TILES + 2 * GROUPS, KC])
        conv_b = sb("conv_b", [P, TILES + 2 * GROUPS])
        d_skip = sb("d_skip", [P, TILES])
        gnorm = sb("gnorm", [P, TILES])
        dt_bias = sb("dt_bias", [P, 1])
        a_log = sb("a_log", [P, 1])
        h_hi = sb("h_hi", [P, KD, T], F32R)
        h_lo = sb("h_lo", [P, KD, T], F32R)
        ident_b = sb("ident_b", [P, P], BF16)
        above = sb("above", [P, TT, P], BF16)
        dt_tok = sb("dt_tok", [P, TT, HEADS])
        dec_tok = sb("dec_tok", [P, NB, HEADS])
        w_raw = sb("w_raw", [P, WR, 2, KD, P])
        w_hi = sb("w_hi", [P, WR, KD, P], F32R)
        w_lo = sb("w_lo", [P, WR, KD, P], F32R)
        wo_raw = sb("wo_raw", [P, 2, 2, D])
        wo_hi = sb("wo_hi", [P, U, D], F32R)
        wo_lo = sb("wo_lo", [P, U, D], F32R)
        dif_l = sb("dif_l", [P, HG // 4, T], BF16)
        dif_r = sb("dif_r", [P, HG // 4, T], BF16)
        e_bc = sb("e_bc", [P, 2, 2, NB, P])
        bT = sb("bT", [P, T])
        cT = sb("cT", [P, T])
        b_tok = sb("b_tok", [P, NB, P])
        cb = sb("cb", [P, T])
        m_mat = early.space[:].rearrange("p (h t) -> p h t", h=HG)
        conv_acc = sb("conv_acc", [P, 2, T])
        hid = sb("hid", [P, 2, T])
        gate = sb("gate", [P, 2, T])
        hc = sb("hc", [P, 2, TT, P])
        hcd = sb("hcd", [P, 2, NB, P])
        state = sb("state", [P, 2, NB, P])
        y_tmp = sb("y_tmp", [P, 2, T])
        off_tmp = sb("off_tmp", [P, 2, NB, P])
        y_hi = sb("y_hi", [P, U, T], F32R)
        y_lo = sb("y_lo", [P, U, T], F32R)
        sq_sum = sb("sq_sum", [P, T])
        mean_sq = sb("mean_sq", [P, TT])
        rstd_g = sb("rstd_g", [P, TT])
        minus_half = sb("minus_half", [P, 8])
        ss = sb("ss", [P, TT])
        rs = sb("rs", [P, TT])
        lead = sb("lead", [P, 8])
        lead_act = sb("lead_act", [P, 2])
        bn6 = sb("bn6", [P, TT, 6])
        mv = sb("mv", [P, TT, 2])
        a_neg = sb("a_neg", [P, 1])
        a_exp = sb("a_exp", [P, 1])

        sq = bT

        x_norm = m_mat[:, 0:4, :]
        dt_u = m_mat[:, 4, :]
        dt_abs = m_mat[:, 5, :]
        dt_e = m_mat[:, 6, :]
        dt_den = m_mat[:, 7, :]
        dt_z = m_mat[:, 8, :]
        dt_z2 = m_mat[:, 9, :]
        dt_s = m_mat[:, 10, :]
        dtT = m_mat[:, 11, :]
        acs = m_mat[:, 12, :]
        rest = m_mat[:, 13, :]
        decT = m_mat[:, 14, 0:NB * P]
        eT = m_mat[:, 14, NB * P:2 * NB * P]
        aT = m_mat[:, 15, :]
        rest2 = y_tmp[:, 1, :]
        sq_junk = y_tmp[:, 0, :]
        w_dt = gate[:, 0, :].rearrange("p (k o) -> p k o", k=KD)
        hT = [conv_acc[:, 0, :], conv_acc[:, 1, :], hid[:, 0, :], hid[:, 1, :]]
        x_tok = wo_raw[:].rearrange("p a b d -> p (a b) d")
        all_parts = m_mat[:, 0:3, :].rearrange("p k t -> p (k t)").bitcast(BF16).rearrange(
            "p (k t) -> p k t", k=6)
        parts, nparts = all_parts[:, 0:3, :], all_parts[:, 3:6, :]

        h_split = sem("h_split"); h_low = sem("h_low"); s_const = sem("s_const"); s_chan = sem("s_chan"); s_x = sem("s_x"); s_wdt = sem("s_wdt")
        w_loaded = [sem(f"w_loaded{i}") for i in range(WR)]
        w_hi_done = sem("w_hi_done"); w_lo_done = sem("w_lo_done")
        dif_loaded = sem("dif_loaded")
        e_loaded = [sem(f"e_loaded{i}") for i in range(2)]; wo_loaded = [sem(f"wo_loaded{i}") for i in range(2)]
        scratch_out = sem("scratch_out");
        act_step = sem("act_step"); vec_step = sem("vec_step"); pool_step = sem("pool_step")
        pe_step = sem("pe_step")
        proj_ready = sem("proj_ready"); dif_ready = sem("dif_ready"); exp_done = sem("exp_done")
        tap_done = sem("tap_done"); conv_step = sem("conv_step"); conv_done = sem("conv_done")
        hid_ready = sem("hid_ready"); gate_done = sem("gate_done")
        tr_ready = sem("tr_ready"); hc_done = sem("hc_done"); hcd_done = sem("hcd_done")
        cb_ready = sem("cb_ready"); cb_done = sem("cb_done"); m_done = sem("m_done")
        st_ready = sem("st_ready"); st_copied = sem("st_copied")
        yd_ready = sem("yd_ready"); off_ready = sem("off_ready"); comb_done = sem("comb_done"); within_done = sem("within_done")
        y_added = sem("y_added"); y_hi_done = sem("y_hi_done"); y_lo_done = sem("y_lo_done"); gated = sem("gated"); sq_done = sem("sq_done")
        squared = sem("squared"); wo_hi_done = sem("wo_hi_done"); wo_lo_done = sem("wo_lo_done"); ss_ready = sem("ss_ready"); ms_done = sem("ms_done")
        rstd_ready = sem("rstd_ready"); out_ready = sem("out_ready"); out_added = sem("out_added")
        block = ctx.enter_context(nc.Block())

        HV = 2 * PAIRS
        def hid_half(u):
            return 2 + 2 * u
        def gate_half(u):
            return 3 + 2 * u

        @block.sync
        def _(sp):
            sp.dma_start(x_tok[:], A["x"]).then_inc(s_x, 16)
            for dst, src in ((ident, "ident"), (causal, "causal"), (norm_w, "norm_w"), (dt_bias, "dt_bias"),
                             (a_log, "a_log")):
                sp.dma_start(dst[:], A[src]).then_inc(s_const, 16)
            sp.dma_start(w_dt, A["w_dt"]).then_inc(s_wdt, 16)

            def load_w(g, j):
                sp.dma_start(w_raw[:, j % WR], A["w_main"][bass.ds(g * PAIRS + j, 1)].rearrange(
                    "a p j k o -> (a p) j k o")).then_inc(w_loaded[j % WR], 16)

            def load_dif(g):
                for r in range(4):
                    for dst, src, row in ((dif_l, acs_neg, 3), (dif_r, acs_pos, 0)):
                        sp.dma_start(dst[32 * r + row:32 * r + row + 3],
                                     src[:, bass.ds(g * HG + r, HG // 4, 4), :]).then_inc(dif_loaded, 16)

            def load_e(g, q):
                for half in range(2):
                    src = exp_acs[bass.ds(g * HG + 4 * q + half, 2, 2)]
                    sp.dma_start(e_bc[half * HD:(half + 1) * HD, q % 2],
                                 src.unsqueeze(0).to_broadcast([HD, 2, NB, P])).then_inc(e_loaded[q % 2], 16)

            def load_wo(g, q):
                sp.dma_start(wo_raw[:, q % 2], A["w_out"][bass.ds(g * (U // 2) + q, 1)].rearrange(
                    "a p u o -> (a p) u o")).then_inc(wo_loaded[q % 2], 16)

            for j in range(WR):
                load_w(0, j)
            for dst, src in ((ident_b, "ident_b"), (above, "above"), (conv_w, "conv_w"), (conv_b, "conv_b"), (d_skip, "d_skip"), 
                             (gnorm, "gnorm")):
                sp.dma_start(dst[:], A[src]).then_inc(s_chan, 16)
            sp.wait_ge(vec_step, V["x2"])
            load_wo(0, 0)
            load_wo(0, 1)
            sp.wait_ge(vec_step, V["parts"])
            sp.dma_start(acs_pos.rearrange("k h t -> h k t"), parts[:]).then_inc(scratch_out, 16)
            sp.dma_start(acs_neg.rearrange("k h t -> h k t"), nparts[:]).then_inc(scratch_out, 16)
            sp.wait_ge(act_step, S["eT"])
            sp.dma_start(exp_acs.rearrange("h b t -> h (b t)"), eT).then_inc(scratch_out, 16)
            sp.wait_ge(scratch_out, 48)
            sp.wait_ge(pool_step, 3)
            load_dif(0)
            load_e(0, 0)
            load_e(0, 1)

            def refill_w(g, j, ahead=0):
                sp.wait_ge(w_lo_done, HV * (g + ahead) + 2 * (j - WR) + 2)
                load_w(g + ahead, j)

            def refill_wo(g, q, ahead=0):
                sp.wait_ge(wo_lo_done, U * (g + ahead) + 2 * (q - 2) + 2)
                load_wo(g + ahead, q)

            def refill_e(g, q, ahead=0):
                sp.wait_ge(comb_done, U * (g + ahead) + 2 * (q - 2) + 2 + 1)
                load_e(g + ahead, q)

            def group(g, last):
                refill_w(g, 3)
                if not last:
                    sp.wait_ge(dif_ready, HG * g + HG)
                    load_dif(g + 1)
                for j in (4, 5, 6):
                    refill_w(g, j)
                refill_wo(g, 2)
                refill_w(g, 7)
                refill_wo(g, 3)
                refill_w(g, 8)
                refill_e(g, 2)
                refill_w(g, 0, 1)
                refill_e(g, 3)
                if not last:
                    refill_wo(g, 0, 1)
                refill_w(g, 1, 1)
                refill_w(g, 2, 1)
                if not last:
                    refill_wo(g, 1, 1)
                    refill_e(g, 0, 1)
                    refill_e(g, 1, 1)

            with sp.Fori(0, GROUPS - 1) as g:
                group(g, False)
            group(GROUPS - 1, True)
            sp.wait_ge(yd_ready, U * GROUPS)
            for name, dst in (("wk", early.wk), ("ctxT", early.ctxT), ("wv", early.wv), ("wq", early.wq)):
                sp.dma_start(dst, A[name]).then_inc(early.loaded, 16)
            sp.wait_ge(vec_step, V["ln"])

        @block.gpsimd
        def _(pool):
            nc.gpsimd.memset(dif_l[:], 1.0).then_inc(pool_step, 1)
            nc.gpsimd.memset(dif_r[:], 1.0).then_inc(pool_step, 1)
            nc.gpsimd.memset(minus_half[:], -0.5).then_inc(pool_step, 1)
            pool.wait_ge(pool_step, 3)
            pool.wait_ge(vec_step, V["ms"])
            nc.gpsimd.tensor_tensor(rs[:], ss[:], minus_half[:, 0:TT], ALU.pow).then_inc(pool_step, 1)
            with pool.Fori(0, GROUPS) as g:
                def decay(u):
                    pool.wait_ge(hc_done, (U + 1) * g + 2 + u)
                    for hh in range(2):
                        ins = nc.gpsimd.tensor_tensor(
                            hcd[:, u % 2, :, hh * HD:(hh + 1) * HD], hc[:, u % 2, 0:TT:2, hh * HD:(hh + 1) * HD],
                            dec_tok[:, :, bass.ds(g * HG + 2 * u + hh, 1)].to_broadcast([P, NB, HD]), ALU.mult)
                    ins.then_inc(hcd_done, 1)

                def gated_y(u):
                    pool.wait_ge(comb_done, U * g + u + 1 + 1)
                    late = y_tmp[:, u % 2, :].rearrange("p (b c t) -> p b c t", b=NB, c=2)[:, :, 1, :]
                    nc.gpsimd.tensor_tensor(late, late, off_tmp[:, u % 2], ALU.add).then_inc(y_added, 1)
                    pool.wait_ge(gate_done, U * g + u + 1 + 1)
                    pool.wait_ge(y_added, U * g + u + 1)
                    nc.gpsimd.tensor_tensor(y_tmp[:, u % 2, :], y_tmp[:, u % 2, :], gate[:, u % 2, :],
                                            ALU.mult).then_inc(gated, 1)

                def low_y(u):
                    pool.wait_ge(y_hi_done, U * g + u + 1)
                    nc.gpsimd.tensor_tensor(y_lo[:, u, :], y_tmp[:, u % 2, :], y_hi[:, u, :].bitcast(F32),
                                            ALU.subtract).then_inc(y_lo_done, 1)
                    pool.wait_ge(squared, U * g + u + 1)
                    if u:
                        pool.wait_ge(sq_done, U * g + u + 1)
                        nc.gpsimd.tensor_tensor(sq_sum[:], sq_sum[:], sq[:], ALU.add).then_inc(sq_done, 1)
                    else:
                        nc.gpsimd.tensor_tensor(sq_sum[:].rearrange("p (c t) -> p c t", c=TT),
                                                sq[:].rearrange("p (c t) -> p c t", c=TT),
                                                ones[:].unsqueeze(1).to_broadcast([P, TT, P]), ALU.mult
                                                ).then_inc(sq_done, 1)

                decay(0)
                for u in range(2, U):
                    decay(u - 1)
                    gated_y(u - 2)
                    low_y(u - 2)
                decay(U - 1)
                gated_y(U - 2)
                low_y(U - 2)
                gated_y(U - 1)
                low_y(U - 1)
                pool.wait_ge(ms_done, g + 1 + 1)
                nc.gpsimd.tensor_tensor(rstd_g[:], mean_sq[:], minus_half[:, 0:TT], ALU.pow).then_inc(rstd_ready, 1)
            pool.wait_ge(vec_step, V["var"])
            nc.gpsimd.tensor_tensor(rs[:], ss[:], minus_half[:, 0:TT], ALU.pow).then_inc(pool_step, 1)

        @block.scalar
        def _(act):
            act.wait_ge(s_x, 16)
            for t in range(TT):
                nc.scalar.activation(sq_junk, x_tok[:, t, :], ACT.Square, accum_out=ss[:, t:t + 1]).then_inc(act_step, 1)
                if t < TT - 1:
                    act.wait_ge(act_step, t + 1)
            act.wait_ge(s_const, 5 * 16)
            nc.scalar.activation(a_exp[:], a_log[:], ACT.Exp).then_inc(act_step, 1)
            act.wait_ge(pe_step, E["dt"])
            act.wait_ge(vec_step, V["u"])
            nc.scalar.activation(dt_abs, dt_u, ACT.Abs).then_inc(act_step, 1)
            act.wait_ge(act_step, 6)
            nc.scalar.activation(dt_e, dt_abs, ACT.Exp, scale=-1.0).then_inc(act_step, 1)
            act.wait_ge(vec_step, V["acs"])
            for b in range(NB):
                last = acs[:, b * EB + P - 1:b * EB + P]
                nc.scalar.activation(decT[:, b * P:(b + 1) * P], acs[:, b * EB:b * EB + P], ACT.Exp, bias=last,
                                     scale=-1.0).then_inc(act_step, 1)
            nc.scalar.activation(eT.rearrange("p (b t) -> p b t", b=NB),
                                 acs.rearrange("p (b t) -> p b t", b=NB)[:, :, P:2 * P], ACT.Exp).then_inc(act_step, 1)
            act.wait_ge(s_chan, 6 * 16)
            for k, s in enumerate((hid_ready, gate_done)):
                nc.scalar.copy(lead_act[:, k:k + 1], ones[:, 0:1]).then_inc(s, 1)
            for k in range(KD):
                act.wait_ge(vec_step, V["hT%d" % k])
                nc.scalar.copy(h_hi[:, k, :], hT[k]).then_inc(h_split, 1)

            def split_hi(g, n, ahead=0):
                j = n // 2
                act.wait_ge(w_loaded[j % WR], 16 * (PAIRS // WR * (g + ahead) + j // WR + 1))
                act.wait_ge(proj_ready, HV * (g + ahead) + n + 1)
                nc.scalar.copy(w_hi[:, n % WR].rearrange("p k o -> p (k o)"),
                               w_raw[:, j % WR, n % 2].rearrange("p k o -> p (k o)")).then_inc(w_hi_done, 1)

            act.wait_ge(vec_step, V["start"])
            for n in range(WR):
                split_hi(0, n)
            with act.Fori(0, GROUPS) as g:
                def tap(n, col, ps):
                    act.wait_ge(proj_ready, HV * g + (hid_half(n - 2) if n >= 2 else n) + 1 + WR)
                    act.wait_ge(hid_ready, (U + 2) * g + max(n - 1, 0) + 1)
                    nc.scalar.activation(conv_acc[:, n % 2, :], ps[:], ACT.Identity, bias=conv_b[:, col],
                                         scale=conv_w[:, col, KC - 1]).then_inc(tap_done, 1)

                def exps(h0, h1):
                    for h in range(h0, h1):
                        act.wait_ge(dif_ready, HG * g + h + 1)
                        nc.scalar.activation(m_mat[:, h, :], dif_ring[h % 4][:], ACT.Exp).then_inc(exp_done, 1)

                def silu(n, dst):
                    act.wait_ge(conv_done, (U + 2) * g + n + 1 + 1)
                    nc.scalar.activation(dst, conv_acc[:, n % 2, :], ACT.Silu).then_inc(hid_ready, 1)

                def hid_tile(u):
                    act.wait_ge(comb_done, U * g + max(u - 1, 0) + 1)
                    silu(2 + u, hid[:, u % 2, :])

                def silu_gate(u):
                    act.wait_ge(proj_ready, HV * g + gate_half(u) + 1 + WR)
                    if u >= 2:
                        act.wait_ge(gated, U * g + u - 1)
                    else:
                        act.wait_ge(y_lo_done, U * g + 1)
                    nc.scalar.activation(gate[:, u % 2, :], proj_ps[1][:], ACT.Silu).then_inc(gate_done, 1)

                def state_copy(u):
                    act.wait_ge(st_ready, U * g + u + 1)
                    nc.scalar.copy(state[:, u % 2], st_ps[:, 0:NB * P].rearrange("p (b t) -> p b t", b=NB)
                                   ).then_inc(st_copied, 1)

                def scale_wo(u):
                    if u % 2 == 0:
                        act.wait_ge(wo_loaded[u // 2 % 2], 16 * (2 * g + u // 4 + 1))
                    nc.scalar.activation(wo_hi[:, u, :], wo_raw[:, u // 2 % 2, u % 2, :], ACT.Copy,
                                         scale=gnorm[:, bass.ds(g * U + u, 1)]).then_inc(wo_hi_done, 1)

                def high_y(u):
                    act.wait_ge(gated, U * g + u + 1)
                    nc.scalar.copy(y_hi[:, u, :], y_tmp[:, u % 2, :]).then_inc(y_hi_done, 1)
                    act.wait_ge(sq_done, U * g + u + 1)
                    nc.scalar.activation(sq[:], y_tmp[:, u % 2, :], ACT.Square).then_inc(squared, 1)

                exps(0, 6)
                tap(0, bass.ds(TILES + g, 1), proj_ps[0])
                split_hi(g, gate_half(0))
                exps(6, 12)
                tap(1, bass.ds(TILES + GROUPS + g, 1), proj_ps[1])
                split_hi(g, hid_half(1))
                exps(12, 16)
                act.wait_ge(sq_done, U * g + 1)
                silu(0, bT[:])
                silu(1, cT[:])
                tap(2, bass.ds(g * U, 1), proj_ps[0])
                split_hi(g, gate_half(1))
                hid_tile(0)
                silu_gate(0)
                scale_wo(0)
                for u in range(1, U):
                    if u >= 2:
                        state_copy(u - 2)
                    if u < U - 1:
                        split_hi(g, hid_half(u + 1))
                    else:
                        split_hi(g, 0, 1)
                    tap(2 + u, bass.ds(g * U + u, 1), proj_ps[0])
                    if u < U - 1:
                        split_hi(g, gate_half(u + 1))
                    else:
                        split_hi(g, 1, 1)
                    hid_tile(u)
                    if u >= 2:
                        high_y(u - 2)
                    silu_gate(u)
                    scale_wo(u)
                state_copy(U - 2)
                split_hi(g, 2, 1)
                high_y(U - 2)
                state_copy(U - 1)
                high_y(U - 1)

        @block.vector
        def _(dve):
            n = [0]

            def step(ins, name=None, wait=True):
                n[0] += 1
                ins.then_inc(vec_step, 1)
                if name:
                    assert V[name] == n[0], (name, n[0])
                if wait:
                    dve.wait_ge(vec_step, n[0])

            step(nc.vector.memset(ones[:], 1.0))
            dve.wait_ge(act_step, 4)
            step(nc.vector.tensor_scalar(ss[:], ss[:], 1.0 / D, EPS, ALU.mult, ALU.add), "ms")
            dve.wait_ge(pool_step, 4)
            for t in range(TT):
                step(nc.vector.tensor_scalar(x_norm[:, t, :], x_tok[:, t, :], rs[:, t:t + 1], None, ALU.mult),
                     "xn" if t == TT - 1 else None, wait=t == TT - 1)
            step(nc.vector.tensor_scalar(x_acc[:], x_tok[:], 2.0, None, ALU.mult), "x2")
            dve.wait_ge(s_const, 5 * 16)
            for k in range(KD):
                dve.wait_ge(pe_step, k + 1)
                step(nc.vector.tensor_scalar(hT[k], proj_ps[k % 2][:], norm_w[:, k:k + 1], None, ALU.mult),
                     "hT%d" % k)
            dve.wait_ge(pe_step, E["dt"])
            step(nc.vector.tensor_scalar(dt_u, proj_ps[0][:], dt_bias[:], None, ALU.add), "u")
            dve.wait_ge(act_step, 7)
            step(nc.vector.tensor_scalar(dt_den, dt_e, 2.0, None, ALU.add))
            step(nc.vector.reciprocal(dt_den, dt_den))
            step(nc.vector.tensor_tensor(dt_z, dt_e, dt_den, ALU.mult))
            step(nc.vector.tensor_tensor(dt_z2, dt_z, dt_z, ALU.mult))
            step(nc.vector.tensor_scalar(dt_s, dt_z2, 2.0 / 17, None, ALU.mult))
            for k in range(15, 1, -2):
                step(nc.vector.scalar_tensor_tensor(dt_s, dt_s, 2.0 / k, dt_z2, ALU.add, ALU.mult))
            step(nc.vector.scalar_tensor_tensor(dt_s, dt_s, 2.0, dt_z, ALU.add, ALU.mult))
            step(nc.vector.scalar_tensor_tensor(dtT, dt_u, 0.0, dt_s, ALU.max, ALU.add), "dtT")
            dve.wait_ge(act_step, 5)
            step(nc.vector.tensor_scalar(a_neg[:], a_exp[:], -1.0, None, ALU.mult))
            step(nc.vector.tensor_scalar(aT, dtT, a_neg[:], None, ALU.mult))
            for c in range(TT):
                step(nc.vector.tensor_tensor_scan(acs[:, c * P:(c + 1) * P], ones[:], aT[:, c * P:(c + 1) * P],
                                                  0.0, ALU.mult, ALU.add), "acs" if c == TT - 1 else None)
            step(nc.vector.tensor_copy(parts[:, 0, :], acs))
            step(nc.vector.tensor_tensor(rest, acs, parts[:, 0, :], ALU.subtract))
            step(nc.vector.tensor_copy(parts[:, 1, :], rest))
            step(nc.vector.tensor_tensor(rest2, rest, parts[:, 1, :], ALU.subtract))
            step(nc.vector.tensor_copy(parts[:, 2, :], rest2))
            step(nc.vector.tensor_scalar(nparts[:], parts[:], -1.0, None, ALU.mult), "parts")
            dve.wait_ge(pe_step, E["dt_tr"])
            step(nc.vector.tensor_copy(dt_tok[:], tr_ps[:].rearrange("p (c h) -> p c h", c=TT)))
            dve.wait_ge(pe_step, E["dec_tr"])
            step(nc.vector.tensor_copy(dec_tok[:], st_ps[:, 0:NB * P].rearrange("p (b h) -> p b h", b=NB)), "start")
            nc.vector.memset(rstd_g[:], 0.0).then_inc(out_added, TT)
            for k, s in enumerate((conv_done, comb_done, ms_done, y_lo_done)):
                nc.vector.memset(lead[:, k:k + 1], 0.0).then_inc(s, 1)
            nc.vector.memset(lead[:, 6:7], 0.0).then_inc(proj_ready, WR)
            nc.vector.memset(lead[:, 7:8], 0.0).then_inc(sq_done, 1)
            for k in range(KD):
                dve.wait_ge(h_split, k + 1)
                nc.vector.tensor_tensor(h_lo[:, k, :], hT[k], h_hi[:, k, :].bitcast(F32), ALU.subtract
                                        ).then_inc(h_low, 1)

            def split_lo(g, n, ahead=0):
                dve.wait_ge(w_hi_done, HV * (g + ahead) + n + 1)
                nc.vector.tensor_tensor(w_lo[:, n % WR].rearrange("p k o -> p (k o)"),
                                        w_raw[:, n // 2 % WR, n % 2].rearrange("p k o -> p (k o)"),
                                        w_hi[:, n % WR].rearrange("p k o -> p (k o)").bitcast(F32), ALU.subtract
                                        ).then_inc(w_lo_done, 1)

            for first in range(WR):
                split_lo(0, first)
            dve.wait_ge(s_chan, 6 * 16)

            with dve.Fori(0, GROUPS) as g:
                def conv(n, col, ps, between=()):
                    dve.wait_ge(tap_done, (U + 2) * g + n + 1)
                    acc = conv_acc[:, n % 2, :].rearrange("p (b t) -> p b t", b=NB)
                    src = ps[:].rearrange("p (b t) -> p b t", b=NB)
                    for k in range(1, KC):
                        ins = nc.vector.scalar_tensor_tensor(
                            acc[:, :, k:], src[:, :, :SEQ - k], conv_w[:, col, KC - 1 - k], acc[:, :, k:],
                            ALU.mult, ALU.add)
                        if k < KC - 1:
                            ins.then_inc(conv_step, 1)
                            if between:
                                between[k - 1]()
                            dve.wait_ge(conv_step, (KC - 2) * ((U + 2) * g + n) + k)
                        else:
                            ins.then_inc(conv_done, 1)

                def to_tokens(u):
                    dve.wait_ge(tr_ready, (U + 1) * g + 2 + u)
                    nc.vector.tensor_tensor(
                        hc[:, u % 2].rearrange("p c (h d) -> p c h d", h=2),
                        tr_ps[:].rearrange("p (c h d) -> p c h d", c=TT, h=2),
                        dt_tok[:, :, bass.ds(g * HG + 2 * u, 2)].unsqueeze(3).to_broadcast([P, TT, 2, HD]),
                        ALU.mult).then_inc(hc_done, 1)

                def mix_head(h):
                    dve.wait_ge(exp_done, HG * g + h + 1)
                    nc.vector.tensor_tensor(m_mat[:, h, :], m_mat[:, h, :], cb[:], ALU.mult).then_inc(m_done, 1)

                def within(u):
                    dve.wait_ge(yd_ready, U * g + u + 1)
                    dve.wait_ge(y_lo_done, U * g + max(u - 1, 0) + 1)
                    dve.wait_ge(sq_done, U * g + max(u - 1, 0) + 1)
                    nc.vector.scalar_tensor_tensor(y_tmp[:, u % 2, :], hid[:, u % 2, :],
                                                   d_skip[:, bass.ds(g * U + u, 1)], y_ps[:], ALU.mult, ALU.add
                                                   ).then_inc(within_done, 1)

                def carried(u):
                    dve.wait_ge(e_loaded[u // 2 % 2], 32 * (2 * g + u // 4 + 1))
                    dve.wait_ge(off_ready, U * g + u + 1)
                    dve.wait_ge(within_done, U * g + u + 1)
                    nc.vector.tensor_tensor(off_tmp[:, u % 2], off_ps[:, 0:NB * P].rearrange("p (b t) -> p b t", b=NB),
                                            e_bc[:, u // 2 % 2, u % 2], ALU.mult).then_inc(comb_done, 1)

                def low_wo(u):
                    dve.wait_ge(wo_hi_done, U * g + u + 1)
                    nc.vector.scalar_tensor_tensor(wo_lo[:, u, :], wo_raw[:, u // 2 % 2, u % 2, :],
                                                   gnorm[:, bass.ds(g * U + u, 1)], wo_hi[:, u, :].bitcast(F32),
                                                   ALU.mult, ALU.subtract).then_inc(wo_lo_done, 1)

                conv(0, bass.ds(TILES + g, 1), proj_ps[0])
                split_lo(g, gate_half(0))
                conv(1, bass.ds(TILES + GROUPS + g, 1), proj_ps[1])
                split_lo(g, hid_half(1))
                conv(2, bass.ds(g * U, 1), proj_ps[0])
                dve.wait_ge(tr_ready, (U + 1) * g + 1)
                nc.vector.tensor_copy(b_tok[:], tr_ps[:, 0:NB * P].rearrange("p (b t) -> p b t", b=NB)
                                      ).then_inc(hc_done, 1)
                dve.wait_ge(cb_ready, g + 1)
                nc.vector.tensor_tensor(cb[:].rearrange("p (c t) -> p c t", c=TT),
                                        y_ps[:].rearrange("p (c t) -> p c t", c=TT),
                                        causal[:].unsqueeze(1).to_broadcast([P, TT, P]), ALU.mult
                                        ).then_inc(cb_done, 1)
                dve.wait_ge(cb_done, g + 1)
                split_lo(g, gate_half(1))
                mix_head(0)
                mix_head(1)
                low_wo(0)
                for u in range(1, U):
                    to_tokens(u - 1)
                    if u < U - 1:
                        split_lo(g, hid_half(u + 1))
                    else:
                        split_lo(g, 0, 1)
                    conv(2 + u, bass.ds(g * U + u, 1), proj_ps[0],
                         (lambda: carried(u - 2) if u >= 2 else None, lambda: mix_head(2 * u)))
                    mix_head(2 * u + 1)
                    if u < U - 1:
                        split_lo(g, gate_half(u + 1))
                    else:
                        split_lo(g, 1, 1)
                    within(u - 1)
                    low_wo(u)
                to_tokens(U - 1)
                carried(U - 2)
                split_lo(g, 2, 1)
                within(U - 1)
                carried(U - 1)
                dve.wait_ge(ss_ready, g + 1)
                nc.vector.tensor_scalar(mean_sq[:], off_ps[:, 0:TT], 1.0 / GCH, EPS, ALU.mult, ALU.add
                                        ).then_inc(ms_done, 1)
                dve.wait_ge(rstd_ready, g + 1)
                for t in range(TT):
                    dve.wait_ge(out_ready, TT * g + t + 1)
                    dve.wait_ge(out_added, TT * g + t + 1)
                    nc.vector.scalar_tensor_tensor(x_acc[:, t, :], out_ps[t][:], rstd_g[:, t:t + 1], x_acc[:, t, :],
                                                   ALU.mult, ALU.add).then_inc(out_added, 1)
            dve.wait_ge(out_added, TT * (GROUPS + 1))
            for t in range(TT):
                step(nc.vector.bn_stats(bn6[:, t, :], x_acc[:, t, :]), wait=t == TT - 1)
            for t in range(TT):
                step(nc.vector.bn_aggr(mv[:, t, :], bn6[:, t, :]), wait=t == TT - 1)
            step(nc.vector.tensor_scalar(ss[:], mv[:, :, 1], EPS, None, ALU.add), "var")
            dve.wait_ge(pool_step, 5)
            for t in range(TT):
                step(nc.vector.tensor_scalar(x_acc[:, t, :], x_acc[:, t, :], mv[:, t, 0:1], rs[:, t:t + 1],
                                             ALU.subtract, ALU.mult), "ln" if t == TT - 1 else None, wait=False)

        @block.tensor
        def _(pe):
            pe.wait_ge(vec_step, V["xn"])
            pe.wait_ge(s_const, 5 * 16)
            for k in range(KD):
                if k >= 2:
                    pe.wait_ge(vec_step, V["hT%d" % (k - 2)])
                for t in range(TT):
                    ins = nc.tensor.transpose(proj_ps[k % 2][:, t * P:(t + 1) * P],
                                              x_norm[:, t, k * P:(k + 1) * P], ident[:])
                ins.then_inc(pe_step, 1)
            pe.wait_ge(vec_step, V["hT%d" % (KD - 1)])
            pe.wait_ge(s_wdt, 16)
            for k in range(KD):
                ins = nc.tensor.matmul(proj_ps[0][:], w_dt[:, k, :], hT[k], start=k == 0, stop=k == KD - 1)
            ins.then_inc(pe_step, 1)
            pe.wait_ge(vec_step, V["dtT"])
            for c in range(TT):
                ins = nc.tensor.transpose(tr_ps[:, c * P:(c + 1) * P], dtT[:, c * P:(c + 1) * P], ident[:])
            ins.then_inc(pe_step, 1)
            pe.wait_ge(act_step, 9)
            for b in range(NB):
                ins = nc.tensor.transpose(st_ps[:, b * P:(b + 1) * P], decT[:, b * P:(b + 1) * P], ident[:])
            ins.then_inc(pe_step, 1)
            pe.wait_ge(vec_step, V["start"])
            pe.wait_ge(h_low, KD)
            pe.wait_ge(s_chan, 6 * 16)
            with pe.Fori(0, GROUPS) as g:
                def project(n, ks=range(KD)):
                    ps = proj_ps[n % 2]
                    if 0 in ks:
                        pe.wait_ge(w_lo_done, HV * g + n + 1)
                        if n == 0:
                            pe.wait_ge(conv_done, (U + 2) * g + 1)
                        elif n == 1:
                            pe.wait_ge(gate_done, U * g + 1)
                        elif n == 3:
                            pe.wait_ge(conv_done, (U + 2) * g + 2 + 1)
                        elif n % 2:
                            pe.wait_ge(gate_done, U * g + (n - 3) // 2 + 1)
                        else:
                            u = (n - 2) // 2
                            pe.wait_ge(conv_done, (U + 2) * g + (u + 2 if u else 1) + 1)
                    for k in ks:
                        for i, (w, h) in enumerate(((w_hi, h_hi), (w_hi, h_lo), (w_lo, h_hi))):
                            ins = nc.tensor.matmul(ps[:], w[:, n % WR, k, :], h[:, k, :], start=k == 0 and i == 0,
                                                   stop=k == KD - 1 and i == 2)
                    if KD - 1 in ks:
                        ins.then_inc(proj_ready, 1)

                def difs(h0, h1):
                    for h in range(h0, h1):
                        if h >= 4:
                            pe.wait_ge(exp_done, HG * g + h - 3)
                        r, j = 32 * (h % 4), h // 4
                        nc.tensor.matmul(dif_ring[h % 4][:], ident_b[:], above[:].rearrange("p c t -> p (c t)"),
                                         start=True, stop=False)
                        for c in range(TT):
                            cols = slice(c * P, (c + 1) * P)
                            ins = nc.tensor.matmul(dif_ring[h % 4][:, cols], dif_l[r:r + 6, j, cols],
                                                   dif_r[r:r + 6, j, cols], start=False, stop=c == TT - 1)
                        ins.then_inc(dif_ready, 1)

                def transposes(u):
                    pe.wait_ge(hid_ready, (U + 2) * g + 3 + u + 1)
                    pe.wait_ge(hc_done, (U + 1) * g + 1 + u)
                    for c in range(TT):
                        cols = slice(c * P, (c + 1) * P)
                        ins = nc.tensor.transpose(tr_ps[:, cols], hid[:, u % 2, cols], ident[:])
                    ins.then_inc(tr_ready, 1)

                def states(u):
                    pe.wait_ge(hcd_done, U * g + u + 1)
                    if u == 0:
                        pe.wait_ge(out_added, TT * g + TT)
                    else:
                        pe.wait_ge(st_copied, U * g + u)
                    for b in range(NB):
                        ins = nc.tensor.matmul(st_ps[:, b * P:(b + 1) * P], b_tok[:, b, :], hcd[:, u % 2, b, :],
                                               start=True, stop=True)
                    ins.then_inc(st_ready, 1)

                def within(u):
                    if u == 0:
                        pe.wait_ge(cb_done, g + 1)
                    else:
                        pe.wait_ge(within_done, U * g + u)
                    pe.wait_ge(hc_done, (U + 1) * g + 2 + u)
                    pe.wait_ge(m_done, HG * g + 2 * u + 2)
                    for c in range(TT):
                        cols = slice(c * P, (c + 1) * P)
                        for hh in range(2):
                            rows = slice(hh * HD, (hh + 1) * HD)
                            ins = nc.tensor.matmul(y_ps[rows, cols], hc[:, u % 2, c, rows],
                                                   m_mat[:, 2 * u + hh, cols], start=True, stop=True)
                    ins.then_inc(yd_ready, 1)

                def carried(u):
                    pe.wait_ge(st_copied, U * g + u + 1)
                    if u == 0:
                        pe.wait_ge(ms_done, g + 1)
                    else:
                        pe.wait_ge(comb_done, U * g + u + 1)
                    for b in range(NB):
                        late = slice(b * EB + P, (b + 1) * EB)
                        ins = nc.tensor.matmul(off_ps[:, b * P:(b + 1) * P], state[:, u % 2, b, :], cT[:, late],
                                               start=True, stop=True)
                    ins.then_inc(off_ready, 1)

                def out_proj(t, ks):
                    for k in ks:
                        for i, (y, w) in enumerate(((y_hi, wo_hi), (y_hi, wo_lo), (y_lo, wo_hi))):
                            ins = nc.tensor.matmul(out_ps[t][:], y[:, k, t * P:(t + 1) * P], w[:, k, :],
                                                   start=k == 0 and i == 0, stop=k == U - 1 and i == 2)
                    if U - 1 in ks:
                        ins.then_inc(out_ready, 1)

                pe.wait_ge(dif_loaded, 128 * g + 128)
                pe.wait_ge(comb_done, U * g + 1)
                pe.wait_ge(ms_done, g + 1)
                pe.wait_ge(out_added, TT * g + 2)
                for n in range(2):
                    difs(6 * n, 6 * n + 3)
                    project(n, (0, 1))
                    difs(6 * n + 3, 6 * n + 6)
                    project(n, (2, 3))
                difs(12, 16)
                project(hid_half(0))
                project(gate_half(0), (0, 1))
                pe.wait_ge(hid_ready, (U + 2) * g + 1 + 1)
                pe.wait_ge(out_added, TT * g + 3)
                for b in range(NB):
                    ins = nc.tensor.transpose(tr_ps[:, b * P:(b + 1) * P], bT[:, b * EB:b * EB + P], ident[:])
                ins.then_inc(tr_ready, 1)
                project(gate_half(0), (2, 3))
                pe.wait_ge(hid_ready, (U + 2) * g + 2 + 1)
                pe.wait_ge(exp_done, HG * g + HG)
                for c in range(TT):
                    cols = slice(c * P, (c + 1) * P)
                    ins = nc.tensor.matmul(y_ps[:, cols], bT[:, cols], cT[:, cols], start=True, stop=True)
                ins.then_inc(cb_ready, 1)
                for u in range(1, U):
                    project(hid_half(u), (0, 1))
                    transposes(u - 1)
                    project(hid_half(u), (2, 3))
                    if u >= 2:
                        carried(u - 2)
                    project(gate_half(u))
                    within(u - 1)
                    states(u - 1)
                pe.wait_ge(y_lo_done, U * g + 4 + 1)
                out_proj(0, range(0, 4))
                transposes(U - 1)
                out_proj(1, range(0, 4))
                carried(U - 2)
                within(U - 1)
                states(U - 1)
                pe.wait_ge(wo_lo_done, U * g + U)
                pe.wait_ge(y_lo_done, U * g + U - 2 + 1)
                out_proj(0, (4, 5))
                out_proj(1, (4, 5))
                carried(U - 1)
                pe.wait_ge(y_lo_done, U * g + U - 1 + 1)
                out_proj(0, (6,))
                out_proj(1, (6,))
                pe.wait_ge(hc_done, (U + 1) * g + U + 1)
                out_proj(2, range(7))
                out_proj(3, range(7))
                pe.wait_ge(sq_done, U * g + U + 1)
                pe.wait_ge(comb_done, U * g + U + 1)
                for t in range(TT):
                    ins = nc.tensor.matmul(off_ps[:, t:t + 1], sq_sum[:, t * P:(t + 1) * P], ones[:, 0:1],
                                           start=True, stop=True)
                ins.then_inc(ss_ready, 1)
                pe.wait_ge(y_lo_done, U * g + U + 1)
                for t in range(TT):
                    out_proj(t, (7,))




def attention_ffn_block(nc, A, x_acc, early):
    k_parts_d = nc.dram_tensor("k_parts_d", [3, KVW, CT], BF16).ap()
    q_parts_d = nc.dram_tensor("q_parts_d", [3, D, T], BF16).ap()
    TERMS = ((0, 0), (0, 1), (1, 0), (1, 1), (0, 2), (2, 0))
    ROWS = len(TERMS) * AD

    with ExitStack() as ctx:
        def sb(name, shape, dt=F32):
            return ctx.enter_context(nc.sbuf_tensor(name, shape, dt))

        def sem(name):
            return ctx.enter_context(nc.semaphore(name))

        max_ps = ctx.enter_context(nc.psum_tensor("max_ps", [P, 2, 512], F32))
        sc_ps = [ctx.enter_context(nc.psum_tensor(f"sc_ps{i}", [P, 2, 512], F32)) for i in range(2)]
        pv_ps = ctx.enter_context(nc.psum_tensor("pv_ps", [P, 512], F32))
        odd_ps = ctx.enter_context(nc.psum_tensor("odd_ps", [P, 512], F32))
        banks = [max_ps[:, 0, :], max_ps[:, 1, :], sc_ps[0][:, 0, :], sc_ps[0][:, 1, :],
                 sc_ps[1][:, 0, :], sc_ps[1][:, 1, :], pv_ps[:], odd_ps[:]]

        ident = sb("ident2", [P, P])
        ctxT, wk, wv, wq = early.ctxT, early.wk, early.wv, early.wq
        wo = sb("wo", [P, KD, D])
        w1 = sb("w1", [P, NE, KD, D])
        w2 = sb("w2", [P, NE, KD, D])
        b1 = sb("b1", [P, NE, KD])
        b2 = sb("b2", [P, NE, D])
        gate_w = sb("gate_w", [P, KD, NE])
        gate_r = sb("gate_r", [P, NE])
        gate_b = sb("gate_b", [P, NE])
        vision = sb("vision", [P, P])
        text = sb("text", [P, P])
        every = sb("every", [P, P])
        first = sb("first", [P, P])
        ident_b = sb("ident_b2", [P, P], BF16)
        k_parts = sb("k_parts", [P, 3, CT], BF16)
        v_tok = sb("v_tok", [P, CT // P, KVH, 2 * AD])
        x1T = sb("x1T", [P, KD, T])
        q_parts = sb("q_parts", [P, 3, KD, T], BF16)
        k_st = [sb(f"k_st{i}", [P, CT], BF16) for i in range(RING)]
        q_st = [sb(f"q_st{i}", [P, REP, T], BF16) for i in range(RING)]
        nmax = sb("nmax", [P, RING, TT, REP])
        m_parts = sb("m_parts", [P, RING, TT, REP, 3], BF16)
        m_rest = sb("m_rest", [P, TT, REP])
        probs = sb("probs", [P, 2, 2 * 512])
        rest = probs[:].rearrange("p a (b t) -> p (a b) t", b=2)
        rden = sb("rden", [P, TT, REP])
        v_kv = [sb(f"v_kv{i}", [P, CT // P, 2 * AD]) for i in range(RING)]
        pv = sb("pv", [P, T])
        attn = sb("attn", [P, TT, D])
        attnT = x1T
        x2T = attn
        actT = [ctxT[:, :, 0:T], ctxT[:, :, T:2 * T]]
        bn6 = sb("bn6b", [P, TT, 6])
        mv = sb("mvb", [P, TT, 2])
        var = sb("varb", [P, TT])
        rs = sb("rsb", [P, TT])
        minus_half = sb("minus_halfb", [P, 8])
        lead = sb("leadb", [P, 8])
        asum = sb("asum", [P, TT])
        strength = sb("strength", [P, NB, 2])
        ratio = sb("ratio", [P, NB])
        lg = sb("lg", [P, TT, NE])
        lmax = sb("lmax", [P, TT])
        pe_ = sb("pe_", [P, TT, NE])
        lsum = sb("lsum", [P, TT])
        sel = sb("sel", [P, TT, 2, NE])
        keep = sb("keep", [P, TT])
        v1 = sb("v1", [P, TT])
        v2 = sb("v2", [P, TT])
        coef = sb("coef", [P, TT, NE])
        coef2 = sb("coef2", [P, TT, NE])
        sel_b = sb("sel_b", [P, NB, 2, NE])

        const_in = sem("const_in")
        wo_in = sem("wo_in"); w1_in = sem("w1_in"); w2_in = sem("w2_in"); small_in = sem("small_in")
        k_out = sem("k_out"); q_out = sem("q_out"); out_done = sem("out_done2")
        v_done = sem("v_done"); xT_ready = sem("xT_ready"); xT_done = sem("xT_done")
        q_ready = sem("q_ready"); k_ready = sem("k_ready"); v_ready = sem("v_ready")
        part1_done = sem("part1_done"); rest_done = sem("rest_done"); part2_done = sem("part2_done")
        part3_done = sem("part3_done")
        ones_set = sem("ones_set"); halves_set = sem("halves_set")
        st_in = [sem(f"st_in{i}") for i in range(RING)]
        smax_ready = sem("smax_ready"); smax_done = sem("smax_done"); mT_ready = sem("mT_ready")
        m_split = sem("m_split"); m_row_done = sem("m_row_done")
        sc_ready = sem("sc_ready"); probs_done = sem("probs_done"); pv_ready = sem("pv_ready")
        pv_done = sem("pv_done"); v_slot = sem("v_slot"); pvT_ready = sem("pvT_ready")
        rden_done = sem("rden_done"); attn_done = sem("attn_done")
        aT_ready = sem("aT_ready"); aT_done = sem("aT_done"); o_ready = sem("o_ready")
        ln_step = sem("ln_step"); pow_done = sem("pow_done"); x2_done = sem("x2_done")
        x2T_ready = sem("x2T_ready"); x2T_done = sem("x2T_done")
        asum_done = sem("asum_done"); str_ready = sem("str_ready"); lg_ready = sem("lg_ready")
        soft_in = sem("soft_in"); soft_out = sem("soft_out"); sel_done = sem("sel_done"); sel_ready = sem("sel_ready")
        chain = sem("chain"); pre_ready = sem("pre_ready"); act_done = sem("act_done")
        moe_ready = sem("moe_ready"); moe_done = sem("moe_done"); ln_done = sem("ln_done")
        block = ctx.enter_context(nc.Block())
        AHEAD = 7

        @block.sync
        def _(sp):
            sp.dma_start(ident[:], A["ident"]).then_inc(const_in, 16)
            sp.dma_start(ident_b[:], A["ident_b"]).then_inc(const_in, 16)
            sp.wait_ge(part3_done, NB)
            sp.dma_start(k_parts_d.rearrange("j p t -> p j t"), k_parts[:]).then_inc(k_out, 16)
            sp.wait_ge(ones_set, RING)

            def load_keys(kv):
                s = kv % RING
                for i, (_, kj) in enumerate(TERMS):
                    sp.dma_start(k_st[s][AD * i:AD * (i + 1)], k_parts_d[kj, kv * AD:(kv + 1) * AD]
                                 ).then_inc(st_in[s], 16)

            def load_queries(kv):
                s = kv % RING
                for i, (qj, _) in enumerate(TERMS):
                    sp.dma_start(q_st[s][AD * i:AD * (i + 1)],
                                 q_parts_d[qj, kv * REP * AD:(kv + 1) * REP * AD].rearrange("(h d) t -> d h t", h=REP)
                                 ).then_inc(st_in[s], 16)

            sp.wait_ge(k_out, 16)
            for kv in range(RING):
                load_keys(kv)
            for j, (first_tile, tiles) in enumerate(((0, 1), (1, KD))):
                sp.wait_ge(part3_done, NB + tiles)
                for part in range(3):
                    sp.dma_start(q_parts_d[part, first_tile * P:tiles * P].rearrange("(k p) t -> p k t", p=P),
                                 q_parts[:, part, first_tile:tiles]).then_inc(q_out, 16)
                sp.wait_ge(q_out, 3 * 16 * (j + 1))
                for kv in ((0, 1), (2,))[j]:
                    load_queries(kv)
            sp.dma_start(wo[:], A["wo"]).then_inc(wo_in, 16)
            for name, dst in (("vision", vision), ("text", text), ("first", first), ("every", every),
                              ("b1", b1), ("gate_w", gate_w)):
                sp.dma_start(dst[:], A[name]).then_inc(small_in, 16)
            sp.dma_start(gate_r[:], A["gate_r"].partition_broadcast(P)).then_inc(small_in, 16)
            sp.dma_start(gate_b[:], A["gate_b"].partition_broadcast(P)).then_inc(small_in, 16)
            sp.dma_start(b2[:], A["b2"].partition_broadcast(P)).then_inc(small_in, 16)
            sp.dma_start(w1[:], A["w1"]).then_inc(w1_in, 16)
            sp.dma_start(w2[:], A["w2"]).then_inc(w2_in, 16)
            for kv in range(RING, KVH):
                sp.wait_ge(sc_ready, 8 * (kv - RING + 1))
                load_keys(kv)
                load_queries(kv)
            sp.wait_ge(ln_done, TT)
            sp.dma_start(A["out"], x_acc[:]).then_inc(out_done, 16)
            sp.wait_ge(out_done, 16)

        @block.gpsimd
        def _(pool):
            nc.gpsimd.memset(minus_half[:], -0.5).then_inc(halves_set, 1)
            pool.wait_ge(halves_set, 1)
            pool.wait_ge(v_done, 3)

            def fill_v(kv, s):
                nc.gpsimd.tensor_copy(v_kv[s][:], v_tok[:, :, bass.ds(kv, 1), :].rearrange("p c a d -> p c (a d)")
                                      ).then_inc(v_slot, 1)

            def split_max(kv):
                s = kv % RING
                pool.wait_ge(smax_done, 16 * kv + 16 + 2)
                parts = m_parts[:, s].rearrange("p t h j -> p (t h) j")
                left, most = m_rest[:].rearrange("p t h -> p (t h)"), nmax[:, s].rearrange("p t h -> p (t h)")
                at = 5 * kv
                nc.gpsimd.tensor_copy(parts[:, :, 0], most).then_inc(m_split, 1)
                pool.wait_ge(m_split, at + 1)
                nc.gpsimd.tensor_tensor(left, most, parts[:, :, 0], ALU.subtract).then_inc(m_split, 1)
                pool.wait_ge(m_split, at + 2)
                nc.gpsimd.tensor_copy(parts[:, :, 1], left).then_inc(m_split, 1)
                pool.wait_ge(m_split, at + 3)
                nc.gpsimd.tensor_tensor(left, left, parts[:, :, 1], ALU.subtract).then_inc(m_split, 1)
                pool.wait_ge(m_split, at + 4)
                nc.gpsimd.tensor_copy(parts[:, :, 2], left).then_inc(m_split, 1)

            for kv in range(RING):
                fill_v(kv, kv)
            split_max(0)
            for kv in range(1, KVH):
                split_max(kv)
                if kv + 2 < KVH:
                    pool.wait_ge(pv_ready, kv)
                    fill_v(kv + 2, (kv + 2) % RING)
            for n in range(2):
                pool.wait_ge(ln_step, 9 * n + 9)
                nc.gpsimd.tensor_tensor(rs[:], var[:], minus_half[:, 0:TT], ALU.pow).then_inc(pow_done, 1)

        @block.scalar
        def _(act):
            act.wait_ge(halves_set, 1)
            for b in range(NB):
                act.wait_ge(k_ready, b + 1)
                nc.scalar.copy(k_parts[:, 0, b * CS:(b + 1) * CS], banks[b]).then_inc(part1_done, 1)
            for b in range(NB):
                act.wait_ge(rest_done, b + 1)
                nc.scalar.copy(k_parts[:, 1, b * CS:(b + 1) * CS], rest[:, b, :]).then_inc(part2_done, 1)
            for j in range(KD + 1):
                if j < KD:
                    act.wait_ge(q_ready, j + 1)
                    nc.scalar.mul(q_parts[:, 0, j, :], banks[j], SCALE).then_inc(part1_done, 1)
                if j > 0:
                    act.wait_ge(rest_done, NB + j)
                    nc.scalar.copy(q_parts[:, 1, j - 1, :], rest[:, j - 1, :]).then_inc(part2_done, 1)

            def max_row(kv, s, h):
                act.wait_ge(mT_ready, REP * kv + h + 1)
                nc.scalar.copy(q_st[s][ROWS:ROWS + 3, h, :], odd_ps[ROWS:ROWS + 3, :]).then_inc(m_row_done, 1)

            def exps(kv, n):
                act.wait_ge(sc_ready, 8 * kv + n + 1)
                nc.scalar.activation(probs[:, n % 2, :], sc_ps[n % 2][:].rearrange("p a k -> p (a k)"), ACT.Exp
                                     ).then_inc(probs_done, 1)

            nc.scalar.copy(lead[:, 4:5], minus_half[:, 0:1]).then_inc(probs_done, 2)
            nc.scalar.copy(lead[:, 5:6], minus_half[:, 0:1]).then_inc(pv_done, 1)
            for h in (0, 1):
                max_row(0, 0, h)

            def head(kv, s, more=True):
                for n in range(2, 8):
                    exps(kv, n)
                    if n in (4, 5) and more:
                        max_row(kv + 1, (s + 1) % RING, n - 4)
                if more:
                    exps(kv + 1, 0)
                act.wait_ge(pv_ready, kv + 1)
                nc.scalar.copy(pv[:], pv_ps[:]).then_inc(pv_done, 1)
                if more:
                    exps(kv + 1, 1)

            exps(0, 0)
            exps(0, 1)
            with act.Fori(0, 2) as i:
                for s in range(RING):
                    head(RING * i + s, s)
            head(KVH - 2, 0)
            head(KVH - 1, 1, False)
            act.wait_ge(soft_in, 1)
            nc.scalar.activation(pe_[:], lg[:], ACT.Exp).then_inc(soft_out, 1)
            act.wait_ge(small_in, 9 * 16)
            for e, func in enumerate((ACT.Tanh, ACT.Gelu, ACT.Silu)):
                for f in range(KD):
                    act.wait_ge(pre_ready, KD * e + f + 1)
                    nc.scalar.activation(actT[e % 2][:, f, :], banks[f], func, bias=b1[:, e, f:f + 1]
                                         ).then_inc(act_done, 1)

        @block.vector
        def _(dve):
            for s in range(RING):
                nc.vector.memset(k_st[s][:], 1.0).then_inc(ones_set, 1)
            nc.vector.memset(v_tok[:, :, :, AD:2 * AD], 1.0).then_inc(v_done, 1)
            nc.vector.memset(lead[:, 0:1], 0.0).then_inc(attn_done, 1)
            nc.vector.memset(lead[:, 1:2], 0.0).then_inc(smax_done, 2)
            for b in range(NB):
                dve.wait_ge(part1_done, b + 1)
                nc.vector.tensor_tensor(rest[:, b, :], banks[b], k_parts[:, 0, b * CS:(b + 1) * CS], ALU.subtract
                                        ).then_inc(rest_done, 1)
            for b in range(NB):
                cols = slice(b * CS, (b + 1) * CS)
                dve.wait_ge(part2_done, b + 1)
                nc.vector.tensor_tensor(k_parts[:, 2, cols], rest[:, b, :], k_parts[:, 1, cols], ALU.subtract
                                        ).then_inc(part3_done, 1)
            for h in range(2):
                dve.wait_ge(v_ready, h + 1)
                nc.vector.tensor_copy(v_tok[:, 4 * h:4 * h + 4, :, 0:AD],
                                      banks[2 + h].rearrange("p (c k d) -> p c k d", c=4, k=KVH)).then_inc(v_done, 1)
            for k in range(KD):
                dve.wait_ge(xT_ready, k + 1)
                nc.vector.tensor_copy(x1T[:, k, :], banks[4 + k]).then_inc(xT_done, 1)
            for j in range(KD + 1):
                if j < KD:
                    dve.wait_ge(part1_done, NB + j + 1)
                    if j == 0:
                        dve.wait_ge(part3_done, NB)
                    nc.vector.scalar_tensor_tensor(rest[:, j, :], banks[j], SCALE, q_parts[:, 0, j, :],
                                                   ALU.mult, ALU.subtract).then_inc(rest_done, 1)
                if j > 0:
                    dve.wait_ge(part2_done, NB + j)
                    nc.vector.tensor_tensor(q_parts[:, 2, j - 1, :], rest[:, j - 1, :], q_parts[:, 1, j - 1, :],
                                            ALU.subtract).then_inc(part3_done, 1)

            def row_max(kv, s, n):
                t, m = n // 2, n % 2
                for i in range(2):
                    dve.wait_ge(smax_ready, 16 * kv + 2 * n + i + 1)
                    nc.vector.tensor_reduce(nmax[:, s, t, 2 * m + i:2 * m + i + 1], max_ps[:, i, :], AX.X, ALU.max,
                                            negate=True).then_inc(smax_done, 1)

            def max_row(kv, s, h):
                dve.wait_ge(mT_ready, REP * kv + h + 1)
                nc.vector.tensor_copy(q_st[s][ROWS:ROWS + 3, h, :], odd_ps[ROWS:ROWS + 3, :]).then_inc(m_row_done, 1)

            def normalise(kv):
                dve.wait_ge(pvT_ready, kv + 1)
                out = odd_ps[:].rearrange("p (t h d) -> p t h d", t=TT, h=REP)
                nc.vector.reciprocal(rden[:], out[:, :, :, AD]).then_inc(rden_done, 1)
                dve.wait_ge(rden_done, kv + 1)
                nc.vector.tensor_tensor(
                    attn[:, :, bass.ds(kv * REP * AD, REP * AD)].rearrange("p t (h d) -> p t h d", h=REP),
                    out[:, :, :, 0:AD], rden[:].unsqueeze(3).to_broadcast([P, TT, REP, AD]),
                    ALU.mult).then_inc(attn_done, 1)

            def head(kv, s, rest, ahead):
                for n in range(8):
                    if rest and n < 8 - AHEAD:
                        row_max(kv + 1, (s + 1) % RING, n + AHEAD)
                    if ahead and n >= 8 - AHEAD:
                        row_max(kv + 2, (s + 2) % RING, n - 8 + AHEAD)
                    if rest and n in (4, 5):
                        max_row(kv + 1, (s + 1) % RING, n - 2)
                normalise(kv)

            for n in range(8):
                row_max(0, 0, n)
            row_max(1, 1, 0)
            for h in (1, 2, 3):
                row_max(1, 1, h)
                if h > 1:
                    max_row(0, 0, h)
            for n in range(REP, AHEAD):
                row_max(1, 1, n)
            with dve.Fori(0, 2) as i:
                for s in range(RING):
                    head(RING * i + s, s, True, True)
            head(KVH - 2, 0, True, False)
            head(KVH - 1, 1, False, False)
            for k in range(KD):
                dve.wait_ge(aT_ready, k + 1)
                nc.vector.tensor_copy(attnT[:, k, :], banks[k]).then_inc(aT_done, 1)

            def layernorm(n, done):
                at = 9 * n
                for t in range(TT):
                    nc.vector.bn_stats(bn6[:, t, :], x_acc[:, t, :]).then_inc(ln_step, 1)
                for t in range(TT):
                    dve.wait_ge(ln_step, at + TT)
                    nc.vector.bn_aggr(mv[:, t, :], bn6[:, t, :]).then_inc(ln_step, 1)
                dve.wait_ge(ln_step, at + 2 * TT)
                nc.vector.tensor_scalar(var[:], mv[:, :, 1], EPS, None, ALU.add).then_inc(ln_step, 1)
                dve.wait_ge(pow_done, n + 1)
                for t in range(TT):
                    nc.vector.tensor_scalar(x_acc[:, t, :], x_acc[:, t, :], mv[:, t, 0:1], rs[:, t:t + 1],
                                            ALU.subtract, ALU.mult).then_inc(done, 1)

            c = [0]

            def link(ins):
                c[0] += 1
                ins.then_inc(chain, 1)
                dve.wait_ge(chain, c[0])

            for t in range(TT):
                dve.wait_ge(o_ready, t + 1)
                link(nc.vector.tensor_tensor(x_acc[:, t, :], x_acc[:, t, :], banks[4 + t], ALU.add))
            layernorm(0, x2_done)
            dve.wait_ge(x2_done, TT)
            for k in range(KD):
                dve.wait_ge(x2T_ready, k + 1)
                nc.vector.tensor_copy(x2T[:, k, :], banks[k]).then_inc(x2T_done, 1)
            nc.vector.tensor_reduce(asum[:], x_acc[:], AX.X, ALU.add, apply_absolute_value=True).then_inc(asum_done, 1)

            dve.wait_ge(str_ready, 1)
            dve.wait_ge(small_in, 9 * 16)
            sums = odd_ps[:, 0:2 * NB].rearrange("p (b s) -> p b s", b=NB)
            link(nc.vector.tensor_scalar(strength[:, :, 0], sums[:, :, 0], 1.0 / (VIS * D), 1e-8, ALU.mult, ALU.add))
            link(nc.vector.tensor_scalar(strength[:, :, 1], sums[:, :, 1], 1.0 / ((SEQ - VIS) * D), None, ALU.mult))
            link(nc.vector.reciprocal(ratio[:], strength[:, :, 0]))
            link(nc.vector.tensor_tensor(ratio[:], ratio[:], strength[:, :, 1], ALU.mult))
            dve.wait_ge(lg_ready, 1)
            logits = odd_ps[:, 16:16 + TT * NE].rearrange("p (t e) -> p t e", t=TT)
            link(nc.vector.tensor_tensor(lg[:], logits, gate_b[:].unsqueeze(1).to_broadcast([P, TT, NE]), ALU.add))
            for t in range(TT):
                link(nc.vector.scalar_tensor_tensor(lg[:, t, :], gate_r[:], ratio[:, t // 2:t // 2 + 1], lg[:, t, :],
                                                    ALU.mult, ALU.add))
            link(nc.vector.tensor_reduce(lmax[:], lg[:], AX.X, ALU.max))
            link(nc.vector.tensor_tensor(lg[:], lg[:], lmax[:].unsqueeze(2).to_broadcast([P, TT, NE]), ALU.subtract))
            nc.vector.memset(keep[:], 0.0).then_inc(soft_in, 1)
            dve.wait_ge(soft_out, 1)
            link(nc.vector.tensor_reduce(lsum[:], pe_[:], AX.X, ALU.add))
            link(nc.vector.reciprocal(lsum[:], lsum[:]))
            link(nc.vector.tensor_tensor(pe_[:], pe_[:], lsum[:].unsqueeze(2).to_broadcast([P, TT, NE]), ALU.mult))
            for i, best in enumerate((v1, v2)):
                s = sel[:, :, i, :]
                link(nc.vector.tensor_reduce(best[:], pe_[:], AX.X, ALU.max))
                link(nc.vector.tensor_tensor(s, pe_[:], best[:].unsqueeze(2).to_broadcast([P, TT, NE]), ALU.is_ge))
                link(nc.vector.tensor_scalar(keep[:], s[:, :, 0], -1.0, 1.0, ALU.mult, ALU.add))
                link(nc.vector.tensor_tensor(s[:, :, 1], s[:, :, 1], keep[:], ALU.mult))
                link(nc.vector.tensor_tensor(s[:, :, 2], keep[:], s[:, :, 1], ALU.subtract))
                if i == 0:
                    link(nc.vector.scalar_tensor_tensor(pe_[:], s, -2.0, pe_[:], ALU.mult, ALU.add))
            link(nc.vector.scalar_tensor_tensor(lsum[:], v1[:], 1e-8, v2[:], ALU.add, ALU.add))
            link(nc.vector.reciprocal(lsum[:], lsum[:]))
            link(nc.vector.tensor_tensor(v1[:], v1[:], lsum[:], ALU.mult))
            nc.vector.tensor_tensor(v2[:], v2[:], lsum[:], ALU.mult).then_inc(sel_done, 1)
            dve.wait_ge(sel_done, 1)
            dve.wait_ge(sel_ready, 1)
            link(nc.vector.tensor_copy(sel_b[:].rearrange("p b i e -> p (b i e)"), odd_ps[:, 64:64 + NB * 2 * NE]))
            for t in range(TT):
                link(nc.vector.tensor_scalar(coef[:, t, :], sel_b[:, t // 2, 0, :], v1[:, t:t + 1], None, ALU.mult))
                link(nc.vector.scalar_tensor_tensor(coef[:, t, :], sel_b[:, t // 2, 1, :], v2[:, t:t + 1],
                                                    coef[:, t, :], ALU.mult, ALU.add))
            for e in range(NE):
                for t in range(TT):
                    link(nc.vector.scalar_tensor_tensor(x_acc[:, t, :], b2[:, e, :], coef[:, t, e:e + 1],
                                                        x_acc[:, t, :], ALU.mult, ALU.add))
            for e in range(NE):
                for t in range(TT):
                    dve.wait_ge(moe_ready, TT * e + t + 1)
                    if e:
                        dve.wait_ge(moe_done, TT * (e - 1) + t + 1)
                    nc.vector.scalar_tensor_tensor(x_acc[:, t, :], banks[4 + t], coef[:, t, e:e + 1], x_acc[:, t, :],
                                                   ALU.mult, ALU.add).then_inc(moe_done, 1)
            dve.wait_ge(moe_done, TT * NE)
            layernorm(1, ln_done)

        @block.tensor
        def _(pe):
            pe.wait_ge(early.loaded, 4 * 16)
            for b in range(NB):
                for k in range(KD):
                    ins = nc.tensor.matmul(banks[b], wk[:, k, :], ctxT[:, k, b * CS:(b + 1) * CS],
                                           start=k == 0, stop=k == KD - 1)
                ins.then_inc(k_ready, 1)
            for h in range(2):
                for c in range(4):
                    for k in range(KD):
                        t = 4 * h + c
                        ins = nc.tensor.matmul(banks[2 + h][:, c * P:(c + 1) * P], ctxT[:, k, t * P:(t + 1) * P],
                                               wv[:, k, :], start=k == 0, stop=k == KD - 1)
                ins.then_inc(v_ready, 1)

            def turn(src, ready, first_bank):
                for k in range(KD):
                    for t in range(TT):
                        ins = nc.tensor.transpose(banks[first_bank + k][:, t * P:(t + 1) * P],
                                                  src[:, t, k * P:(k + 1) * P], ident[:])
                    ins.then_inc(ready, 1)

            pe.wait_ge(const_in, 32)
            turn(x_acc, xT_ready, 4)
            pe.wait_ge(xT_done, KD)
            pe.wait_ge(rest_done, NB)
            for j in range(KD):
                if j == 2:
                    pe.wait_ge(v_done, 3)
                for k in range(KD):
                    ins = nc.tensor.matmul(banks[j], wq[:, k, j * P:(j + 1) * P], x1T[:, k, :],
                                           start=k == 0, stop=k == KD - 1)
                ins.then_inc(q_ready, 1)
            pe.wait_ge(rest_done, NB + KD)

            def row_scores(kv, s, n, visit):
                t, m = n // 2, n % 2
                if n == 0:
                    pe.wait_ge(st_in[s], 16 * 2 * len(TERMS) * visit)
                for i in range(2):
                    pe.wait_ge(smax_done, 16 * kv + 2 * n + i + 1)
                    nc.tensor.matmul(max_ps[:, i, :], q_st[s][0:ROWS, 2 * m + i, t * P:(t + 1) * P],
                                     k_st[s][0:ROWS, (t // 2) * CS:(t // 2 + 1) * CS], start=True, stop=True
                                     ).then_inc(smax_ready, 1)

            def max_row(kv, s, h, first=False):
                if h == 0:
                    pe.wait_ge(m_split, 5 * kv + 5)
                if not first or h:
                    pe.wait_ge(m_row_done, REP * kv + h)
                if h == 0 and not first:
                    pe.wait_ge(attn_done, kv - 1 + 1)
                for t in range(TT):
                    ins = nc.tensor.matmul(odd_ps[ROWS:ROWS + 3, t * P:(t + 1) * P], m_parts[:, s, t, h, :],
                                           ident_b[:], start=True, stop=True)
                ins.then_inc(mT_ready, 1)

            def scores(kv, s, n):
                b, c = divmod(n, CS // P)
                if n == 0:
                    pe.wait_ge(m_row_done, REP * kv + REP)
                pe.wait_ge(probs_done, 8 * kv + n - 1 + 2)
                for m in range(REP // 2):
                    ins = nc.tensor.matmul(sc_ps[n % 2][:, m, :].rearrange("p (h t) -> p h t", h=2),
                                           k_st[s][0:ROWS + 3, b * CS + c * P:b * CS + (c + 1) * P],
                                           q_st[s][0:ROWS + 3, 2 * m:2 * m + 2, b * SEQ:(b + 1) * SEQ],
                                           start=True, stop=True)
                ins.then_inc(sc_ready, 1)

            def values(kv, s, n):
                b, c = divmod(n, CS // P)
                pe.wait_ge(probs_done, 8 * kv + n + 1 + 2)
                if n == 0:
                    pe.wait_ge(v_slot, kv + 1)
                    pe.wait_ge(pv_done, kv + 1)
                for h in range(REP):
                    at = h * SEQ
                    ins = nc.tensor.matmul(pv_ps[32 * h:32 * h + 2 * AD, b * SEQ:(b + 1) * SEQ],
                                           v_kv[s][:, b * (CS // P) + c, :], probs[:, n % 2, at:at + SEQ],
                                           start=c == 0, stop=c == CS // P - 1)
                if n == 7:
                    ins.then_inc(pv_ready, 1)

            def turn_pv(kv):
                pe.wait_ge(pv_done, kv + 1 + 1)
                pe.wait_ge(m_row_done, REP * (min(kv + 2, KVH) if isinstance(kv, int) else kv + 2))
                pe.wait_ge(attn_done, kv + 1)
                for t in range(TT):
                    ins = nc.tensor.transpose(odd_ps[:, t * P:(t + 1) * P], pv[:, t * P:(t + 1) * P], ident[:])
                ins.then_inc(pvT_ready, 1)

            for n in range(8):
                row_scores(0, 0, n, 1)
            for h in range(REP):
                max_row(0, 0, h, True)
                row_scores(1, 1, h, 1)
            scores(0, 0, 0)
            scores(0, 0, 1)
            for n in range(REP, AHEAD):
                row_scores(1, 1, n, 1)

            def head(kv, s, visit, rest=True, ahead=True):
                s1, s2 = (s + 1) % RING, (s + 2) % RING
                for n in range(8):
                    values(kv, s, n)
                    if n < 6:
                        scores(kv, s, n + 2)
                    elif rest:
                        scores(kv + 1, s1, n - 6)
                    if rest and n < 8 - AHEAD:
                        row_scores(kv + 1, s1, n + AHEAD, None)
                    if ahead and n >= 8 - AHEAD:
                        row_scores(kv + 2, s2, n - 8 + AHEAD, visit + (s > 0))
                    if rest and n in range(2, 6):
                        max_row(kv + 1, s1, n - 2)
                turn_pv(kv)

            with pe.Fori(0, 2) as i:
                for s in range(RING):
                    head(RING * i + s, s, i + 1)
            head(KVH - 2, 0, 3, True, False)
            head(KVH - 1, 1, 3, False, False)
            pe.wait_ge(attn_done, KVH + 1)
            turn(attn, aT_ready, 0)
            pe.wait_ge(wo_in, 16)
            pe.wait_ge(aT_done, KD)
            for t in range(TT):
                for k in range(KD):
                    ins = nc.tensor.matmul(banks[4 + t], attnT[:, k, t * P:(t + 1) * P], wo[:, k, :],
                                           start=k == 0, stop=k == KD - 1)
                ins.then_inc(o_ready, 1)
            pe.wait_ge(x2_done, TT)
            turn(x_acc, x2T_ready, 0)
            pe.wait_ge(x2T_done, KD)

            def strengths():
                pe.wait_ge(small_in, 9 * 16)
                pe.wait_ge(chain, TT)
                pe.wait_ge(asum_done, 1)
                for b in range(NB):
                    for i, parts in enumerate(((vision,), (text, every))):
                        for j, mask in enumerate(parts):
                            at = 2 * b + i
                            ins = nc.tensor.matmul(odd_ps[:, at:at + 1], mask[:], asum[:, 2 * b + j:2 * b + j + 1],
                                                   start=j == 0, stop=j == len(parts) - 1)
                ins.then_inc(str_ready, 1)

            def logits():
                pe.wait_ge(chain, TT + 4)
                for t in range(TT):
                    for k in range(KD):
                        at = 16 + NE * t
                        ins = nc.tensor.matmul(odd_ps[:, at:at + NE], x2T[:, k, t * P:(t + 1) * P], gate_w[:, k, :],
                                               start=k == 0, stop=k == KD - 1)
                ins.then_inc(lg_ready, 1)

            def up(e):
                for f in range(KD):
                    if e == 0 and f == 2:
                        strengths()
                    if e == 0 and f == 3:
                        logits()
                    if e:
                        pe.wait_ge(act_done, KD * (e - 1) + f + 1)
                    for k in range(KD):
                        ins = nc.tensor.matmul(banks[f], w1[:, e, k, f * P:(f + 1) * P], x2T[:, k, :],
                                               start=k == 0, stop=k == KD - 1)
                    ins.then_inc(pre_ready, 1)

            def down(e):
                pe.wait_ge(act_done, KD * (e + 1))
                for t in range(TT):
                    if e:
                        pe.wait_ge(moe_done, TT * (e - 1) + t + 1)
                    for f in range(KD):
                        ins = nc.tensor.matmul(banks[4 + t], actT[e % 2][:, f, t * P:(t + 1) * P], w2[:, e, f, :],
                                               start=f == 0, stop=f == KD - 1)
                    ins.then_inc(moe_ready, 1)

            pe.wait_ge(w1_in, 16)
            up(0)
            up(1)
            pe.wait_ge(sel_done, 1)
            for b in range(NB):
                at = 64 + 2 * NE * b
                ins = nc.tensor.matmul(odd_ps[:, at:at + 2 * NE], first[:],
                                       sel[:, 2 * b].rearrange("p i e -> p (i e)"), start=True, stop=True)
            ins.then_inc(sel_ready, 1)
            pe.wait_ge(w2_in, 16)
            pe.wait_ge(chain, SEL_B)
            down(0)
            up(2)
            down(1)
            down(2)


V = {"ms": 2, "xn": 6, "x2": 7, "hT0": 8, "hT1": 9, "hT2": 10, "hT3": 11, "u": 12, "dtT": 26, "acs": 32, "parts": 38,
     "start": 40, "var": 49, "ln": 53}
S = {"eT": 10}
E = {"dt": 5, "dt_tr": 6, "dec_tr": 7}


def kernel(**inputs):
    import numpy as np
    import concourse.bacc as bacc
    from concourse.bass_utils import run_bass_kernel_spmd

    w = {k: np.asarray(v) for k, v in inputs.items()}

    def columns(vec, n):
        return np.ascontiguousarray(vec.reshape(n, P).T)

    def weight_tiles(rows):
        n = rows.shape[0] // P
        return rows.reshape(n, P, KD, P).transpose(0, 3, 2, 1)

    wi = w["L0_attn_in_proj_w"]
    parts = {}
    gate_w, hid_w = weight_tiles(wi[:DIN]), weight_tiles(wi[DIN:2 * DIN])
    b_w = weight_tiles(wi[2 * DIN:2 * DIN + GROUPS * NST])
    c_w = weight_tiles(wi[2 * DIN + GROUPS * NST:2 * DIN + 2 * GROUPS * NST])
    main = np.stack([hid_w, gate_w], axis=2).reshape(GROUPS, U, P, 2, KD, P)
    bc = np.stack([b_w, c_w], axis=2)[:, None]
    pairs = np.concatenate([bc, main], axis=1).reshape(GROUPS * PAIRS, P, 2, KD, P)
    parts["w_main"] = np.concatenate([pairs, np.zeros((PAIRS,) + pairs.shape[1:], np.float32)])
    parts["w_dt"] = weight_tiles(wi[2 * DIN + 2 * GROUPS * NST:])[0]
    parts["w_out"] = w["L0_attn_out_proj_w"].T.reshape(GROUPS * U // 2, 2, P, D).transpose(0, 2, 1, 3)
    parts["x"] = w["x"].reshape(TT, P, D).transpose(1, 0, 2)
    nch = TILES + 2 * GROUPS
    parts["conv_w"] = w["L0_attn_conv_w"].reshape(nch, P, KC).transpose(1, 0, 2)
    parts["conv_b"] = columns(w["L0_attn_conv_b"], nch)
    parts["norm_w"] = columns(w["L0_attn_norm_w"], KD)
    parts["gnorm"] = columns(w["L0_attn_gnorm_w"], TILES)
    parts["d_skip"] = columns(np.repeat(w["L0_attn_Dp"], HD), TILES)
    parts["dt_bias"] = w["L0_attn_dt_bias"].reshape(HEADS, 1)
    parts["a_log"] = w["L0_attn_A_log"].reshape(HEADS, 1)
    parts["ident"] = np.eye(P, dtype=np.float32)
    import ml_dtypes
    parts["ident_b"] = np.eye(P).astype(ml_dtypes.bfloat16)
    parts["above"] = np.ascontiguousarray(np.broadcast_to(
        (np.tril(np.ones((P, P)), -1) * -BIG)[:, None], (P, TT, P))).astype(ml_dtypes.bfloat16)
    parts["causal"] = np.triu(np.ones((P, P), np.float32))

    def rows_k(m):
        return m.reshape(-1, P, m.shape[-1]).transpose(1, 0, 2)

    parts["ctxT"] = rows_k(w["ctx_4096"].reshape(CT, D).T)
    parts["wk"], parts["wv"] = rows_k(w["L0_xattn_Wk"]), rows_k(w["L0_xattn_Wv"])
    parts["wq"], parts["wo"] = rows_k(w["L0_xattn_Wq"]), rows_k(w["L0_xattn_Wo"])
    parts["w1"] = w["L0_ffn_w1"].reshape(NE, KD, P, D).transpose(2, 0, 1, 3)
    parts["w2"] = w["L0_ffn_w2"].reshape(NE, KD, P, D).transpose(2, 0, 1, 3)
    parts["b1"] = w["L0_ffn_b1"].reshape(NE, KD, P).transpose(2, 0, 1)
    parts["b2"] = w["L0_ffn_b2"]
    parts["gate_w"] = rows_k(w["L0_ffn_gate_w"][:D])
    parts["gate_r"] = w["L0_ffn_gate_w"][D]
    parts["gate_b"] = w["L0_ffn_gate_b"]
    token = np.arange(P).reshape(P, 1) * np.ones((1, P))
    parts["vision"] = (token < VIS).astype(np.float32)
    parts["text"] = (token >= VIS).astype(np.float32)
    parts["every"] = np.ones((P, P), np.float32)
    parts["first"] = (token == 0).astype(np.float32)

    nc = bacc.Bacc("TRN2", target_bir_lowering=False, num_devices=1)
    arrays, aps = {}, {}
    for name, a in parts.items():
        arrays["in_" + name] = np.ascontiguousarray(a)
        aps[name] = nc.dram_tensor("in_" + name, a.shape, mybir.dt.from_np(a.dtype), kind="ExternalInput").ap()
    aps["out"] = nc.dram_tensor("out_dram", [P, TT, D], F32, kind="ExternalOutput").ap()
    decoder_program(nc, aps)
    r = run_bass_kernel_spmd(nc, [arrays], core_ids=[0])
    got = np.asarray(r.results[0]["out_dram"]).reshape(P, TT, D)
    return np.ascontiguousarray(got.transpose(1, 0, 2).reshape(NB, SEQ, D))
```
